# Optimizing a Trainium2 kernel written in Bass

```python
import numpy as np
import jax
import jax.numpy as jnp

def _softmax(x, axis=-1):
    return jax.nn.softmax(x, axis=axis)

def _gelu(x):
    return jax.nn.gelu(x, approximate=True)

def _silu(x):
    return jax.nn.silu(x)

def _sigmoid(x):
    return jax.nn.sigmoid(x)

def _layernorm(x, axis=-1, eps=1e-05):
    m = jnp.mean(x, axis=axis, keepdims=True)
    v = jnp.var(x, axis=axis, keepdims=True)
    return (x - m) / jnp.sqrt(v + eps)

def _scatter_add(tgt, idx, src, axis=0):
    return tgt.at[idx].add(src)

def _segment_sum(src, seg, n):
    return jax.ops.segment_sum(src, seg, n)
kernel_name = 'mk_seq_postln_d1_jaxref_r8_668804'

def setup_inputs(seed: int=0):
    np.random.seed(seed)
    _w = jnp.asarray

    def _L0_attn_setup():
        import jax, jax.numpy as jnp
        import numpy as np
        D_MODEL = 128
        D_STATE = 64
        D_CONV = 7
        EXPAND = 2
        HEADDIM = 64
        NGROUPS = 1
        D_INNER = EXPAND * D_MODEL
        NHEADS = D_INNER // HEADDIM
        D_XBC = D_INNER + 2 * (2 * NGROUPS * D_STATE)
        D_IN_PROJ = 2 * D_INNER + 2 * (2 * NGROUPS * D_STATE) + 2 * NHEADS
        RMS_EPS = 1e-05

        def _dwconv(x, w, b):
            C = x.shape[-1]
            out = jax.lax.conv_general_dilated(x.transpose(0, 2, 1), w, window_strides=(1,), padding='SAME', feature_group_count=C)
            return out.transpose(0, 2, 1) + b

        def _selective_scan(x, dt, A, Bm, Cm):
            b, l, h, p = x.shape
            g = Bm.shape[2]
            hpg = h // g
            Bh = jnp.repeat(Bm, hpg, axis=2)
            Ch = jnp.repeat(Cm, hpg, axis=2)
            decay = jnp.exp(dt * A)

            def step(hstate, inp):
                dec_t, dt_t, x_t, B_t, C_t = inp
                hstate = hstate * dec_t[..., None, None] + jnp.einsum('bh,bhn,bhp->bhpn', dt_t, B_t, x_t)
                y = jnp.einsum('bhpn,bhn->bhp', hstate, C_t)
                return (hstate, y)
            h0 = jnp.zeros((b, h, p, Bh.shape[-1]), x.dtype)
            xs = (decay.transpose(1, 0, 2), dt.transpose(1, 0, 2), x.transpose(1, 0, 2, 3), Bh.transpose(1, 0, 2, 3), Ch.transpose(1, 0, 2, 3))
            _, ys = jax.lax.scan(step, h0, xs)
            return ys.transpose(1, 0, 2, 3)
        key = jax.random.key(seed)
        ks = jax.random.split(key, 8)
        B, L = (2, 512)
        u = jax.random.normal(ks[0], (B, L, D_MODEL), jnp.float32)
        in_proj_w = jax.random.normal(ks[1], (D_IN_PROJ, D_MODEL), jnp.float32) * 0.02
        conv1d_w = jax.random.normal(ks[2], (D_XBC, 1, D_CONV), jnp.float32) * 0.2
        conv1d_b = jnp.zeros((D_XBC,), jnp.float32)
        dt_bias = jax.random.normal(ks[3], (NHEADS,), jnp.float32) * 0.5 - 4.0
        A_log = jnp.zeros((NHEADS,), jnp.float32)
        D_w = jax.random.normal(ks[4], (NHEADS, D_INNER), jnp.float32) * 0.02
        D_b = jnp.zeros((NHEADS,), jnp.float32)
        rms_w = jnp.ones((D_INNER,), jnp.float32)
        outproj_w = jax.random.normal(ks[5], (D_MODEL, D_INNER), jnp.float32) * 0.02
        return dict(u=u, in_proj_w=in_proj_w, conv1d_w=conv1d_w, conv1d_b=conv1d_b, dt_bias=dt_bias, A_log=A_log, D_w=D_w, D_b=D_b, rms_w=rms_w, outproj_w=outproj_w)
    _L0_attn_in = _L0_attn_setup()

    def _L0_ffn_setup():
        import jax, jax.numpy as jnp
        import numpy as np
        L, H, NH, NKV, HD, FF, E, K = (4, 128, 16, 4, 64, 256, 8, 2)
        B, S = (2, 256)
        THETA, EPS = (10000.0, 1e-05)

        def _rms(x, w):
            return x * jax.lax.rsqrt(jnp.mean(x * x, axis=-1, keepdims=True) + EPS) * w

        def _rope_cos_sin(seq_len, head_dim, theta):
            inv = 1.0 / theta ** (jnp.arange(0, head_dim, 2, dtype=jnp.float32) / head_dim)
            f = jnp.arange(seq_len, dtype=jnp.float32)[:, None] * inv
            emb = jnp.concatenate([f, f], axis=-1)
            return (jnp.cos(emb), jnp.sin(emb))

        def _rot_half(x):
            h = x.shape[-1] // 2
            return jnp.concatenate([-x[..., h:], x[..., :h]], axis=-1)

        def _attention(x, wq, wk, wv, wo, cos, sin, causal_bias):
            b, s, _ = x.shape
            q = (x @ wq).reshape(b, s, NH, HD).transpose(0, 2, 1, 3)
            k = (x @ wk).reshape(b, s, NKV, HD).transpose(0, 2, 1, 3)
            v = (x @ wv).reshape(b, s, NKV, HD).transpose(0, 2, 1, 3)
            c = cos[None, None]
            sn = sin[None, None]
            q = q * c + _rot_half(q) * sn
            k = k * c + _rot_half(k) * sn
            rep = NH // NKV
            k = jnp.repeat(k, rep, axis=1)
            v = jnp.repeat(v, rep, axis=1)
            scores = jnp.einsum('bhqd,bhkd->bhqk', q, k) / jnp.sqrt(jnp.asarray(HD, x.dtype))
            scores = scores + causal_bias
            attn = jax.nn.softmax(scores, axis=-1)
            out = jnp.einsum('bhqk,bhkd->bhqd', attn, v)
            out = out.transpose(0, 2, 1, 3).reshape(b, s, NH * HD)
            return out @ wo

        def _moe(x, wr, wg, wu, wd):
            logits = x @ wr
            probs = jax.nn.softmax(logits, axis=-1)
            topv, topi = jax.lax.top_k(probs, K)
            topv = topv / jnp.sum(topv, axis=-1, keepdims=True)
            comb = jnp.sum(jax.nn.one_hot(topi, E, dtype=x.dtype) * topv[..., None], axis=-2)
            out = jnp.zeros_like(x)
            for e in range(E):
                h = jax.nn.silu(x @ wg[e]) * (x @ wu[e])
                out = out + comb[..., e:e + 1] * (h @ wd[e])
            return out
        key = jax.random.key(seed)
        ks = jax.random.split(key, 12)
        sc = 0.02
        inp = {'hidden_states': jax.random.normal(ks[0], (B, S, H), jnp.float32), 'ln1_w': jnp.ones((L, H), jnp.float32), 'ln2_w': jnp.ones((L, H), jnp.float32), 'wq': jax.random.normal(ks[1], (L, H, NH * HD), jnp.float32) * sc, 'wk': jax.random.normal(ks[2], (L, H, NKV * HD), jnp.float32) * sc, 'wv': jax.random.normal(ks[3], (L, H, NKV * HD), jnp.float32) * sc, 'wo': jax.random.normal(ks[4], (L, NH * HD, H), jnp.float32) * sc, 'wr': jax.random.normal(ks[5], (L, H, E), jnp.float32) * sc, 'wg': jax.random.normal(ks[6], (L, E, H, FF), jnp.float32) * sc, 'wu': jax.random.normal(ks[7], (L, E, H, FF), jnp.float32) * sc, 'wd': jax.random.normal(ks[8], (L, E, FF, H), jnp.float32) * sc}
        return inp
    _L0_ffn_in = _L0_ffn_setup()
    _d = {'L0_attn_u': _L0_attn_in['u'], 'L0_attn_in_proj_w': _L0_attn_in['in_proj_w'], 'L0_attn_conv1d_w': _L0_attn_in['conv1d_w'], 'L0_attn_conv1d_b': _L0_attn_in['conv1d_b'], 'L0_attn_dt_bias': _L0_attn_in['dt_bias'], 'L0_attn_A_log': _L0_attn_in['A_log'], 'L0_attn_D_w': _L0_attn_in['D_w'], 'L0_attn_D_b': _L0_attn_in['D_b'], 'L0_attn_rms_w': _L0_attn_in['rms_w'], 'L0_attn_outproj_w': _L0_attn_in['outproj_w'], 'L0_ffn_ln1_w': _L0_ffn_in['ln1_w'], 'L0_ffn_ln2_w': _L0_ffn_in['ln2_w'], 'L0_ffn_wq': _L0_ffn_in['wq'], 'L0_ffn_wk': _L0_ffn_in['wk'], 'L0_ffn_wv': _L0_ffn_in['wv'], 'L0_ffn_wo': _L0_ffn_in['wo'], 'L0_ffn_wr': _L0_ffn_in['wr'], 'L0_ffn_wg': _L0_ffn_in['wg'], 'L0_ffn_wu': _L0_ffn_in['wu'], 'L0_ffn_wd': _L0_ffn_in['wd']}
    _x0 = _d['L0_attn_u']
    _d['L0_attn_u'] = jax.random.normal(jax.random.fold_in(jax.random.key(seed), 1), (2, 1024, 128), dtype=_x0.dtype)
    del _x0
    return _d

def reference(L0_attn_u, L0_attn_in_proj_w, L0_attn_conv1d_w, L0_attn_conv1d_b, L0_attn_dt_bias, L0_attn_A_log, L0_attn_D_w, L0_attn_D_b, L0_attn_rms_w, L0_attn_outproj_w, L0_ffn_ln1_w, L0_ffn_ln2_w, L0_ffn_wq, L0_ffn_wk, L0_ffn_wv, L0_ffn_wo, L0_ffn_wr, L0_ffn_wg, L0_ffn_wu, L0_ffn_wd):

    def _L0_attn_ref(u, in_proj_w, conv1d_w, conv1d_b, dt_bias, A_log, D_w, D_b, rms_w, outproj_w):
        import jax, jax.numpy as jnp
        import numpy as np
        D_MODEL = 128
        D_STATE = 64
        D_CONV = 7
        EXPAND = 2
        HEADDIM = 64
        NGROUPS = 1
        D_INNER = EXPAND * D_MODEL
        NHEADS = D_INNER // HEADDIM
        D_XBC = D_INNER + 2 * (2 * NGROUPS * D_STATE)
        D_IN_PROJ = 2 * D_INNER + 2 * (2 * NGROUPS * D_STATE) + 2 * NHEADS
        RMS_EPS = 1e-05

        def _dwconv(x, w, b):
            C = x.shape[-1]
            out = jax.lax.conv_general_dilated(x.transpose(0, 2, 1), w, window_strides=(1,), padding='SAME', feature_group_count=C)
            return out.transpose(0, 2, 1) + b

        def _selective_scan(x, dt, A, Bm, Cm):
            b, l, h, p = x.shape
            g = Bm.shape[2]
            hpg = h // g
            Bh = jnp.repeat(Bm, hpg, axis=2)
            Ch = jnp.repeat(Cm, hpg, axis=2)
            decay = jnp.exp(dt * A)

            def step(hstate, inp):
                dec_t, dt_t, x_t, B_t, C_t = inp
                hstate = hstate * dec_t[..., None, None] + jnp.einsum('bh,bhn,bhp->bhpn', dt_t, B_t, x_t)
                y = jnp.einsum('bhpn,bhn->bhp', hstate, C_t)
                return (hstate, y)
            h0 = jnp.zeros((b, h, p, Bh.shape[-1]), x.dtype)
            xs = (decay.transpose(1, 0, 2), dt.transpose(1, 0, 2), x.transpose(1, 0, 2, 3), Bh.transpose(1, 0, 2, 3), Ch.transpose(1, 0, 2, 3))
            _, ys = jax.lax.scan(step, h0, xs)
            return ys.transpose(1, 0, 2, 3)
        B, L, _ = u.shape
        zxBCdt = u @ in_proj_w.T
        z = zxBCdt[..., :D_INNER]
        xBC_og = zxBCdt[..., D_INNER:D_INNER + D_XBC]
        dt = zxBCdt[..., D_INNER + D_XBC:]
        xBC = jax.nn.silu(_dwconv(xBC_og, conv1d_w, conv1d_b))
        x_og = xBC[..., :D_INNER]
        BC = xBC[..., D_INNER:]
        flip = lambda t: jnp.flip(t, axis=1)
        x2 = jnp.concatenate([x_og, flip(x_og)], axis=0)
        BC_f, BC_b = jnp.split(BC, 2, axis=-1)
        BC2 = jnp.concatenate([BC_f, flip(BC_b)], axis=0)
        Bm, Cm = jnp.split(BC2, 2, axis=-1)
        dt_f, dt_b = jnp.split(dt, 2, axis=-1)
        dt2 = jnp.concatenate([dt_f, flip(dt_b)], axis=0)
        x2 = x2.reshape(2 * B, L, NHEADS, HEADDIM)
        Bm = Bm.reshape(2 * B, L, NGROUPS, D_STATE)
        Cm = Cm.reshape(2 * B, L, NGROUPS, D_STATE)
        dt_eff = jax.nn.softplus(dt2 + dt_bias)
        A = -jnp.exp(A_log)
        scan = _selective_scan(x2, dt_eff, A, Bm, Cm)
        scan = scan.reshape(2 * B, L, D_INNER)
        y = jnp.concatenate([jnp.zeros_like(scan[:, :1]), scan[:, :-1]], axis=1)
        y = y[:B] + flip(y[B:])
        D = jnp.repeat(x_og @ D_w.T + D_b, HEADDIM, axis=-1)
        y = y + D * x_og
        rstd = jax.lax.rsqrt(jnp.mean(y * y, axis=-1, keepdims=True) + RMS_EPS)
        un = y * rstd * rms_w * jax.nn.silu(z)
        return un @ outproj_w.T

    def _L0_ffn_ref(hidden_states, ln1_w, ln2_w, wq, wk, wv, wo, wr, wg, wu, wd):
        import jax, jax.numpy as jnp
        import numpy as np
        L, H, NH, NKV, HD, FF, E, K = (4, 128, 16, 4, 64, 256, 8, 2)
        B, S = (2, 256)
        THETA, EPS = (10000.0, 1e-05)

        def _rms(x, w):
            return x * jax.lax.rsqrt(jnp.mean(x * x, axis=-1, keepdims=True) + EPS) * w

        def _rope_cos_sin(seq_len, head_dim, theta):
            inv = 1.0 / theta ** (jnp.arange(0, head_dim, 2, dtype=jnp.float32) / head_dim)
            f = jnp.arange(seq_len, dtype=jnp.float32)[:, None] * inv
            emb = jnp.concatenate([f, f], axis=-1)
            return (jnp.cos(emb), jnp.sin(emb))

        def _rot_half(x):
            h = x.shape[-1] // 2
            return jnp.concatenate([-x[..., h:], x[..., :h]], axis=-1)

        def _attention(x, wq, wk, wv, wo, cos, sin, causal_bias):
            b, s, _ = x.shape
            q = (x @ wq).reshape(b, s, NH, HD).transpose(0, 2, 1, 3)
            k = (x @ wk).reshape(b, s, NKV, HD).transpose(0, 2, 1, 3)
            v = (x @ wv).reshape(b, s, NKV, HD).transpose(0, 2, 1, 3)
            c = cos[None, None]
            sn = sin[None, None]
            q = q * c + _rot_half(q) * sn
            k = k * c + _rot_half(k) * sn
            rep = NH // NKV
            k = jnp.repeat(k, rep, axis=1)
            v = jnp.repeat(v, rep, axis=1)
            scores = jnp.einsum('bhqd,bhkd->bhqk', q, k) / jnp.sqrt(jnp.asarray(HD, x.dtype))
            scores = scores + causal_bias
            attn = jax.nn.softmax(scores, axis=-1)
            out = jnp.einsum('bhqk,bhkd->bhqd', attn, v)
            out = out.transpose(0, 2, 1, 3).reshape(b, s, NH * HD)
            return out @ wo

        def _moe(x, wr, wg, wu, wd):
            logits = x @ wr
            probs = jax.nn.softmax(logits, axis=-1)
            topv, topi = jax.lax.top_k(probs, K)
            topv = topv / jnp.sum(topv, axis=-1, keepdims=True)
            comb = jnp.sum(jax.nn.one_hot(topi, E, dtype=x.dtype) * topv[..., None], axis=-2)
            out = jnp.zeros_like(x)
            for e in range(E):
                h = jax.nn.silu(x @ wg[e]) * (x @ wu[e])
                out = out + comb[..., e:e + 1] * (h @ wd[e])
            return out
        s = hidden_states.shape[1]
        cos, sin = _rope_cos_sin(s, HD, THETA)
        causal_bias = jnp.where(jnp.tril(jnp.ones((s, s), bool))[None, None], 0.0, -1000000000.0).astype(hidden_states.dtype)
        x = hidden_states
        for l in range(L):
            res = x
            h = _rms(x, ln1_w[l])
            h = _attention(h, wq[l], wk[l], wv[l], wo[l], cos, sin, causal_bias)
            x = jnp.clip(res + h, -100.0, 100.0)
            res = x
            h = _rms(x, ln2_w[l])
            h = _moe(h, wr[l], wg[l], wu[l], wd[l])
            x = jnp.clip(res + h, -100.0, 100.0)
        return x
    x = L0_attn_u
    x = _layernorm(x + _L0_attn_ref(x, L0_attn_in_proj_w, L0_attn_conv1d_w, L0_attn_conv1d_b, L0_attn_dt_bias, L0_attn_A_log, L0_attn_D_w, L0_attn_D_b, L0_attn_rms_w, L0_attn_outproj_w), axis=-1)
    x = _layernorm(x + _L0_ffn_ref(x, L0_ffn_ln1_w, L0_ffn_ln2_w, L0_ffn_wq, L0_ffn_wk, L0_ffn_wv, L0_ffn_wo, L0_ffn_wr, L0_ffn_wg, L0_ffn_wu, L0_ffn_wd), axis=-1)
    return x

_drawn_inputs = setup_inputs


def setup_inputs(seed=0):
    import zlib

    import numpy as np

    out = dict(_drawn_inputs(seed))
    spreads = {'L0_attn_conv1d_b': (0.0, 0.321),
     'L0_attn_A_log': (0.0, 0.8),
     'L0_attn_D_b': (0.0, 0.1),
     'L0_attn_rms_w': (1.0, 0.6),
     'L0_ffn_ln1_w': (1.0, 0.6),
     'L0_ffn_ln2_w': (1.0, 0.6)}
    factors = {'L0_attn_dt_bias': 64.0,
     'L0_attn_D_w': 6.646,
     'L0_ffn_wq': 8.0,
     'L0_ffn_wk': 8.0,
     'L0_ffn_wv': 4.134,
     'L0_ffn_wo': 4.212,
     'L0_ffn_wr': 8.0,
     'L0_ffn_wg': 8.0,
     'L0_ffn_wu': 8.0,
     'L0_ffn_wd': 8.0}
    for name, (base, spread) in spreads.items():
        noise = np.random.default_rng([zlib.crc32(name.encode()), seed]).standard_normal(out[name].shape)
        drawn = base * np.exp(spread * noise) if base else spread * noise
        out[name] = jnp.asarray(drawn.astype(out[name].dtype))
    for name, factor in factors.items():
        out[name] = (out[name] * factor).astype(out[name].dtype)
    return out
```

```python
from contextlib import ExitStack

import numpy as np
import concourse.bass as bass
from concourse import mybir

F32 = mybir.dt.float32
F32R = mybir.dt.float32r
BF16 = mybir.dt.bfloat16
U32 = mybir.dt.uint32
ALU = mybir.AluOpType
ACT = mybir.ActivationFunctionType
AX = mybir.AxisListType

P = 128
BATCH, SEQ, DM = 2, 1024, 128
TOK = BATCH * SEQ
NT = TOK // P
TB = SEQ // P
CW = 512
NC4 = TOK // CW

SH, SP, SN = 4, 64, 64
DI = SH * SP
TAPS = 7
PAD = TAPS // 2
RMS_EPS = 1e-5

LAYERS, NH, NKV, HD, FF, NE = 4, 16, 4, 64, 256, 8
REP = NH // NKV
QW = REP * HD
WQKV = 2 * QW + 2 * P
WLAY = 2 + NE + NKV * HD
WEXP = 3 * FF
THETA, EPS = 10000.0, 1e-5
CLIP = 100.0

UNITS = [(b, p, qt, hh) for b in range(BATCH) for p in range(REP // 2) for qt in range(TB) for hh in range(2)]
NU = len(UNITS)
WIDE = [qt >= 4 for _, _, qt, _ in UNITS]
N_WIDE = sum(WIDE)


def wide_upto(u):
    return sum(WIDE[:u + 1])


CHUNKS = [(u, part) for u in range(NU) for part in range(2 if WIDE[u] else 1)]
CHUNK_OF = {c: n for n, c in enumerate(CHUNKS)}
ROPES = NC4 * 3
GU = NC4 * 2
ITER_GU, ITER_Y = 2 * GU, 2 * NC4


def build(nc, u_tok, u_feat, w_in, conv_w, w_scan_out, rope, w_attn, w_o, w_layer, w_expert, out):
    with ExitStack() as ctx:
        def sb(name, shape, dt=F32):
            return ctx.enter_context(nc.sbuf_tensor(name, shape, dt))

        def sem(name):
            return ctx.enter_context(nc.semaphore(name))

        x = sb("x", [P, NT, DM])
        x1 = sb("x1", [P, NT, DM])
        hT = sb("hT", [P, TOK])
        cos_t = sb("cos_t", [P, SEQ])
        sin_t = sb("sin_t", [P, SEQ])
        wqkv = sb("wqkv", [P, WQKV])
        wo = sb("wo", [P, 2, DM])
        wlay = sb("wlay", [P, WLAY])
        wexp = sb("wexp", [P, 2, WEXP])
        ident = sb("ident", [P, P])
        ident_b = sb("ident_b", [P, P], BF16)
        causal_b = sb("causal_b", [P, P], BF16)
        iota8 = sb("iota8", [P, NE])
        sq = sb("sq", [P, DM])
        ssq = sb("ssq", [P, NT])
        var = sb("var", [P, NT])
        rstd = sb("rstd", [P, NT])
        mean_var = sb("mean_var", [P, NT, 2])
        bn = sb("bn", [P, 2, 6])
        neg_half = sb("neg_half", [P, NT])
        negmax = sb("negmax", [P, NU])
        rowsum = sb("rowsum", [P, NU])
        rrow = sb("rrow", [P, NU])
        pr = sb("pr", [P, NT, NE])
        pe_ = sb("pe_", [P, NT, NE])
        top = sb("top", [P, NT, 8])
        topi = sb("topi", [P, NT, 8], U32)
        topif = sb("topif", [P, NT, 8])
        r1 = sb("r1", [P, NT])
        r2 = sb("r2", [P, NT])
        wtop = sb("wtop", [P, NT, 2])
        comb = sb("comb", [P, NT, NE])
        qs = sb("qs", [P, REP, TOK], F32R)
        k_hi = sb("k_hi", [P, TOK], F32R)
        k_lo = sb("k_lo", [P, TOK], F32R)

        arena = sb("arena", [P, 19488])
        at = [0]

        def cut(*dims, new=False):
            if new:
                at[0] = 0
            n = int(np.prod(dims))
            v = arena[:, at[0]:at[0] + n]
            at[0] += n
            assert at[0] <= 19488
            if len(dims) == 2:
                v = v.rearrange("p (a b) -> p a b", b=dims[1])
            if len(dims) == 3:
                v = v.rearrange("p (a b c) -> p a b c", b=dims[1], c=dims[2])
            return v

        ra = cut(2, CW, new=True)
        rb = cut(2, CW)
        v_all = cut(NT, NKV * HD)
        v_g = cut(NT, HD)
        prob = cut(3, SEQ)
        prob_t = cut(4, TB, P)
        o_t = cut(2, TOK)
        hn = o_t.rearrange("p a b -> p (a b)")[:, 0:TOK].rearrange("p (t d) -> p t d", d=DM)
        sg = prob_t[:, 0]
        sg = sg.rearrange("p a b -> p (a b)").rearrange("p (a b) -> p a b", b=CW)
        a_t = prob_t[:, 1:3].rearrange("p a b c -> p (a b c)").rearrange("p (s f n) -> p s f n", s=2, f=2)

        SEQP = SEQ + 2 * PAD
        proj = cut(4, SEQP, new=True)
        xbT = cut(3, TOK)
        c_pad = cut(BATCH, SEQ + 2)
        xb = cut(NT, DI + P)
        state = cut(BATCH, DI)
        mask4 = cut(2, SH * P // 2)
        y = xbT.rearrange("p a b -> p (a b)")[:, 0:NT * DI].rearrange("p (t d) -> p t d", d=DI)
        flat = proj.rearrange("p a b -> p (a b)")
        a_u = flat[:, 0:1024].rearrange("p (r h t) -> p r h t", r=2, h=SH)
        dec = flat[:, 1024:2048].rearrange("p (r h t) -> p r h t", r=2, h=SH)
        mix = flat[:, 2048:3072].rearrange("p (r h t) -> p r h t", r=2, h=SH)
        xw = flat[:, 3072:3584].rearrange("p (r d) -> p r d", r=2)
        tmp = flat[:, 3584:3840]
        tmp_h = flat[:, 3840:4096]
        unT = flat[:, 0:2 * TOK].rearrange("p (j t) -> p j t", j=2)
        mask4_b = mask4.bitcast(BF16)
        wsm = sb("wsm", [P, 4 * P + DI + 8])
        wout = wqkv[:, 0:2 * DM].rearrange("p (j d) -> p j d", j=2)
        dw = wqkv[:, 256:264].rearrange("p (j h) -> p j h", j=2)
        cw = wqkv[:, 264:264 + 4 * TAPS].rearrange("p (j k) -> p j k", j=4)
        cb = wqkv[:, 292:296]
        rmsw = wqkv[:, 296:298]
        hc = wqkv[:, 298:298 + 20]
        tri = prob_tri = sb("tri", [P, 4, P])
        ones = sb("ones", [P, P])
        dtr = sb("dtr", [P, NT, 8])
        dt_e = sb("dt_e", [P, NT, 8])
        dt_u = sb("dt_u", [P, NT, 8])
        dt_l = sb("dt_l", [P, NT, 8])
        dt_z = sb("dt_z", [P, NT, 8])
        dt_s = sb("dt_s", [P, NT, 8])
        a_dt = sb("a_dt", [P, NT, 8])
        ncum = sb("ncum", [P, NT, 8])
        exp_e = sb("exp_e", [P, NT, 8])
        exp_w = sb("exp_w", [P, NT, 8])
        exp_t = sb("exp_t", [P, NT, 8])
        d_t = sb("d_t", [P, NT, SH])
        exp_a = sb("exp_a", [P, 8])

        ps_s = ctx.enter_context(nc.psum_tensor("ps_s", [P, 2, 2 * CW], F32))
        ps_t = ctx.enter_context(nc.psum_tensor("ps_t", [P, 2, CW], F32))
        ps_o = ctx.enter_context(nc.psum_tensor("ps_o", [P, 2, CW], F32))

        def bank(i):
            if i < 4:
                return ps_s[:, i // 2, (i % 2) * CW:(i % 2 + 1) * CW]
            return (ps_t if i < 6 else ps_o)[:, i % 2, :]

        s_const = sem("s_const")
        s_cstep = sem("s_cstep")
        s_in = sem("s_in")
        s_u = sem("s_u")
        s_wa = sem("s_wa")
        s_wo = sem("s_wo")
        s_wl = sem("s_wl")
        s_we = [sem("s_we0"), sem("s_we1")]
        s_out = sem("s_out")
        s_pj = sem("s_pj")
        s_pje = sem("s_pje")
        s_conv = sem("s_conv")
        s_silu = sem("s_silu")
        s_vs = sem("s_vs")
        s_as = sem("s_as")
        s_tr = sem("s_tr")
        s_tre = sem("s_tre")
        s_dd = sem("s_dd")
        s_cum = sem("s_cum")
        s_coef = sem("s_coef")
        s_yi = sem("s_yi")
        s_au = sem("s_au")
        s_xw = sem("s_xw")
        s_eg = sem("s_eg")
        s_dec = sem("s_dec")
        s_mix = sem("s_mix")
        s_y = sem("s_y")
        s_yr = sem("s_yr")
        s_z = sem("s_z")
        s_zs = sem("s_zs")
        s_pow = sem("s_pow")
        s_var = sem("s_var")
        s_un = sem("s_un")
        s_unt = sem("s_unt")
        s_une = sem("s_une")
        s_so = sem("s_so")
        s_x = sem("s_x")
        s_x1 = sem("s_x1")
        s_hn = sem("s_hn")
        s_nt = sem("s_nt")
        s_ht = sem("s_ht")
        s_vn = sem("s_vn")
        s_v = sem("s_v")
        s_ve = sem("s_ve")
        s_vg = sem("s_vg")
        s_qk = sem("s_qk")
        s_rm = sem("s_rm")
        s_rs = sem("s_rs")
        s_hi = sem("s_hi")
        s_lo = sem("s_lo")
        s_s = sem("s_s")
        s_m = sem("s_m")
        s_e = sem("s_e")
        s_r = sem("s_r")
        s_p = sem("s_p")
        s_ta = sem("s_ta")
        s_tb = sem("s_tb")
        s_ea = sem("s_ea")
        s_eb = sem("s_eb")
        s_pv = sem("s_pv")
        s_oe = sem("s_oe")
        s_ow = sem("s_ow")
        s_xa = sem("s_xa")
        s_rt = sem("s_rt")
        s_rmax = sem("s_rmax")
        s_alone = sem("s_alone")
        s_clip = sem("s_clip")
        s_rv = sem("s_rv")
        s_re = sem("s_re")
        s_gu = sem("s_gu")
        s_sg = sem("s_sg")
        s_a = sem("s_a")
        s_dn = sem("s_dn")
        s_ya = sem("s_ya")
        s_fin = sem("s_fin")

        block = ctx.enter_context(nc.Block())

        def scan_unit(v):
            c, b, d = v // 4, v // 2 % 2, v % 2
            return c, b, d, b * TB + (c if d == 0 else TB - 1 - c)

        NV = 4 * TB

        def c_cols(t, d):
            b, lo = t // TB, t % TB * P
            return c_pad[d * SN:(d + 1) * SN, b, lo + 2 * d:lo + 2 * d + P]

        @block.sync
        def _(sp):
            sp.dma_start(wsm[:, :], w_in).then_inc(s_in, 16)
            sp.dma_start(hT[:, :], u_feat).then_inc(s_in, 16)
            sp.dma_start(wqkv[:, 264:318], conv_w).then_inc(s_in, 16)
            sp.dma_start(wqkv[:, 0:264], w_scan_out).then_inc(s_in, 16)
            sp.dma_start(x[:, :, :], u_tok).then_inc(s_u, 16)
            sp.dma_start(cos_t[:, :], rope[0]).then_inc(s_u, 16)
            sp.dma_start(sin_t[:, :], rope[1]).then_inc(s_u, 16)
            sp.dma_start(wlay[:, :], w_layer[0]).then_inc(s_wl, 16)
            sp.dma_start(wo[:, :, :], w_o[0]).then_inc(s_wo, 16)
            for q in range(2):
                sp.dma_start(wexp[:, q, :], w_expert[q]).then_inc(s_we[q], 16)
            sp.wait_ge(s_x, 1)
            sp.dma_start(wqkv[:, :], w_attn[0]).then_inc(s_wa, 16)
            with sp.Fori(0, LAYERS) as layer:
                with sp.Fori(0, NKV) as g:
                    it = layer * NKV + g
                    sp.wait_ge(s_qk, it * ROPES + ROPES)
                    sp.dma_start(wqkv[:, :], w_attn[it + 1]).then_inc(s_wa, 16)
                    sp.wait_ge(s_ow, it * 4 + 4)
                    sp.dma_start(wo[:, :, :], w_o[it + 1]).then_inc(s_wo, 16)
                sp.wait_ge(s_rt, layer + 1)
                sp.dma_start(wlay[:, :], w_layer[layer + 1]).then_inc(s_wl, 16)
                with sp.Fori(0, NE // 2) as e2:
                    it = layer * (NE // 2) + e2
                    for q in range(2):
                        sp.wait_ge(s_dn, it * ITER_Y + (q + 1) * NC4)
                        sp.dma_start(wexp[:, q, :], w_expert[it * 2 + 2 + q]).then_inc(s_we[q], 16)
            for c in range(NC4):
                sp.wait_ge(s_fin, c + 1)
                sp.dma_start(out[:, 4 * c:4 * c + 4, :], x[:, 4 * c:4 * c + 4, :]).then_inc(s_out, 16)
            sp.wait_ge(s_out, 16 * NC4)
            sp.wait_ge(s_wa, 16 * (LAYERS * NKV + 1))
            sp.wait_ge(s_wo, 16 * (LAYERS * NKV + 1))
            sp.wait_ge(s_wl, 16 * (LAYERS + 1))
            for q in range(2):
                sp.wait_ge(s_we[q], 16 * (LAYERS * NE // 2 + 1))

        @block.gpsimd
        def _(pool):
            steps = [0]

            def fill(ap, value):
                steps[0] += 1
                pool.memset(ap, value).then_inc(s_cstep, 1)
                return steps[0]

            def keep(ap, pattern, base, ch, fill_value):
                pool.affine_select(out=ap, in_=ap, compare_op=ALU.is_ge, fill=fill_value, base=base,
                                   pattern=pattern, channel_multiplier=ch).then_inc(s_const, 1)

            fill(ident[:, :], 0.0)
            fill(ident_b[:, :], 0.0)
            fill(causal_b[:, :], 0.0)
            fill(mask4_b[:, :, :], 0.0)
            fill(tri[:, :, :], 1.0)
            fill(ones[:, :], 1.0)
            fill(neg_half[:, :], -0.5)
            fill(proj[:, :, 0:PAD], 0.0)
            fill(proj[:, :, PAD + SEQ:SEQP], 0.0)
            fill(c_pad[:, :, 0:1], 0.0)
            fill(c_pad[:, :, SEQ + 1:SEQ + 2], 0.0)
            pool.wait_ge(s_cstep, steps[0])
            for m in (ident, ident_b):
                pool.affine_select(out=m[:, :], in_=m[:, :], compare_op=ALU.not_equal, fill=1.0, base=0,
                                   pattern=[[-1, P]], channel_multiplier=1).then_inc(s_const, 1)
            keep(causal_b[:, :], [[-1, P]], 0, 1, -1e9)
            keep(mask4_b[:, 0, :].rearrange("p (h t) -> p h t", h=SH), [[0, SH], [1, P]], -1, -1, -1e30)
            keep(mask4_b[:, 1, :].rearrange("p (h t) -> p h t", h=SH), [[0, SH], [-1, P]], -1, 1, -1e30)
            keep(tri[:, 0, :], [[1, P]], 0, -1, 0.0)
            keep(tri[:, 1, :], [[-1, P]], 0, 1, 0.0)
            keep(tri[:, 2, :], [[1, P]], -1, -1, 0.0)
            keep(tri[:, 3, :], [[-1, P]], -1, 1, 0.0)
            pool.iota(iota8[:, :], pattern=[[1, NE]], base=0, channel_multiplier=0,
                      allow_small_or_imprecise_dtypes=True).then_inc(s_const, 1)

            pool.wait_ge(s_coef, 1)
            pool.wait_ge(s_tre, NT)
            for t in range(NT):
                ins = pool.tensor_tensor(
                    y[:, t, :].rearrange("p (h e) -> p h e", h=SH),
                    xb[:, t, 0:DI].rearrange("p (h e) -> p h e", h=SH),
                    d_t[:, t, :].unsqueeze(2).to_broadcast([P, SH, SP]), ALU.mult)
            ins.then_inc(s_yi, 1)
            pool.wait_ge(s_coef, 2)
            for v in range(NV):
                c, b, d, t = scan_unit(v)
                if v >= 2:
                    pool.wait_ge(s_eg, v - 1)
                pool.tensor_tensor(
                    a_u[:, v % 2], tri[:, 2 + d, :].unsqueeze(1).to_broadcast([P, SH, P]),
                    a_dt[:, t, d * SH:(d + 1) * SH].unsqueeze(2).to_broadcast([P, SH, P]), ALU.mult)\
                    .then_inc(s_au, 1)
                if v >= 2:
                    pool.wait_ge(s_y, v - 1)
                pool.tensor_tensor(
                    xw[:, v % 2, :].rearrange("p (h e) -> p h e", h=SH),
                    xb[:, t, 0:DI].rearrange("p (h e) -> p h e", h=SH),
                    exp_w[:, t, d * SH:(d + 1) * SH].unsqueeze(2).to_broadcast([P, SH, SP]), ALU.mult)\
                    .then_inc(s_xw, 1)

            def root(n):
                pool.wait_ge(s_var, n)
                pool.tensor_tensor(rstd[:, :], var[:, :], neg_half[:, :], ALU.pow).then_inc(s_pow, 1)

            root(1)
            root(2)
            pool.wait_ge(s_x, 2)
            pool.tensor_copy(x1[:, :, :], x[:, :, :]).then_inc(s_x1, 1)
            with pool.Fori(0, LAYERS) as layer:
                root(layer * 2 + 3)
                with pool.Fori(0, NKV) as g:
                    it = layer * NKV + g
                    pool.wait_ge(s_ve, layer * (NT // 2) + NT // 2)
                    pool.wait_ge(s_qk, it * ROPES + 1)
                    pool.tensor_copy(v_g[:, :, :], v_all[:, :, bass.ts(g, HD)]).then_inc(s_vg, 1)
                    for i in range(ROPES):
                        pool.wait_ge(s_rm, it * ROPES + i + 1)
                        pool.tensor_tensor(ra[:, i % 2, :], ra[:, i % 2, :], rb[:, i % 2, :], ALU.add)\
                            .then_inc(s_rs, 1)
                root(layer * 2 + 4)
            root(2 * LAYERS + 3)

        @block.scalar
        def _(act):
            for b in range(BATCH):
                for j in range(4):
                    for c in range(2):
                        i = (b * 4 + j) * 2 + c
                        act.wait_ge(s_pj, i + 1)
                        if b == 1 and c == 0:
                            act.wait_ge(s_conv, j + 1)
                        act.activation(proj[:, j, PAD + c * CW:PAD + (c + 1) * CW], bank(i % 8), ACT.Copy)\
                            .then_inc(s_pje, 1)
                if b == 0:
                    pass
                for j in range(4):
                    act.wait_ge(s_conv, b * 4 + j + 1)
                    dst = xbT[:, j, b * SEQ:(b + 1) * SEQ] if j < 3 else c_pad[:, b, 1:SEQ + 1]
                    act.activation(dst, dst, ACT.Silu).then_inc(s_silu, 1)
            for t in range(NT):
                act.wait_ge(s_tr, t + 1)
                act.activation(xb[:, t, :], bank(t % 4)[:, 0:DI + P], ACT.Copy).then_inc(s_tre, 1)
            act.activation(exp_a[:, :], hc[:, 8:16], ACT.Exp).then_inc(s_as, 1)
            act.wait_ge(s_vs, 3)
            act.activation(dt_e[:, :, :], dt_u[:, :, :], ACT.Exp, scale=-1.0).then_inc(s_as, 1)
            act.wait_ge(s_vs, 4)
            act.activation(dt_l[:, :, :], dt_u[:, :, :], ACT.Ln).then_inc(s_as, 1)
            act.wait_ge(s_cum, 1)
            act.activation(exp_t[:, :, :], bank(5)[:, 0:P].rearrange("p (t h) -> p t h", h=8), ACT.Exp)\
                .then_inc(s_as, 1)
            act.wait_ge(s_vs, 14)
            act.activation(exp_e[:, :, :], exp_e[:, :, :], ACT.Exp).then_inc(s_as, 1)
            act.wait_ge(s_vs, 15)
            act.activation(exp_w[:, :, :], exp_w[:, :, :], ACT.Exp).then_inc(s_as, 1)
            act.wait_ge(s_vs, 13)
            for v in range(NV):
                c, b, d, t = scan_unit(v)
                act.wait_ge(s_eg, v + 1)
                if v >= 2:
                    act.wait_ge(s_mix, v - 1)
                for h in range(SH):
                    ins = act.activation(dec[:, v % 2, h, :], bank(v % 2)[:, h * P:(h + 1) * P], ACT.Exp,
                                         bias=ncum[:, t, d * SH + h:d * SH + h + 1])
                ins.then_inc(s_dec, 1)
            for i in range(NT // 2):
                act.wait_ge(s_z, i + 1)
                act.activation(xb[:, 2 * i:2 * i + 2, 0:DI],
                               bank(i % 4).rearrange("p (t d) -> p t d", t=2), ACT.Silu).then_inc(s_zs, 1)
            for i in range(NT // 2):
                act.wait_ge(s_unt, i + 1)
                src = bank(4 + i % 2).rearrange("p (t j n) -> p j t n", t=2, j=2)
                for j in range(2):
                    ins = act.activation(
                        unT[:, j, i * 2 * P:(i + 1) * 2 * P].rearrange("p (t n) -> p t n", t=2),
                        src[:, j], ACT.Copy, scale=rmsw[:, j:j + 1])
                ins.then_inc(s_une, 1)

            def norm_out(n, w):
                for c in range(NC4):
                    act.wait_ge(s_nt, n * NC4 + c + 1)
                    act.activation(hT[:, c * CW:(c + 1) * CW], bank(c), ACT.Copy, scale=wlay[:, w:w + 1])\
                        .then_inc(s_ht, 1)

            with act.Fori(0, LAYERS) as layer:
                act.wait_ge(s_wl, layer * 16 + 16)
                norm_out(layer * 2, 0)
                for i in range(NT // 2):
                    act.wait_ge(s_v, layer * (NT // 2) + i + 1)
                    act.activation(v_all[:, 2 * i:2 * i + 2, :],
                                   bank(4 + i % 4).rearrange("p (t n) -> p t n", t=2), ACT.Copy)\
                        .then_inc(s_ve, 1)
                with act.Fori(0, NKV) as g:
                    it = layer * NKV + g
                    for i in range(ROPES):
                        c, what = i // 3, i % 3
                        cols = slice(c * CW, (c + 1) * CW)
                        act.wait_ge(s_rs, it * ROPES + i + 1)
                        if what == 0:
                            act.activation(k_hi[:, cols], ra[:, i % 2, :], ACT.Copy).then_inc(s_hi, 1)
                        else:
                            h = 2 * (what - 1)
                            act.activation(qs[0:HD, h, cols], ra[0:HD, i % 2, :], ACT.Copy,
                                           scale=HD ** -0.5)
                            act.activation(qs[HD:P, h + 1, cols], ra[HD:P, i % 2, :], ACT.Copy,
                                           scale=HD ** -0.5).then_inc(s_hi, 1)
                    for s in range(NU + 2):
                        if s < NU:
                            act.wait_ge(s_m, it * NU + s + 1)
                            if s >= 3:
                                act.wait_ge(s_ta, it * NU + s - 2)
                                if WIDE[s - 3]:
                                    act.wait_ge(s_tb, it * N_WIDE + wide_upto(s - 3))
                            w = (UNITS[s][2] + 1) * P
                            act.activation(prob[:, s % 3, 0:w], ps_s[:, s % 2, 0:w], ACT.Exp,
                                           bias=negmax[:, s:s + 1], accum_out=rowsum[:, s:s + 1])\
                                .then_inc(s_e, 1)
                        u = s - 2
                        if u >= 0:
                            n = CHUNK_OF[(u, 0)]
                            k = min(UNITS[u][2] + 1, 4)
                            act.wait_ge(s_ta, it * NU + u + 1)
                            if u >= 4:
                                act.wait_ge(s_pv, it * (NU // 2) + (u - 4) // 2 + 1)
                            act.activation(prob_t[:, u % 4, 0:k, :],
                                           ps_t[:, n % 2, 0:k * P].rearrange("p (k n) -> p k n", n=P),
                                           ACT.Copy).then_inc(s_ea, 1)
                norm_out(layer * 2 + 1, 1)
                act.wait_ge(s_rv, layer * 14 + 2)
                act.activation(pe_[:, :, :], pe_[:, :, :], ACT.Exp).then_inc(s_re, 1)
                with act.Fori(0, NE // 2) as e2:
                    it = layer * (NE // 2) + e2
                    for m in range(ITER_GU):
                        act.wait_ge(s_gu, it * ITER_GU + m + 1)
                        if m >= 2:
                            act.wait_ge(s_a, it * ITER_GU + m - 1)
                        r = m % 3
                        act.activation(sg[:, m % 2, :], bank(2 * r), ACT.Silu).then_inc(s_sg, 1)

        @block.vector
        def _(dve):
            vs = [0]

            def step(ins):
                vs[0] += 1
                ins.then_inc(s_vs, 1)
                dve.wait_ge(s_vs, vs[0])

            dve.wait_ge(s_in, 64)
            dve.wait_ge(s_cstep, 11)
            cstep = [0]
            for b in range(BATCH):
                for j in range(4):
                    dve.wait_ge(s_pje, (b * 4 + j) * 2 + 2)
                    dst = xbT[:, j, b * SEQ:(b + 1) * SEQ] if j < 3 else c_pad[:, b, 1:SEQ + 1]
                    dve.tensor_scalar(dst, proj[:, j, 0:SEQ], cw[:, j, 0:1], cb[:, j:j + 1], ALU.mult, ALU.add)\
                        .then_inc(s_vn, 1)
                    for k in range(1, TAPS):
                        cstep[0] += 1
                        dve.wait_ge(s_vn, cstep[0])
                        ins = dve.scalar_tensor_tensor(out=dst, in0=proj[:, j, k:k + SEQ], scalar=cw[:, j, k:k + 1],
                                                       in1=dst, op0=ALU.mult, op1=ALU.add)
                        ins.then_inc(s_vn if k < TAPS - 1 else s_conv, 1)
            N_CONV = cstep[0]
            dve.wait_ge(s_dd, 1)
            dve.tensor_tensor(d_t[:, :, :], bank(7)[:, 0:NT * SH].rearrange("p (t h) -> p t h", h=SH),
                              hc[:, 16:20].unsqueeze(1).to_broadcast([P, NT, SH]), ALU.add).then_inc(s_coef, 1)
            step(dve.tensor_tensor(dtr[:, :, :], bank(7)[:, P:2 * P].rearrange("p (t h) -> p t h", h=8),
                                   hc[:, 0:8].unsqueeze(1).to_broadcast([P, NT, 8]), ALU.add))
            step(dve.tensor_scalar(dt_s[:, :, :], dtr[:, :, :], 0.0, None, ALU.max))
            step(dve.scalar_tensor_tensor(out=dt_u[:, :, :], in0=dtr[:, :, :], scalar=-1.0, in1=dtr[:, :, :],
                                          op0=ALU.mult, op1=ALU.max))
            dve.wait_ge(s_as, 2)
            step(dve.tensor_scalar(dt_u[:, :, :], dt_e[:, :, :], 1.0, None, ALU.add))
            step(dve.tensor_scalar(dt_z[:, :, :], dt_u[:, :, :], 1.0, None, ALU.is_equal))
            step(dve.scalar_tensor_tensor(out=dtr[:, :, :], in0=dt_u[:, :, :], scalar=-1.0, in1=dt_z[:, :, :],
                                          op0=ALU.add, op1=ALU.add))
            step(dve.reciprocal(dtr[:, :, :], dtr[:, :, :]))
            dve.wait_ge(s_as, 3)
            step(dve.tensor_tensor(dtr[:, :, :], dtr[:, :, :], dt_l[:, :, :], ALU.mult))
            step(dve.tensor_tensor(dtr[:, :, :], dtr[:, :, :], dt_z[:, :, :], ALU.add))
            step(dve.tensor_tensor(dtr[:, :, :], dtr[:, :, :], dt_e[:, :, :], ALU.mult))
            step(dve.tensor_tensor(dt_s[:, :, :], dt_s[:, :, :], dtr[:, :, :], ALU.add))
            step(dve.scalar_tensor_tensor(out=a_dt[:, :, :], in0=dt_s[:, :, :], scalar=-1.0,
                                          in1=exp_a[:, :].unsqueeze(1).to_broadcast([P, NT, 8]),
                                          op0=ALU.mult, op1=ALU.mult))
            dve.wait_ge(s_cum, 1)
            step(dve.tensor_scalar(ncum[:, :, :], bank(4)[:, 0:P].rearrange("p (t h) -> p t h", h=8),
                                   -1.0, None, ALU.mult))
            step(dve.scalar_tensor_tensor(out=exp_e[:, :, :], in0=ncum[:, :, :], scalar=-1.0, in1=a_dt[:, :, :],
                                          op0=ALU.mult, op1=ALU.subtract))
            dve.wait_ge(s_as, 4)
            step(dve.tensor_tensor(exp_w[:, :, :], bank(5)[:, 0:P].rearrange("p (t h) -> p t h", h=8),
                                   ncum[:, :, :], ALU.add))
            dve.wait_ge(s_as, 6)
            dve.tensor_tensor(exp_w[:, :, :], exp_w[:, :, :], dt_s[:, :, :], ALU.mult).then_inc(s_coef, 1)

            def combine(v):
                c, b, d, t = scan_unit(v)
                rows = slice(d * SN, (d + 1) * SN)
                dh = slice(d * SH, (d + 1) * SH)
                dve.wait_ge(s_y, v + 1)
                if c > 0:
                    dve.tensor_tensor(tmp_h[rows, :].rearrange("p (h e) -> p h e", h=SH),
                                      state[rows, b, :].rearrange("p (h e) -> p h e", h=SH),
                                      exp_t[rows, t, dh].unsqueeze(2).to_broadcast([SN, SH, SP]), ALU.mult)\
                        .then_inc(s_vs, 1)
                    step(dve.tensor_tensor(tmp[:, :].rearrange("p (h e) -> p h e", h=SH),
                                           bank(4 + v % 2)[:, DI:2 * DI].rearrange("p (h e) -> p h e", h=SH),
                                           exp_e[:, t, dh].unsqueeze(2).to_broadcast([P, SH, SP]), ALU.mult))
                    vs[0] += 1
                    dve.wait_ge(s_vs, vs[0])
                    dve.tensor_tensor(state[rows, b, :], tmp_h[rows, :], bank(6 + v % 2)[rows, 0:DI], ALU.add)\
                        .then_inc(s_vs, 1)
                    step(dve.tensor_tensor(tmp[:, :], tmp[:, :], bank(4 + v % 2)[:, 0:DI], ALU.add))
                    vs[0] += 1
                    dve.wait_ge(s_vs, vs[0])
                    dve.tensor_tensor(y[:, t, :], y[:, t, :], tmp[:, :], ALU.add).then_inc(s_yr, 1)
                else:
                    dve.tensor_copy(state[rows, b, :], bank(6 + v % 2)[rows, 0:DI])
                    dve.tensor_tensor(y[:, t, :], y[:, t, :], bank(4 + v % 2)[:, 0:DI], ALU.add)\
                        .then_inc(s_yr, 1)
                dve.wait_ge(s_yr, v + 1)

            dve.wait_ge(s_yi, 1)
            for v in range(NV + 1):
                if v < NV:
                    c, b, d, t = scan_unit(v)
                    dve.wait_ge(s_dec, v + 1)
                    if v >= 2:
                        dve.wait_ge(s_y, v - 1)
                    for h in range(SH):
                        ins = dve.scalar_tensor_tensor(
                            out=mix[:, v % 2, h, :], in0=dec[:, v % 2, h, :],
                            scalar=dt_s[:, t, d * SH + h:d * SH + h + 1], in1=bank(2 + v % 2)[:, 0:P],
                            op0=ALU.mult, op1=ALU.mult)
                    ins.then_inc(s_mix, 1)
                if v >= 1:
                    combine(v - 1)

            def squares(src, width, chain):
                for t in range(NT):
                    ins = dve.tensor_tensor_reduce(out=sq_for(width, t), in0=src[:, t, :], in1=src[:, t, :], scale=1.0,
                                                   scalar=0.0, op0=ALU.mult, op1=ALU.add,
                                                   accum_out=ssq[:, t:t + 1])
                chain(ins)
                dve.tensor_scalar(var[:, :], ssq[:, :], 1.0 / width, EPS, ALU.mult, ALU.add).then_inc(s_var, 1)

            def sq_for(width, t):
                return hn[:, t, :] if width == DM else flat[:, t * DI:(t + 1) * DI]

            squares(y, DI, step)
            dve.wait_ge(s_pow, 1)
            for t in range(NT):
                dve.wait_ge(s_zs, t // 2 + 1)
                dve.scalar_tensor_tensor(out=y[:, t, :], in0=y[:, t, :], scalar=rstd[:, t:t + 1],
                                         in1=xb[:, t, 0:DI], op0=ALU.mult, op1=ALU.mult).then_inc(s_un, 1)
            for c in range(NC4):
                dve.wait_ge(s_so, c + 1)
                if c == 0:
                    dve.wait_ge(s_u, 48)
                ins = dve.tensor_tensor(x[:, 4 * c:4 * c + 4, :], bank(c).rearrange("p (t d) -> p t d", t=4),
                                        x[:, 4 * c:4 * c + 4, :], ALU.add)
            ins.then_inc(s_x, 1)
            dve.wait_ge(s_x, 1)

            def moments(chain):
                for t in range(NT):
                    if t >= 2:
                        pass
                    chain(dve.bn_stats(bn[:, t % 2, :], x[:, t, :]))
                    ins = dve.bn_aggr(mean_var[:, t, :], bn[:, t % 2, :])
                chain(ins)
                dve.tensor_scalar(var[:, :], mean_var[:, :, 1], EPS, None, ALU.add).then_inc(s_var, 1)

            moments(step)
            dve.wait_ge(s_pow, 2)
            for t in range(NT):
                ins = dve.tensor_scalar(x[:, t, :], x[:, t, :], mean_var[:, t, 0:1], rstd[:, t:t + 1],
                                        ALU.subtract, ALU.mult)
            ins.then_inc(s_x, 1)
            dve.wait_ge(s_x, 2)

            def norm(n, first):
                def chain(ins):
                    ins.then_inc(s_vn, 1)
                    dve.wait_ge(s_vn, N_CONV + n + 1)
                squares(x, DM, chain)
                dve.wait_ge(s_pow, n + 3)
                for t in range(NT):
                    ins = dve.tensor_scalar(hn[:, t, :], x[:, t, :], rstd[:, t:t + 1], None, ALU.mult)
                    if t % 4 == 3:
                        ins.then_inc(s_hn, 1)

            with dve.Fori(0, LAYERS) as layer:
                norm(layer * 2, True)
                with dve.Fori(0, NKV) as g:
                    it = layer * NKV + g
                    for i in range(ROPES + 1):
                        if i < ROPES:
                            cols = slice(i // 3 % 2 * CW, (i // 3 % 2 + 1) * CW)
                            dve.wait_ge(s_qk, it * ROPES + i + 1)
                            if i >= 2:
                                dve.wait_ge(s_lo, it * ROPES + i - 1)
                            dve.tensor_tensor(ra[:, i % 2, :], ps_s[:, i % 2, 0:CW], cos_t[:, cols], ALU.mult)
                            dve.tensor_tensor(rb[:, i % 2, :], ps_s[:, i % 2, CW:2 * CW], sin_t[:, cols], ALU.mult)\
                                .then_inc(s_rm, 1)
                        if i >= 1:
                            j = i - 1
                            c, what = j // 3, j % 3
                            cols = slice(c * CW, (c + 1) * CW)
                            dve.wait_ge(s_hi, it * ROPES + j + 1)
                            if what == 0:
                                dve.tensor_tensor(k_lo[:, cols], ra[:, j % 2, :], k_hi[:, cols].bitcast(F32),
                                                  ALU.subtract).then_inc(s_lo, 1)
                            else:
                                h = 2 * (what - 1)
                                dve.scalar_tensor_tensor(
                                    out=qs[HD:P, h, cols], in0=ra[0:HD, j % 2, :], scalar=HD ** -0.5,
                                    in1=qs[0:HD, h, cols].bitcast(F32), op0=ALU.mult, op1=ALU.subtract)
                                dve.scalar_tensor_tensor(
                                    out=qs[0:HD, h + 1, cols], in0=ra[HD:P, j % 2, :], scalar=HD ** -0.5,
                                    in1=qs[HD:P, h + 1, cols].bitcast(F32), op0=ALU.mult, op1=ALU.subtract)\
                                    .then_inc(s_lo, 1)
                    for s in range(NU + 4):
                        if s < NU:
                            w = (UNITS[s][2] + 1) * P
                            dve.wait_ge(s_s, it * NU + s + 1)
                            dve.tensor_reduce(negmax[:, s:s + 1], ps_s[:, s % 2, 0:w], AX.X, ALU.max,
                                              negate=True).then_inc(s_m, 1)
                        u = s - 1
                        if 0 <= u < NU:
                            w = (UNITS[u][2] + 1) * P
                            dve.wait_ge(s_e, it * NU + u + 1)
                            dve.reciprocal(rrow[:, u:u + 1], rowsum[:, u:u + 1]).then_inc(s_r, 1)
                            dve.wait_ge(s_r, it * NU + u + 1)
                            dve.tensor_scalar(prob[:, u % 3, 0:w], prob[:, u % 3, 0:w], rrow[:, u:u + 1], None,
                                              ALU.mult).then_inc(s_p, 1)
                        u = s - 2
                        if 0 <= u < NU and WIDE[u]:
                            n = CHUNK_OF[(u, 1)]
                            k = UNITS[u][2] + 1 - 4
                            dve.wait_ge(s_tb, it * N_WIDE + wide_upto(u))
                            if u >= 4:
                                dve.wait_ge(s_pv, it * (NU // 2) + (u - 4) // 2 + 1)
                            dve.tensor_copy(prob_t[:, u % 4, 4:4 + k, :],
                                            ps_t[:, n % 2, 0:k * P].rearrange("p (k n) -> p k n", n=P))\
                                .then_inc(s_eb, 1)
                        if s % 4 == 3 and s >= 7:
                            k = (s - 7) // 4
                            b, p, qt, _ = UNITS[4 * k]
                            dve.wait_ge(s_pv, it * (NU // 2) + 2 * k + 2)
                            col = (b * TB + qt) * P
                            dve.tensor_copy(o_t[:, p, col:col + 2 * P], ps_o[:, k % 2, 0:2 * P]).then_inc(s_oe, 1)
                    for c in range(NC4):
                        dve.wait_ge(s_ow, it * NC4 + c + 1)
                        dve.tensor_tensor(x[:, 4 * c:4 * c + 4, :], bank(c).rearrange("p (t d) -> p t d", t=4),
                                          x[:, 4 * c:4 * c + 4, :], ALU.add).then_inc(s_xa, 1)
                    dve.wait_ge(s_xa, it * NC4 + NC4)
                xf = x[:, :, :].rearrange("p t d -> p (t d)")

                rv = [0]

                def rstep(ins, alone=False):
                    rv[0] += 1
                    ins.then_inc(s_rv, 1)
                    dve.wait_ge(s_rv, layer * 14 + rv[0])
                    if alone:
                        dve.sem_inc(s_alone, 1)

                rstep(dve.tensor_scalar(xf, xf, -CLIP, CLIP, ALU.max, ALU.min))
                norm(layer * 2 + 1, False)
                logits = ps_o[:, 0, 0:NT * NE].rearrange("p (t e) -> p t e", e=NE)
                dve.wait_ge(s_rt, layer + 1)
                dve.tensor_reduce(r1[:, :], logits, AX.X, ALU.max).then_inc(s_rmax, 1)
                dve.wait_ge(s_rmax, layer + 1)
                rstep(dve.tensor_tensor(pe_[:, :, :], logits, r1[:, :].unsqueeze(2).to_broadcast([P, NT, NE]),
                                        ALU.subtract))
                dve.wait_ge(s_re, layer + 1)
                rstep(dve.tensor_reduce(r2[:, :], pe_[:, :, :], AX.X, ALU.add))
                rstep(dve.reciprocal(r2[:, :], r2[:, :]))
                rstep(dve.tensor_tensor(pr[:, :, :], pe_[:, :, :], r2[:, :].unsqueeze(2).to_broadcast([P, NT, NE]),
                                        ALU.mult), alone=True)
                for t in range(NT):
                    ins = dve.max(top[:, t, :], pr[:, t, :])
                rstep(ins, alone=True)
                for t in range(NT):
                    ins = dve.max_index(topi[:, t, :], top[:, t, :], pr[:, t, :])
                rstep(ins)
                rstep(dve.tensor_copy(topif[:, :, :], topi[:, :, :]))
                rstep(dve.tensor_tensor(r1[:, :], top[:, :, 0], top[:, :, 1], ALU.add))
                rstep(dve.reciprocal(r1[:, :], r1[:, :]))
                rstep(dve.tensor_tensor(wtop[:, :, :], top[:, :, 0:2], r1[:, :].unsqueeze(2).to_broadcast([P, NT, 2]),
                                        ALU.mult))
                iob = iota8[:, :].unsqueeze(1).to_broadcast([P, NT, NE])
                dve.tensor_tensor(comb[:, :, :], iob, topif[:, :, 0:1].to_broadcast([P, NT, NE]), ALU.is_equal)
                rstep(dve.tensor_tensor(pr[:, :, :], iob, topif[:, :, 1:2].to_broadcast([P, NT, NE]), ALU.is_equal))
                dve.tensor_tensor(comb[:, :, :], comb[:, :, :], wtop[:, :, 0:1].to_broadcast([P, NT, NE]), ALU.mult)
                rstep(dve.tensor_tensor(pr[:, :, :], pr[:, :, :], wtop[:, :, 1:2].to_broadcast([P, NT, NE]), ALU.mult))
                dve.tensor_tensor(comb[:, :, :], comb[:, :, :], pr[:, :, :], ALU.add).then_inc(s_rv, 1)
                assert rv[0] + 1 == 14
                with dve.Fori(0, NE // 2) as e2:
                    it = layer * (NE // 2) + e2
                    dve.wait_ge(s_rv, layer * 14 + 14)
                    for m in range(ITER_GU + 2):
                        if m < ITER_GU:
                            c, fh, r = m // 2, m % 2, m % 3
                            dve.wait_ge(s_sg, it * ITER_GU + m + 1)
                            if c >= 2:
                                dve.wait_ge(s_dn, it * ITER_Y + c - 1)
                            dve.tensor_tensor(a_t[:, c % 2, fh, :], sg[:, m % 2, :], bank(2 * r + 1), ALU.mult)\
                                .then_inc(s_a, 1)
                        if m % 2 == 1 and m >= 3:
                            yi = (m - 3) // 2
                            q = yi // NC4
                            dve.wait_ge(s_dn, it * ITER_Y + yi + 1)
                            if yi >= NC4:
                                dve.wait_ge(s_ya, it * ITER_Y + yi - NC4 + 1)
                            for t4 in range(4):
                                t = yi % NC4 * 4 + t4
                                ins = dve.scalar_tensor_tensor(
                                    out=x[:, t, :], in0=ps_o[:, yi % 2, t4 * P:(t4 + 1) * P],
                                    scalar=comb[:, t, bass.ds(e2 * 2 + q, 1)], in1=x[:, t, :],
                                    op0=ALU.mult, op1=ALU.add)
                            ins.then_inc(s_ya, 1)
                    dve.wait_ge(s_ya, it * ITER_Y + ITER_Y)
                dve.tensor_scalar(xf, xf, -CLIP, CLIP, ALU.max, ALU.min).then_inc(s_clip, 1)
                dve.wait_ge(s_clip, layer + 1)
            dve.wait_ge(s_x1, 1)
            step(dve.tensor_tensor(x[:, :, :], x[:, :, :], x1[:, :, :], ALU.add))
            moments(step)
            dve.wait_ge(s_pow, 2 * LAYERS + 3)
            for t in range(NT):
                ins = dve.tensor_scalar(x[:, t, :], x[:, t, :], mean_var[:, t, 0:1], rstd[:, t:t + 1],
                                        ALU.subtract, ALU.mult)
                if t % 4 == 3:
                    ins.then_inc(s_fin, 1)

        @block.tensor
        def _(pe):
            pe.wait_ge(s_in, 64)
            for b in range(BATCH):
                for j in range(4):
                    for c in range(2):
                        i = (b * 4 + j) * 2 + c
                        if i >= 8:
                            pe.wait_ge(s_pje, i - 7)
                        pe.matmul(bank(i % 8), wsm[:, j * P:(j + 1) * P],
                                  hT[:, b * SEQ + c * CW:b * SEQ + (c + 1) * CW], start=True, stop=True)\
                            .then_inc(s_pj, 1)
            pe.wait_ge(s_const, 10)
            pe.wait_ge(s_pje, 16)
            for t in range(NT):
                pe.wait_ge(s_silu, 4 * (t // TB) + 4)
                tok = slice(t * P, (t + 1) * P)
                if t >= 4:
                    pe.wait_ge(s_tre, t - 3)
                for j in range(3):
                    ins = pe.transpose(bank(t % 4)[:, j * P:(j + 1) * P], xbT[:, j, tok], ident[:, :])
                ins.then_inc(s_tr, 1)
                for j in range(2):
                    pe.matmul(bank(7)[:, t * SH:(t + 1) * SH], xbT[:, j, tok], dw[:, j, :],
                              start=(j == 0), stop=(j == 1))
                ins = pe.matmul(bank(7)[:, P + t * 8:P + (t + 1) * 8], hT[:, tok], wsm[:, 4 * P + DI:4 * P + DI + 8],
                                start=True, stop=True)
            ins.then_inc(s_dd, 1)
            pe.wait_ge(s_vs, 12)
            for d in range(2):
                pe.matmul(bank(4)[:, 0:P].rearrange("p (t h) -> p t h", h=8)[:, :, d * SH:(d + 1) * SH],
                          tri[:, d, :], a_dt[:, :, d * SH:(d + 1) * SH], start=True, stop=True)
            pe.matmul(bank(5)[:, 0:P], ones[:, :], a_dt[:, :, :].rearrange("p t h -> p (t h)"),
                      start=True, stop=True).then_inc(s_cum, 1)
            pe.wait_ge(s_tre, NT)
            pe.wait_ge(s_coef, 2)

            def products(v):
                c, b, d, t = scan_unit(v)
                rows = slice(d * SN, (d + 1) * SN)
                pe.wait_ge(s_mix, v + 1)
                if v >= 2:
                    pe.wait_ge(s_yr, v - 1)
                for h in range(SH):
                    pe.matmul(bank(4 + v % 2)[:, h * SP:(h + 1) * SP], mix[:, v % 2, h, :],
                              xb[:, t, h * SP:(h + 1) * SP], start=True, stop=True)
                if c > 0:
                    pe.wait_ge(s_yr, v - 3)
                    pe.matmul(bank(4 + v % 2)[:, DI:2 * DI], c_cols(t, d), state[rows, b, :], start=True, stop=True)
                pe.wait_ge(s_xw, v + 1)
                pe.matmul(bank(6 + v % 2)[rows, 0:DI], xb[:, t, DI + d * SN:DI + (d + 1) * SN], xw[:, v % 2, :],
                          start=True, stop=True).then_inc(s_y, 1)

            for v in range(NV + 1):
                if v < NV:
                    c, b, d, t = scan_unit(v)
                    rows = slice(d * SN, (d + 1) * SN)
                    pe.wait_ge(s_au, v + 1)
                    if v >= 2:
                        pe.wait_ge(s_mix, v - 1)
                    pe.matmul(bank(v % 2), ones[:, :], a_u[:, v % 2].rearrange("p h t -> p (h t)"),
                              start=True, stop=False)
                    pe.matmul(bank(v % 2), ident_b[:, :], mask4_b[:, d, :], start=False, stop=True)
                    pe.matmul(bank(2 + v % 2)[:, 0:P], xbT[rows, 2, t * P:(t + 1) * P], c_cols(t, d),
                              start=True, stop=True).then_inc(s_eg, 1)
                if v >= 1:
                    products(v - 1)
            pe.wait_ge(s_mix, NV)
            for i in range(NT // 2):
                if i >= 4:
                    pe.wait_ge(s_zs, i - 3)
                for k in range(2):
                    t = 2 * i + k
                    ins = pe.matmul(bank(i % 4)[:, k * DI:(k + 1) * DI], hT[:, t * P:(t + 1) * P],
                                    wsm[:, 4 * P:4 * P + DI], start=True, stop=True)
                ins.then_inc(s_z, 1)
            pe.wait_ge(s_yr, NV)
            for i in range(NT // 2):
                pe.wait_ge(s_un, 2 * i + 2)
                if i >= 2:
                    pe.wait_ge(s_une, i - 1)
                for k in range(2):
                    for j in range(2):
                        ins = pe.transpose(bank(4 + i % 2)[:, (k * 2 + j) * P:(k * 2 + j + 1) * P],
                                           y[:, 2 * i + k, j * P:(j + 1) * P], ident[:, :])
                ins.then_inc(s_unt, 1)
            pe.wait_ge(s_zs, NT // 2)
            for c in range(NC4):
                pe.wait_ge(s_une, 2 * c + 2)
                for t4 in range(4):
                    t = 4 * c + t4
                    for j in range(2):
                        ins = pe.matmul(bank(c)[:, t4 * P:(t4 + 1) * P], unT[:, j, t * P:(t + 1) * P], wout[:, j, :],
                                        start=(j == 0), stop=(j == 1))
                ins.then_inc(s_so, 1)
            pe.wait_ge(s_x, 1)

            def norm_t(n):
                for c in range(NC4):
                    pe.wait_ge(s_hn, n * NC4 + c + 1)
                    for t4 in range(4):
                        ins = pe.transpose(bank(c)[:, t4 * P:(t4 + 1) * P], hn[:, 4 * c + t4, :], ident[:, :])
                    ins.then_inc(s_nt, 1)

            with pe.Fori(0, LAYERS) as layer:
                norm_t(layer * 2)
                pe.wait_ge(s_wl, layer * 16 + 16)
                for i in range(NT // 2):
                    pe.wait_ge(s_ht, layer * 2 * NC4 + i // 2 + 1)
                    if i >= 4:
                        pe.wait_ge(s_ve, layer * (NT // 2) + i - 3)
                    for k in range(2):
                        t = 2 * i + k
                        ins = pe.matmul(bank(4 + i % 4)[:, k * 256:(k + 1) * 256], hT[:, t * P:(t + 1) * P],
                                        wlay[:, 2 + NE:WLAY], start=True, stop=True)
                    ins.then_inc(s_v, 1)
                with pe.Fori(0, NKV) as g:
                    it = layer * NKV + g
                    pe.wait_ge(s_ve, layer * (NT // 2) + NT // 2)
                    pe.wait_ge(s_wa, it * 16 + 16)
                    for i in range(ROPES):
                        c, what = i // 3, i % 3
                        col = 2 * QW if what == 0 else (what - 1) * P
                        rot = P if what == 0 else QW
                        if i >= 2:
                            pe.wait_ge(s_rm, it * ROPES + i - 1)
                        for k in range(2):
                            ins = pe.matmul(ps_s[:, i % 2, k * CW:(k + 1) * CW],
                                            wqkv[:, col + k * rot:col + k * rot + P],
                                            hT[:, c * CW:(c + 1) * CW], start=True, stop=True)
                        ins.then_inc(s_qk, 1)
                    pe.wait_ge(s_rm, it * ROPES + ROPES)
                    for s in range(NU + 3):
                        if s < NU:
                            b, p, qt, hh = UNITS[s]
                            if s == 0 or s == NU // 2:
                                pe.wait_ge(s_lo, it * ROPES + ROPES // 2 * (b + 1))
                            if s >= 2:
                                pe.wait_ge(s_e, it * NU + s - 1)
                            nk = qt + 1
                            q_cols = slice(b * SEQ + qt * P, b * SEQ + (qt + 1) * P)
                            for k0 in range(0, nk, 4):
                                n = max(min(nk - k0, 4), 2) * P
                                dst = ps_s[:, s % 2, k0 * P:k0 * P + n]
                                k_cols = slice(b * SEQ + k0 * P, b * SEQ + k0 * P + n)
                                pe.matmul(dst, qs[:, 2 * p + hh, q_cols], k_hi[:, k_cols], start=True, stop=False)
                                if k0 + 4 >= nk:
                                    pe.matmul(ps_s[:, s % 2, qt * P:(qt + 1) * P], ident_b[:, :], causal_b[:, :],
                                              start=False, stop=False)
                                ins = pe.matmul(dst, qs[:, 2 * p + hh, q_cols], k_lo[:, k_cols], start=False,
                                                stop=True)
                            ins.then_inc(s_s, 1)
                        u = s - 2
                        if 0 <= u < NU:
                            nk = UNITS[u][2] + 1
                            pe.wait_ge(s_p, it * NU + u + 1)
                            for part in range(2 if WIDE[u] else 1):
                                n = CHUNK_OF[(u, part)]
                                if n >= 2:
                                    pu, pp = CHUNKS[n - 2]
                                    if pp == 0:
                                        pe.wait_ge(s_ea, it * NU + pu + 1)
                                    else:
                                        pe.wait_ge(s_eb, it * N_WIDE + wide_upto(pu))
                                for k in range(part * 4, min(nk, part * 4 + 4)):
                                    ins = pe.transpose(ps_t[:, n % 2, k % 4 * P:(k % 4 + 1) * P],
                                                       prob[:, u % 3, k * P:(k + 1) * P], ident[:, :])
                                ins.then_inc(s_ta if part == 0 else s_tb, 1)
                        if s % 2 == 0 and s >= 4:
                            j = (s - 4) // 2
                            b, p, qt, _ = UNITS[2 * j]
                            if j == 0:
                                pe.wait_ge(s_vg, it + 1)
                            pe.wait_ge(s_ea, it * NU + 2 * j + 2)
                            if WIDE[2 * j]:
                                pe.wait_ge(s_eb, it * N_WIDE + wide_upto(2 * j + 1))
                            k2 = j // 2
                            if k2 >= 2 and j % 2 == 0:
                                pe.wait_ge(s_oe, it * (NU // 4) + k2 - 1)
                            for kt in range(qt + 1):
                                for hh in range(2):
                                    ins = pe.matmul(
                                        ps_o[hh * HD:(hh + 1) * HD, k2 % 2, (j % 2) * P:(j % 2 + 1) * P],
                                        v_g[:, b * TB + kt, :], prob_t[:, (2 * j + hh) % 4, kt, :],
                                        start=(kt == 0), stop=(kt == qt))
                            ins.then_inc(s_pv, 1)
                    pe.wait_ge(s_oe, it * (NU // 4) + NU // 4)
                    pe.wait_ge(s_wo, it * 16 + 16)
                    for c in range(NC4):
                        for t4 in range(4):
                            t = 4 * c + t4
                            for p in range(2):
                                ins = pe.matmul(bank(c)[:, t4 * P:(t4 + 1) * P], o_t[:, p, t * P:(t + 1) * P],
                                                wo[:, p, :], start=(p == 0), stop=(p == 1))
                        ins.then_inc(s_ow, 1)
                    pe.wait_ge(s_xa, it * NC4 + NC4)
                norm_t(layer * 2 + 1)
                for t in range(NT):
                    pe.wait_ge(s_ht, layer * 2 * NC4 + NC4 + t // 4 + 1)
                    ins = pe.matmul(ps_o[:, 0, t * NE:(t + 1) * NE], hT[:, t * P:(t + 1) * P], wlay[:, 2:2 + NE],
                                    start=True, stop=True)
                ins.then_inc(s_rt, 1)
                with pe.Fori(0, NE // 2) as e2:
                    it = layer * (NE // 2) + e2
                    pe.wait_ge(s_rv, layer * 14 + 2)
                    for m in range(ITER_GU + 2):
                        if m < ITER_GU:
                            q, c, fh, r = m // GU, m // 2 % NC4, m % 2, m % 3
                            if m % GU == 0:
                                pe.wait_ge(s_we[q], it * 16 + 16)
                            if m >= 3:
                                pe.wait_ge(s_a, it * ITER_GU + m - 2)
                            for k in range(2):
                                ins = pe.matmul(bank(2 * r + k), wexp[:, q, k * FF + fh * P:k * FF + (fh + 1) * P],
                                                hT[:, c * CW:(c + 1) * CW], start=True, stop=True)
                            ins.then_inc(s_gu, 1)
                        if m % 2 == 1 and m >= 3:
                            yi = (m - 3) // 2
                            q = yi // NC4
                            pe.wait_ge(s_a, it * ITER_GU + 2 * yi + 2)
                            if yi >= 2:
                                pe.wait_ge(s_ya, it * ITER_Y + yi - 1)
                            for t4 in range(4):
                                for fh in range(2):
                                    ins = pe.matmul(ps_o[:, yi % 2, t4 * P:(t4 + 1) * P],
                                                    a_t[:, yi % 2, fh, t4 * P:(t4 + 1) * P],
                                                    wexp[:, q, 2 * FF + fh * P:2 * FF + (fh + 1) * P],
                                                    start=(fh == 0), stop=(fh == 1))
                            ins.then_inc(s_dn, 1)
                    pe.wait_ge(s_ya, it * ITER_Y + ITER_Y)


def layouts(a):
    def tokens(v):
        return np.ascontiguousarray(v.reshape(NT, P, DM).transpose(1, 0, 2))

    u = a["L0_attn_u"].reshape(TOK, DM)
    w = a["L0_attn_in_proj_w"]
    z, xs = w[:DI], w[DI:2 * DI]
    bc = w[2 * DI:2 * DI + 4 * SN]
    dt = w[2 * DI + 4 * SN:]
    perm = np.concatenate([np.arange(DI), DI + np.concatenate(
        [np.arange(0, SN), np.arange(2 * SN, 3 * SN), np.arange(SN, 2 * SN), np.arange(3 * SN, 4 * SN)])])
    w_in = np.concatenate([np.concatenate([xs, bc])[perm], z, dt]).T
    cw = a["L0_attn_conv1d_w"][:, 0, :][perm].reshape(4, P, TAPS).transpose(1, 0, 2).reshape(P, -1)
    cb = a["L0_attn_conv1d_b"][perm].reshape(4, P).T
    rms = a["L0_attn_rms_w"].reshape(2, P).T

    def rows(v):
        return np.broadcast_to(v[None], (P, v.size))

    small = np.concatenate([cw, cb, rms, rows(a["L0_attn_dt_bias"]), rows(a["L0_attn_dt_bias"]),
                            rows(a["L0_attn_A_log"]), rows(a["L0_attn_A_log"]), rows(a["L0_attn_D_b"])], axis=1)
    wout = a["L0_attn_outproj_w"].T.reshape(2, P, DM).transpose(1, 0, 2).reshape(P, -1)
    dw = a["L0_attn_D_w"].T.reshape(2, P, SH).transpose(1, 0, 2).reshape(P, -1)
    scan_out = np.concatenate([wout, dw], axis=1)

    inv = (np.float32(1.0) / np.float32(THETA) ** (np.arange(0, HD, 2, dtype=np.float32) / np.float32(HD)))
    f = np.arange(SEQ, dtype=np.float32)[:, None] * inv.astype(np.float32)
    c, s = np.cos(f).T, np.sin(f).T
    rope = np.stack([np.concatenate([c, c, c, c]), np.concatenate([-s, s, -s, s])]).astype(np.float32)

    half = np.concatenate([np.arange(HD // 2, HD), np.arange(HD // 2)])
    wq = a["L0_ffn_wq"].reshape(LAYERS, DM, NKV, REP, HD)
    wk = a["L0_ffn_wk"].reshape(LAYERS, DM, NKV, 1, HD)
    attn = np.concatenate([wq, wq[..., half], wk, wk, wk[..., half], wk[..., half]], axis=3)
    attn = attn.transpose(0, 2, 1, 3, 4).reshape(LAYERS * NKV, DM, WQKV)
    w_o = a["L0_ffn_wo"].reshape(LAYERS, NKV, 2, P, DM).transpose(0, 1, 3, 2, 4).reshape(LAYERS * NKV, P, 2, DM)
    lay = np.concatenate([a["L0_ffn_ln1_w"][:, :, None], a["L0_ffn_ln2_w"][:, :, None], a["L0_ffn_wr"],
                          a["L0_ffn_wv"]], axis=2)
    wd = a["L0_ffn_wd"].reshape(LAYERS, NE, 2, P, DM).transpose(0, 1, 3, 2, 4).reshape(LAYERS, NE, P, 2 * DM)
    exp = np.concatenate([a["L0_ffn_wg"], a["L0_ffn_wu"], wd], axis=3).reshape(LAYERS * NE, P, -1)

    def ahead(v, n):
        return np.concatenate([v, v[:n]])

    return {
        "u_tok": tokens(u), "u_feat": u.T, "w_in": w_in, "conv_w": small, "w_scan_out": scan_out, "rope": rope,
        "w_attn": ahead(attn, 1), "w_o": ahead(w_o, 1), "w_layer": ahead(lay, 1), "w_expert": ahead(exp, 2),
    }


def kernel(**inputs):
    import concourse.bacc as bacc
    from concourse.bass_utils import run_bass_kernel_spmd

    arrays = {n: np.ascontiguousarray(v) for n, v in layouts({k: np.asarray(v) for k, v in inputs.items()}).items()}
    nc = bacc.Bacc("TRN2", target_bir_lowering=False, num_devices=1)
    aps = {n: nc.dram_tensor(n, v.shape, F32, kind="ExternalInput").ap() for n, v in arrays.items()}
    out = nc.dram_tensor("out", (P, NT, DM), F32, kind="ExternalOutput").ap()
    build(nc, out=out, **aps)
    r = run_bass_kernel_spmd(nc, [arrays], core_ids=[0])
    return r.results[0]["out"].transpose(1, 0, 2).reshape(BATCH, SEQ, DM)
```

```python
from contextlib import ExitStack

import numpy as np
import concourse.bass as bass
from concourse import mybir

F32 = mybir.dt.float32
F32R = mybir.dt.float32r
BF16 = mybir.dt.bfloat16
U32 = mybir.dt.uint32
ALU = mybir.AluOpType
ACT = mybir.ActivationFunctionType
AX = mybir.AxisListType

P = 128
BATCH, SEQ, DM = 2, 1024, 128
TOK = BATCH * SEQ
NT = TOK // P
TB = SEQ // P
CW = 512
NC4 = TOK // CW

SH, SP, SN = 4, 64, 64
DI = SH * SP
TAPS = 7
PAD = TAPS // 2
RMS_EPS = 1e-5

LAYERS, NH, NKV, HD, FF, NE = 4, 16, 4, 64, 256, 8
REP = NH // NKV
QW = REP * HD
WQKV = 2 * QW + 2 * P
WLAY = 2 + NE + NKV * HD
WEXP = 3 * FF
THETA, EPS = 10000.0, 1e-5
CLIP = 100.0

QT_ORDER = [3, 4, 2, 5, 1, 6, 0, 7]
UNITS = [(b, p, qt, hh) for b in range(BATCH) for p in range(REP // 2) for qt in QT_ORDER for hh in range(2)]
NU = len(UNITS)
NPAIR = NU // 2
CHUNKS = [(u, part) for u in range(NU) for part in range(2 if UNITS[u][2] >= 4 else 1)]
CHUNK_OF = {c: n for n, c in enumerate(CHUNKS)}
NCH = len(CHUNKS)
LAG_N, LAG_T, LAG_PV = 1, 3, 3
R_PROB, R_PT = 5, 4
STEPS = NU - 2 + LAG_T + LAG_PV + 2
ROPES = SEQ // CW * 3
PARTS = 2 * ROPES
SIDE = {1 + 2 * k: ("b1", k) for k in range(PARTS)}
SIDE |= {36 + LAG_T + 2 * c: ("wo", c) for c in range(2)}
SIDE |= {40 + LAG_T + 2 * k: ("b0", k) for k in range(PARTS)}
assert max(SIDE) < STEPS


def at_step(s, lag, kind):
    got = SIDE.get(s - lag)
    return got[1] if got and got[0] == kind else None


LAG_HI, LAG_LO = 2, 3
ARENA = 22528
GU = NC4 * 2
ITER_GU, ITER_Y = 2 * GU, 2 * NC4


def build(nc, u_tok, u_feat, w_in, conv_w, w_scan_out, rope, w_attn, w_o, w_layer, w_expert, out):
    with ExitStack() as ctx:
        def sb(name, shape, dt=F32):
            return ctx.enter_context(nc.sbuf_tensor(name, shape, dt))

        def sem(name):
            return ctx.enter_context(nc.semaphore(name))

        x = sb("x", [P, NT, DM])
        x1 = sb("x1", [P, NT, DM])
        hT = sb("hT", [P, TOK])
        cos_t = sb("cos_t", [P, SEQ])
        sin_t = sb("sin_t", [P, SEQ])
        wqkv = sb("wqkv", [P, WQKV])
        wo = sb("wo", [P, 2, DM])
        wlay = sb("wlay", [P, WLAY])
        wexp = sb("wexp", [P, 2, WEXP])
        ident = sb("ident", [P, P])
        ident_b = sb("ident_b", [P, P], BF16)
        causal_b = sb("causal_b", [P, P], BF16)
        iota8 = sb("iota8", [P, NE])
        sq = sb("sq", [P, DM])
        ssq = sb("ssq", [P, NT])
        var = sb("var", [P, NT])
        rstd = sb("rstd", [P, NT])
        mean_var = sb("mean_var", [P, NT, 2])
        bn = sb("bn", [P, 2, 6])
        neg_half = sb("neg_half", [P, NT])
        negmax = sb("negmax", [P, NU])
        rowsum = sb("rowsum", [P, NU])
        rrow = sb("rrow", [P, NU])
        pr = sb("pr", [P, NT, NE])
        pe_ = sb("pe_", [P, NT, NE])
        top = sb("top", [P, NT, 8])
        topi = sb("topi", [P, NT, 8], U32)
        topif = sb("topif", [P, NT, 8])
        r1 = sb("r1", [P, NT])
        r2 = sb("r2", [P, NT])
        wtop = sb("wtop", [P, NT, 2])
        comb = sb("comb", [P, NT, NE])
        qs = sb("qs", [P, REP, TOK], F32R)
        k_hi = sb("k_hi", [P, TOK], F32R)
        k_lo = sb("k_lo", [P, TOK], F32R)

        arena = sb("arena", [P, ARENA])
        at = [0]

        def cut(*dims, new=False):
            if new:
                at[0] = 0
            n = int(np.prod(dims))
            v = arena[:, at[0]:at[0] + n]
            at[0] += n
            assert at[0] <= ARENA
            if len(dims) == 2:
                v = v.rearrange("p (a b) -> p a b", b=dims[1])
            if len(dims) == 3:
                v = v.rearrange("p (a b c) -> p a b c", b=dims[1], c=dims[2])
            return v

        ra = cut(2, CW, new=True)
        rb = cut(2, CW)
        v_all = cut(NT, NKV * HD)
        v_g = cut(NT, HD)
        prob = cut(R_PROB, SEQ)
        prob_t = cut(R_PT, TB, P)
        o_t = cut(2, TOK)
        hn = o_t.rearrange("p a b -> p (a b)")[:, 0:TOK].rearrange("p (t d) -> p t d", d=DM)
        sg = prob_t[:, 0]
        sg = sg.rearrange("p a b -> p (a b)").rearrange("p (a b) -> p a b", b=CW)
        a_t = prob_t[:, 1:3].rearrange("p a b c -> p (a b c)").rearrange("p (s f n) -> p s f n", s=2, f=2)

        SEQP = SEQ + 2 * PAD
        proj = cut(4, SEQP, new=True)
        xbT = cut(3, TOK)
        c_pad = cut(BATCH, SEQ + 2)
        xb = cut(NT, DI + P)
        state = cut(BATCH, DI)
        mask4 = cut(2, SH * P // 2)
        y = xbT.rearrange("p a b -> p (a b)")[:, 0:NT * DI].rearrange("p (t d) -> p t d", d=DI)
        flat = proj.rearrange("p a b -> p (a b)")
        a_u = flat[:, 0:1024].rearrange("p (r h t) -> p r h t", r=2, h=SH)
        dec = flat[:, 1024:2048].rearrange("p (r h t) -> p r h t", r=2, h=SH)
        mix = flat[:, 2048:3072].rearrange("p (r h t) -> p r h t", r=2, h=SH)
        xw = flat[:, 3072:3584].rearrange("p (r d) -> p r d", r=2)
        tmp = flat[:, 3584:3840]
        tmp_h = flat[:, 3840:4096]
        unT = flat[:, 0:2 * TOK].rearrange("p (j t) -> p j t", j=2)
        mask4_b = mask4.bitcast(BF16)
        wsm = sb("wsm", [P, 4 * P + DI + 8])
        wout = wqkv[:, 0:2 * DM].rearrange("p (j d) -> p j d", j=2)
        dw = wqkv[:, 256:264].rearrange("p (j h) -> p j h", j=2)
        cw = wqkv[:, 264:264 + 4 * TAPS].rearrange("p (j k) -> p j k", j=4)
        cb = wqkv[:, 292:296]
        rmsw = wqkv[:, 296:298]
        hc = wqkv[:, 298:298 + 20]
        tri = prob_tri = sb("tri", [P, 4, P])
        ones = sb("ones", [P, P])
        dtr = sb("dtr", [P, NT, 8])
        dt_e = sb("dt_e", [P, NT, 8])
        dt_u = sb("dt_u", [P, NT, 8])
        dt_l = sb("dt_l", [P, NT, 8])
        dt_z = sb("dt_z", [P, NT, 8])
        dt_s = sb("dt_s", [P, NT, 8])
        a_dt = sb("a_dt", [P, NT, 8])
        ncum = sb("ncum", [P, NT, 8])
        exp_e = sb("exp_e", [P, NT, 8])
        exp_w = sb("exp_w", [P, NT, 8])
        exp_t = sb("exp_t", [P, NT, 8])
        d_t = sb("d_t", [P, NT, SH])
        exp_a = sb("exp_a", [P, 8])

        ps_s = ctx.enter_context(nc.psum_tensor("ps_s", [P, 2, 2 * CW], F32))
        ps_t = ctx.enter_context(nc.psum_tensor("ps_t", [P, 2, CW], F32))
        ps_o = ctx.enter_context(nc.psum_tensor("ps_o", [P, 2, CW], F32))

        def bank(i):
            if i < 4:
                return ps_s[:, i // 2, (i % 2) * CW:(i % 2 + 1) * CW]
            return (ps_t if i < 6 else ps_o)[:, i % 2, :]

        s_const = sem("s_const")
        s_cstep = sem("s_cstep")
        s_in = sem("s_in")
        s_u = sem("s_u")
        s_wa = sem("s_wa")
        s_wo = sem("s_wo")
        s_wl = sem("s_wl")
        s_we = [sem("s_we0"), sem("s_we1")]
        s_out = sem("s_out")
        s_pj = sem("s_pj")
        s_pje = sem("s_pje")
        s_conv = sem("s_conv")
        s_silu = sem("s_silu")
        s_vs = sem("s_vs")
        s_as = sem("s_as")
        s_tr = sem("s_tr")
        s_tre = sem("s_tre")
        s_dd = sem("s_dd")
        s_cum = sem("s_cum")
        s_coef = sem("s_coef")
        s_yi = sem("s_yi")
        s_au = sem("s_au")
        s_xw = sem("s_xw")
        s_eg = sem("s_eg")
        s_dec = sem("s_dec")
        s_mix = sem("s_mix")
        s_y = sem("s_y")
        s_yr = sem("s_yr")
        s_z = sem("s_z")
        s_zs = sem("s_zs")
        s_pow = sem("s_pow")
        s_var = sem("s_var")
        s_un = sem("s_un")
        s_unt = sem("s_unt")
        s_une = sem("s_une")
        s_so = sem("s_so")
        s_x = sem("s_x")
        s_x1 = sem("s_x1")
        s_hn = sem("s_hn")
        s_nt = sem("s_nt")
        s_ht = sem("s_ht")
        s_vn = sem("s_vn")
        s_v = sem("s_v")
        s_ve = sem("s_ve")
        s_vg = sem("s_vg")
        s_qk = sem("s_qk")
        s_rc = sem("s_rc")
        s_rs = sem("s_rs")
        s_hi = sem("s_hi")
        s_lo = sem("s_lo")
        s_s = sem("s_s")
        s_m = sem("s_m")
        s_e = sem("s_e")
        s_r = sem("s_r")
        s_p = sem("s_p")
        s_t = sem("s_t")
        s_ev = sem("s_ev")
        s_pv = sem("s_pv")
        s_oe = sem("s_oe")
        s_ow = sem("s_ow")
        s_xa = sem("s_xa")
        s_rt = sem("s_rt")
        s_rmax = sem("s_rmax")
        s_alone = sem("s_alone")
        s_clip = sem("s_clip")
        s_rv = sem("s_rv")
        s_re = sem("s_re")
        s_gu = sem("s_gu")
        s_sg = sem("s_sg")
        s_a = sem("s_a")
        s_dn = sem("s_dn")
        s_ya = sem("s_ya")
        s_fin = sem("s_fin")

        block = ctx.enter_context(nc.Block())

        def scan_unit(v):
            c, b, d = v // 4, v // 2 % 2, v % 2
            return c, b, d, b * TB + (c if d == 0 else TB - 1 - c)

        NV = 4 * TB

        def c_cols(t, d):
            b, lo = t // TB, t % TB * P
            return c_pad[d * SN:(d + 1) * SN, b, lo + 2 * d:lo + 2 * d + P]

        @block.sync
        def _(sp):
            sp.dma_start(wsm[:, :], w_in).then_inc(s_in, 16)
            sp.dma_start(hT[:, :], u_feat).then_inc(s_in, 16)
            sp.dma_start(wqkv[:, 264:318], conv_w).then_inc(s_in, 16)
            sp.dma_start(wqkv[:, 0:264], w_scan_out).then_inc(s_in, 16)
            sp.dma_start(x[:, :, :], u_tok).then_inc(s_u, 16)
            sp.dma_start(cos_t[:, :], rope[0]).then_inc(s_u, 16)
            sp.dma_start(sin_t[:, :], rope[1]).then_inc(s_u, 16)
            sp.dma_start(wlay[:, :], w_layer[0]).then_inc(s_wl, 16)
            sp.dma_start(wo[:, :, :], w_o[0]).then_inc(s_wo, 16)
            for q in range(2):
                sp.dma_start(wexp[:, q, :], w_expert[q]).then_inc(s_we[q], 16)
            sp.wait_ge(s_x, 1)
            sp.dma_start(wqkv[:, :], w_attn[0]).then_inc(s_wa, 16)
            with sp.Fori(0, LAYERS) as layer:
                with sp.Fori(0, NKV) as g:
                    it = layer * NKV + g
                    sp.wait_ge(s_qk, it * 2 * PARTS + 2 * PARTS)
                    sp.dma_start(wqkv[:, :], w_attn[it + 1]).then_inc(s_wa, 16)
                    sp.wait_ge(s_ow, it * NC4 + NC4)
                    sp.dma_start(wo[:, :, :], w_o[it + 1]).then_inc(s_wo, 16)
                sp.wait_ge(s_rt, layer + 1)
                sp.dma_start(wlay[:, :], w_layer[layer + 1]).then_inc(s_wl, 16)
                with sp.Fori(0, NE // 2) as e2:
                    it = layer * (NE // 2) + e2
                    for q in range(2):
                        sp.wait_ge(s_dn, it * ITER_Y + (q + 1) * NC4)
                        sp.dma_start(wexp[:, q, :], w_expert[it * 2 + 2 + q]).then_inc(s_we[q], 16)
            for c in range(NC4):
                sp.wait_ge(s_fin, c + 1)
                sp.dma_start(out[:, 4 * c:4 * c + 4, :], x[:, 4 * c:4 * c + 4, :]).then_inc(s_out, 16)
            sp.wait_ge(s_out, 16 * NC4)
            sp.wait_ge(s_wa, 16 * (LAYERS * NKV + 1))
            sp.wait_ge(s_wo, 16 * (LAYERS * NKV + 1))
            sp.wait_ge(s_wl, 16 * (LAYERS + 1))
            for q in range(2):
                sp.wait_ge(s_we[q], 16 * (LAYERS * NE // 2 + 1))

        @block.gpsimd
        def _(pool):
            steps = [0]

            def fill(ap, value):
                steps[0] += 1
                pool.memset(ap, value).then_inc(s_cstep, 1)
                return steps[0]

            def keep(ap, pattern, base, ch, fill_value):
                pool.affine_select(out=ap, in_=ap, compare_op=ALU.is_ge, fill=fill_value, base=base,
                                   pattern=pattern, channel_multiplier=ch).then_inc(s_const, 1)

            fill(ident[:, :], 0.0)
            fill(ident_b[:, :], 0.0)
            fill(causal_b[:, :], 0.0)
            fill(mask4_b[:, :, :], 0.0)
            fill(tri[:, :, :], 1.0)
            fill(ones[:, :], 1.0)
            fill(neg_half[:, :], -0.5)
            fill(proj[:, :, 0:PAD], 0.0)
            fill(proj[:, :, PAD + SEQ:SEQP], 0.0)
            fill(c_pad[:, :, 0:1], 0.0)
            fill(c_pad[:, :, SEQ + 1:SEQ + 2], 0.0)
            pool.wait_ge(s_cstep, steps[0])
            for m in (ident, ident_b):
                pool.affine_select(out=m[:, :], in_=m[:, :], compare_op=ALU.not_equal, fill=1.0, base=0,
                                   pattern=[[-1, P]], channel_multiplier=1).then_inc(s_const, 1)
            keep(causal_b[:, :], [[-1, P]], 0, 1, -1e9)
            keep(mask4_b[:, 0, :].rearrange("p (h t) -> p h t", h=SH), [[0, SH], [1, P]], -1, -1, -1e30)
            keep(mask4_b[:, 1, :].rearrange("p (h t) -> p h t", h=SH), [[0, SH], [-1, P]], -1, 1, -1e30)
            keep(tri[:, 0, :], [[1, P]], 0, -1, 0.0)
            keep(tri[:, 1, :], [[-1, P]], 0, 1, 0.0)
            keep(tri[:, 2, :], [[1, P]], -1, -1, 0.0)
            keep(tri[:, 3, :], [[-1, P]], -1, 1, 0.0)
            pool.iota(iota8[:, :], pattern=[[1, NE]], base=0, channel_multiplier=0,
                      allow_small_or_imprecise_dtypes=True).then_inc(s_const, 1)

            pool.wait_ge(s_coef, 1)
            pool.wait_ge(s_tre, NT)
            for t in range(NT):
                ins = pool.tensor_tensor(
                    y[:, t, :].rearrange("p (h e) -> p h e", h=SH),
                    xb[:, t, 0:DI].rearrange("p (h e) -> p h e", h=SH),
                    d_t[:, t, :].unsqueeze(2).to_broadcast([P, SH, SP]), ALU.mult)
            ins.then_inc(s_yi, 1)
            pool.wait_ge(s_coef, 2)
            for v in range(NV):
                c, b, d, t = scan_unit(v)
                if v >= 2:
                    pool.wait_ge(s_eg, v - 1)
                pool.tensor_tensor(
                    a_u[:, v % 2], tri[:, 2 + d, :].unsqueeze(1).to_broadcast([P, SH, P]),
                    a_dt[:, t, d * SH:(d + 1) * SH].unsqueeze(2).to_broadcast([P, SH, P]), ALU.mult)\
                    .then_inc(s_au, 1)
                if v >= 2:
                    pool.wait_ge(s_y, v - 1)
                pool.tensor_tensor(
                    xw[:, v % 2, :].rearrange("p (h e) -> p h e", h=SH),
                    xb[:, t, 0:DI].rearrange("p (h e) -> p h e", h=SH),
                    exp_w[:, t, d * SH:(d + 1) * SH].unsqueeze(2).to_broadcast([P, SH, SP]), ALU.mult)\
                    .then_inc(s_xw, 1)

            def root(n):
                pool.wait_ge(s_var, n)
                pool.tensor_tensor(rstd[:, :], var[:, :], neg_half[:, :], ALU.pow).then_inc(s_pow, 1)

            root(1)
            root(2)
            pool.wait_ge(s_x, 2)
            pool.tensor_copy(x1[:, :, :], x[:, :, :]).then_inc(s_x1, 1)
            with pool.Fori(0, LAYERS) as layer:
                root(layer * 2 + 3)

                def sums(half):
                    for i in range(ROPES):
                        pool.wait_ge(s_rc, half * PARTS + 2 * i + 2)
                        pool.tensor_tensor(ra[:, i % 2, :], ra[:, i % 2, :], rb[:, i % 2, :], ALU.add)\
                            .then_inc(s_rs, 1)

                def group(it, g, last):
                    pool.wait_ge(s_ve, layer * (NT // 2) + NT // 2)
                    pool.wait_ge(s_s, it * NU + 1)
                    pool.sem_inc(s_alone, 1)
                    pool.tensor_copy(v_g[:, :, :], v_all[:, :, bass.ts(g, HD)]).then_inc(s_vg, 1)
                    sums(it * 2 + 1)
                    if not last:
                        sums(it * 2 + 2)

                sums(layer * NKV * 2)
                with pool.Fori(0, NKV - 1) as g:
                    group(layer * NKV + g, g, False)
                group(layer * NKV + NKV - 1, NKV - 1, True)
                root(layer * 2 + 4)
            root(2 * LAYERS + 3)

        @block.scalar
        def _(act):
            for b in range(BATCH):
                for j in range(4):
                    for c in range(2):
                        i = (b * 4 + j) * 2 + c
                        act.wait_ge(s_pj, i + 1)
                        if b == 1 and c == 0:
                            act.wait_ge(s_conv, j + 1)
                        act.activation(proj[:, j, PAD + c * CW:PAD + (c + 1) * CW], bank(i % 8), ACT.Copy)\
                            .then_inc(s_pje, 1)
                if b == 0:
                    pass
                for j in range(4):
                    act.wait_ge(s_conv, b * 4 + j + 1)
                    dst = xbT[:, j, b * SEQ:(b + 1) * SEQ] if j < 3 else c_pad[:, b, 1:SEQ + 1]
                    act.activation(dst, dst, ACT.Silu).then_inc(s_silu, 1)
            for t in range(NT):
                act.wait_ge(s_tr, t + 1)
                act.activation(xb[:, t, :], bank(t % 4)[:, 0:DI + P], ACT.Copy).then_inc(s_tre, 1)
            act.activation(exp_a[:, :], hc[:, 8:16], ACT.Exp).then_inc(s_as, 1)
            act.wait_ge(s_vs, 3)
            act.activation(dt_e[:, :, :], dt_u[:, :, :], ACT.Exp, scale=-1.0).then_inc(s_as, 1)
            act.wait_ge(s_vs, 4)
            act.activation(dt_l[:, :, :], dt_u[:, :, :], ACT.Ln).then_inc(s_as, 1)
            act.wait_ge(s_cum, 1)
            act.activation(exp_t[:, :, :], bank(5)[:, 0:P].rearrange("p (t h) -> p t h", h=8), ACT.Exp)\
                .then_inc(s_as, 1)
            act.wait_ge(s_vs, 14)
            act.activation(exp_e[:, :, :], exp_e[:, :, :], ACT.Exp).then_inc(s_as, 1)
            act.wait_ge(s_vs, 15)
            act.activation(exp_w[:, :, :], exp_w[:, :, :], ACT.Exp).then_inc(s_as, 1)
            act.wait_ge(s_vs, 13)
            for v in range(NV):
                c, b, d, t = scan_unit(v)
                act.wait_ge(s_eg, v + 1)
                if v >= 2:
                    act.wait_ge(s_mix, v - 1)
                for h in range(SH):
                    ins = act.activation(dec[:, v % 2, h, :], bank(v % 2)[:, h * P:(h + 1) * P], ACT.Exp,
                                         bias=ncum[:, t, d * SH + h:d * SH + h + 1])
                ins.then_inc(s_dec, 1)
            for i in range(NT // 2):
                act.wait_ge(s_z, i + 1)
                act.activation(xb[:, 2 * i:2 * i + 2, 0:DI],
                               bank(i % 4).rearrange("p (t d) -> p t d", t=2), ACT.Silu).then_inc(s_zs, 1)
            for i in range(NT // 2):
                act.wait_ge(s_unt, i + 1)
                src = bank(4 + i % 2).rearrange("p (t j n) -> p j t n", t=2, j=2)
                for j in range(2):
                    ins = act.activation(
                        unT[:, j, i * 2 * P:(i + 1) * 2 * P].rearrange("p (t n) -> p t n", t=2),
                        src[:, j], ACT.Copy, scale=rmsw[:, j:j + 1])
                ins.then_inc(s_une, 1)

            def norm_out(n, w):
                for c in range(NC4):
                    act.wait_ge(s_nt, n * NC4 + c + 1)
                    act.activation(hT[:, c * CW:(c + 1) * CW], bank(c), ACT.Copy, scale=wlay[:, w:w + 1])\
                        .then_inc(s_ht, 1)

            with act.Fori(0, LAYERS) as layer:
                act.wait_ge(s_wl, layer * 16 + 16)
                norm_out(layer * 2, 0)
                for i in range(NT // 2):
                    act.wait_ge(s_v, layer * (NT // 2) + i + 1)
                    act.activation(v_all[:, 2 * i:2 * i + 2, :],
                                   bank(4 + i % 4).rearrange("p (t n) -> p t n", t=2), ACT.Copy)\
                        .then_inc(s_ve, 1)

                def high(b, half, i):
                    c, what = i // 3, i % 3
                    cols = slice(b * SEQ + c * CW, b * SEQ + (c + 1) * CW)
                    act.wait_ge(s_rs, half * ROPES + i + 1)
                    if what == 0:
                        act.activation(k_hi[:, cols], ra[:, i % 2, :], ACT.Copy).then_inc(s_hi, 1)
                    else:
                        h = 2 * (what - 1)
                        act.activation(qs[0:HD, h, cols], ra[0:HD, i % 2, :], ACT.Copy, scale=HD ** -0.5)
                        act.activation(qs[HD:P, h + 1, cols], ra[HD:P, i % 2, :], ACT.Copy,
                                       scale=HD ** -0.5).then_inc(s_hi, 1)

                def group(it, last):
                    for s in range(STEPS + 1):
                        j2 = s - 1 - LAG_T - LAG_PV
                        if j2 >= 0 and j2 % 2 == 0 and j2 // 2 < NPAIR:
                            j = j2 // 2
                            b, p, qt, _ = UNITS[2 * j]
                            col = (b * TB + qt) * P
                            act.wait_ge(s_pv, it * NPAIR + j + 1)
                            act.activation(o_t[:, p, col:col + P], ps_o[:, 0, j % 4 * P:(j % 4 + 1) * P],
                                           ACT.Copy).then_inc(s_oe, 1)
                        u = s - LAG_T
                        if 0 <= u < NU:
                            for part in range(2 if (u, 1) in CHUNK_OF else 1):
                                n = CHUNK_OF[(u, part)]
                                k0, k1 = part * 4, min(UNITS[u][2] + 1, part * 4 + 4)
                                act.wait_ge(s_t, it * NCH + n + 1)
                                if u >= R_PT:
                                    act.wait_ge(s_pv, it * NPAIR + (u - R_PT) // 2 + 1)
                                act.activation(prob_t[:, u % R_PT, k0:k1, :],
                                               ps_t[:, n % 2, 0:(k1 - k0) * P].rearrange("p (k n) -> p k n", n=P),
                                               ACT.Copy).then_inc(s_ev, 1)
                        if s < NU:
                            act.wait_ge(s_m, it * NU + s + 1)
                            if s >= R_PROB:
                                v = s - R_PROB
                                act.wait_ge(s_t, it * NCH + CHUNK_OF.get((v, 1), CHUNK_OF[(v, 0)]) + 1)
                            w = (UNITS[s][2] + 1) * P
                            act.activation(prob[:, s % R_PROB, 0:w], ps_s[:, s % 2, 0:w], ACT.Exp,
                                           bias=negmax[:, s:s + 1], accum_out=rowsum[:, s:s + 1])\
                                .then_inc(s_e, 1)
                        k = at_step(s, LAG_HI, "b1")
                        if k is not None and k % 2 == 1:
                            high(1, it * 2 + 1, k // 2)
                        k = at_step(s, LAG_HI, "b0")
                        if k is not None and k % 2 == 1 and not last:
                            high(0, it * 2 + 2, k // 2)

                for i in range(ROPES):
                    high(0, layer * NKV * 2, i)
                with act.Fori(0, NKV - 1) as g:
                    group(layer * NKV + g, False)
                group(layer * NKV + NKV - 1, True)
                norm_out(layer * 2 + 1, 1)
                act.wait_ge(s_rv, layer * 14 + 2)
                act.activation(pe_[:, :, :], pe_[:, :, :], ACT.Exp).then_inc(s_re, 1)
                with act.Fori(0, NE // 2) as e2:
                    it = layer * (NE // 2) + e2
                    for m in range(ITER_GU):
                        act.wait_ge(s_gu, it * ITER_GU + m + 1)
                        if m >= 2:
                            act.wait_ge(s_a, it * ITER_GU + m - 1)
                        r = m % 3
                        act.activation(sg[:, m % 2, :], bank(2 * r), ACT.Silu).then_inc(s_sg, 1)

        @block.vector
        def _(dve):
            vs = [0]

            def step(ins):
                vs[0] += 1
                ins.then_inc(s_vs, 1)
                dve.wait_ge(s_vs, vs[0])

            dve.wait_ge(s_in, 64)
            dve.wait_ge(s_cstep, 11)
            cstep = [0]
            for b in range(BATCH):
                for j in range(4):
                    dve.wait_ge(s_pje, (b * 4 + j) * 2 + 2)
                    dst = xbT[:, j, b * SEQ:(b + 1) * SEQ] if j < 3 else c_pad[:, b, 1:SEQ + 1]
                    dve.tensor_scalar(dst, proj[:, j, 0:SEQ], cw[:, j, 0:1], cb[:, j:j + 1], ALU.mult, ALU.add)\
                        .then_inc(s_vn, 1)
                    for k in range(1, TAPS):
                        cstep[0] += 1
                        dve.wait_ge(s_vn, cstep[0])
                        ins = dve.scalar_tensor_tensor(out=dst, in0=proj[:, j, k:k + SEQ], scalar=cw[:, j, k:k + 1],
                                                       in1=dst, op0=ALU.mult, op1=ALU.add)
                        ins.then_inc(s_vn if k < TAPS - 1 else s_conv, 1)
            N_CONV = cstep[0]
            dve.wait_ge(s_dd, 1)
            dve.tensor_tensor(d_t[:, :, :], bank(7)[:, 0:NT * SH].rearrange("p (t h) -> p t h", h=SH),
                              hc[:, 16:20].unsqueeze(1).to_broadcast([P, NT, SH]), ALU.add).then_inc(s_coef, 1)
            step(dve.tensor_tensor(dtr[:, :, :], bank(7)[:, P:2 * P].rearrange("p (t h) -> p t h", h=8),
                                   hc[:, 0:8].unsqueeze(1).to_broadcast([P, NT, 8]), ALU.add))
            step(dve.tensor_scalar(dt_s[:, :, :], dtr[:, :, :], 0.0, None, ALU.max))
            step(dve.scalar_tensor_tensor(out=dt_u[:, :, :], in0=dtr[:, :, :], scalar=-1.0, in1=dtr[:, :, :],
                                          op0=ALU.mult, op1=ALU.max))
            dve.wait_ge(s_as, 2)
            step(dve.tensor_scalar(dt_u[:, :, :], dt_e[:, :, :], 1.0, None, ALU.add))
            step(dve.tensor_scalar(dt_z[:, :, :], dt_u[:, :, :], 1.0, None, ALU.is_equal))
            step(dve.scalar_tensor_tensor(out=dtr[:, :, :], in0=dt_u[:, :, :], scalar=-1.0, in1=dt_z[:, :, :],
                                          op0=ALU.add, op1=ALU.add))
            step(dve.reciprocal(dtr[:, :, :], dtr[:, :, :]))
            dve.wait_ge(s_as, 3)
            step(dve.tensor_tensor(dtr[:, :, :], dtr[:, :, :], dt_l[:, :, :], ALU.mult))
            step(dve.tensor_tensor(dtr[:, :, :], dtr[:, :, :], dt_z[:, :, :], ALU.add))
            step(dve.tensor_tensor(dtr[:, :, :], dtr[:, :, :], dt_e[:, :, :], ALU.mult))
            step(dve.tensor_tensor(dt_s[:, :, :], dt_s[:, :, :], dtr[:, :, :], ALU.add))
            step(dve.scalar_tensor_tensor(out=a_dt[:, :, :], in0=dt_s[:, :, :], scalar=-1.0,
                                          in1=exp_a[:, :].unsqueeze(1).to_broadcast([P, NT, 8]),
                                          op0=ALU.mult, op1=ALU.mult))
            dve.wait_ge(s_cum, 1)
            step(dve.tensor_scalar(ncum[:, :, :], bank(4)[:, 0:P].rearrange("p (t h) -> p t h", h=8),
                                   -1.0, None, ALU.mult))
            step(dve.scalar_tensor_tensor(out=exp_e[:, :, :], in0=ncum[:, :, :], scalar=-1.0, in1=a_dt[:, :, :],
                                          op0=ALU.mult, op1=ALU.subtract))
            dve.wait_ge(s_as, 4)
            step(dve.tensor_tensor(exp_w[:, :, :], bank(5)[:, 0:P].rearrange("p (t h) -> p t h", h=8),
                                   ncum[:, :, :], ALU.add))
            dve.wait_ge(s_as, 6)
            dve.tensor_tensor(exp_w[:, :, :], exp_w[:, :, :], dt_s[:, :, :], ALU.mult).then_inc(s_coef, 1)

            def combine(v):
                c, b, d, t = scan_unit(v)
                rows = slice(d * SN, (d + 1) * SN)
                dh = slice(d * SH, (d + 1) * SH)
                dve.wait_ge(s_y, v + 1)
                if c > 0:
                    dve.tensor_tensor(tmp_h[rows, :].rearrange("p (h e) -> p h e", h=SH),
                                      state[rows, b, :].rearrange("p (h e) -> p h e", h=SH),
                                      exp_t[rows, t, dh].unsqueeze(2).to_broadcast([SN, SH, SP]), ALU.mult)\
                        .then_inc(s_vs, 1)
                    step(dve.tensor_tensor(tmp[:, :].rearrange("p (h e) -> p h e", h=SH),
                                           bank(4 + v % 2)[:, DI:2 * DI].rearrange("p (h e) -> p h e", h=SH),
                                           exp_e[:, t, dh].unsqueeze(2).to_broadcast([P, SH, SP]), ALU.mult))
                    vs[0] += 1
                    dve.wait_ge(s_vs, vs[0])
                    dve.tensor_tensor(state[rows, b, :], tmp_h[rows, :], bank(6 + v % 2)[rows, 0:DI], ALU.add)\
                        .then_inc(s_vs, 1)
                    step(dve.tensor_tensor(tmp[:, :], tmp[:, :], bank(4 + v % 2)[:, 0:DI], ALU.add))
                    vs[0] += 1
                    dve.wait_ge(s_vs, vs[0])
                    dve.tensor_tensor(y[:, t, :], y[:, t, :], tmp[:, :], ALU.add).then_inc(s_yr, 1)
                else:
                    dve.tensor_copy(state[rows, b, :], bank(6 + v % 2)[rows, 0:DI])
                    dve.tensor_tensor(y[:, t, :], y[:, t, :], bank(4 + v % 2)[:, 0:DI], ALU.add)\
                        .then_inc(s_yr, 1)
                dve.wait_ge(s_yr, v + 1)

            dve.wait_ge(s_yi, 1)
            for v in range(NV + 1):
                if v < NV:
                    c, b, d, t = scan_unit(v)
                    dve.wait_ge(s_dec, v + 1)
                    if v >= 2:
                        dve.wait_ge(s_y, v - 1)
                    for h in range(SH):
                        ins = dve.scalar_tensor_tensor(
                            out=mix[:, v % 2, h, :], in0=dec[:, v % 2, h, :],
                            scalar=dt_s[:, t, d * SH + h:d * SH + h + 1], in1=bank(2 + v % 2)[:, 0:P],
                            op0=ALU.mult, op1=ALU.mult)
                    ins.then_inc(s_mix, 1)
                if v >= 1:
                    combine(v - 1)

            def squares(src, width, chain):
                for t in range(NT):
                    ins = dve.tensor_tensor_reduce(out=sq_for(width, t), in0=src[:, t, :], in1=src[:, t, :], scale=1.0,
                                                   scalar=0.0, op0=ALU.mult, op1=ALU.add,
                                                   accum_out=ssq[:, t:t + 1])
                chain(ins)
                dve.tensor_scalar(var[:, :], ssq[:, :], 1.0 / width, EPS, ALU.mult, ALU.add).then_inc(s_var, 1)

            def sq_for(width, t):
                return hn[:, t, :] if width == DM else flat[:, t * DI:(t + 1) * DI]

            squares(y, DI, step)
            dve.wait_ge(s_pow, 1)
            for t in range(NT):
                dve.wait_ge(s_zs, t // 2 + 1)
                dve.scalar_tensor_tensor(out=y[:, t, :], in0=y[:, t, :], scalar=rstd[:, t:t + 1],
                                         in1=xb[:, t, 0:DI], op0=ALU.mult, op1=ALU.mult).then_inc(s_un, 1)
            for c in range(NC4):
                dve.wait_ge(s_so, c + 1)
                if c == 0:
                    dve.wait_ge(s_u, 48)
                ins = dve.tensor_tensor(x[:, 4 * c:4 * c + 4, :], bank(c).rearrange("p (t d) -> p t d", t=4),
                                        x[:, 4 * c:4 * c + 4, :], ALU.add)
            ins.then_inc(s_x, 1)
            dve.wait_ge(s_x, 1)

            def moments(chain):
                for t in range(NT):
                    if t >= 2:
                        pass
                    chain(dve.bn_stats(bn[:, t % 2, :], x[:, t, :]))
                    ins = dve.bn_aggr(mean_var[:, t, :], bn[:, t % 2, :])
                chain(ins)
                dve.tensor_scalar(var[:, :], mean_var[:, :, 1], EPS, None, ALU.add).then_inc(s_var, 1)

            moments(step)
            dve.wait_ge(s_pow, 2)
            for t in range(NT):
                ins = dve.tensor_scalar(x[:, t, :], x[:, t, :], mean_var[:, t, 0:1], rstd[:, t:t + 1],
                                        ALU.subtract, ALU.mult)
            ins.then_inc(s_x, 1)
            dve.wait_ge(s_x, 2)

            def norm(n, first):
                def chain(ins):
                    ins.then_inc(s_vn, 1)
                    dve.wait_ge(s_vn, N_CONV + n + 1)
                squares(x, DM, chain)
                dve.wait_ge(s_pow, n + 3)
                for t in range(NT):
                    ins = dve.tensor_scalar(hn[:, t, :], x[:, t, :], rstd[:, t:t + 1], None, ALU.mult)
                    if t % 4 == 3:
                        ins.then_inc(s_hn, 1)

            with dve.Fori(0, LAYERS) as layer:
                norm(layer * 2, True)

                def multiply(half, k, src):
                    i, c = k // 2, k // 6
                    dve.wait_ge(s_qk, half * PARTS + k + 1)
                    if i >= 2:
                        dve.wait_ge(s_lo, half * ROPES + i - 1)
                    dst, table = ((ra, cos_t), (rb, sin_t))[k % 2]
                    dve.tensor_tensor(dst[:, i % 2, :], src, table[:, c * CW:(c + 1) * CW], ALU.mult)\
                        .then_inc(s_rc, 1)

                def low(b, half, i):
                    c, what = i // 3, i % 3
                    cols = slice(b * SEQ + c * CW, b * SEQ + (c + 1) * CW)
                    dve.wait_ge(s_hi, half * ROPES + i + 1)
                    if what == 0:
                        dve.tensor_tensor(k_lo[:, cols], ra[:, i % 2, :], k_hi[:, cols].bitcast(F32),
                                          ALU.subtract).then_inc(s_lo, 1)
                    else:
                        h = 2 * (what - 1)
                        dve.scalar_tensor_tensor(
                            out=qs[HD:P, h, cols], in0=ra[0:HD, i % 2, :], scalar=HD ** -0.5,
                            in1=qs[0:HD, h, cols].bitcast(F32), op0=ALU.mult, op1=ALU.subtract)
                        dve.scalar_tensor_tensor(
                            out=qs[0:HD, h + 1, cols], in0=ra[HD:P, i % 2, :], scalar=HD ** -0.5,
                            in1=qs[HD:P, h + 1, cols].bitcast(F32), op0=ALU.mult, op1=ALU.subtract)\
                            .then_inc(s_lo, 1)

                def add_heads(it, c, src):
                    dve.wait_ge(s_ow, it * NC4 + c + 1)
                    dve.tensor_tensor(x[:, 4 * c:4 * c + 4, :], src.rearrange("p (t d) -> p t d", t=4),
                                      x[:, 4 * c:4 * c + 4, :], ALU.add).then_inc(s_xa, 1)

                def group(it, last):
                    for s in range(STEPS + LAG_LO):
                        if s < NU:
                            w = (UNITS[s][2] + 1) * P
                            dve.wait_ge(s_s, it * NU + s + 1)
                            dve.tensor_reduce(negmax[:, s:s + 1], ps_s[:, s % 2, 0:w], AX.X, ALU.max,
                                              negate=True).then_inc(s_m, 1)
                        u = s - LAG_N
                        if 0 <= u < NU:
                            w = (UNITS[u][2] + 1) * P
                            dve.wait_ge(s_e, it * NU + u + 1)
                            dve.reciprocal(rrow[:, u:u + 1], rowsum[:, u:u + 1]).then_inc(s_r, 1)
                            dve.wait_ge(s_r, it * NU + u + 1)
                            dve.tensor_scalar(prob[:, u % R_PROB, 0:w], prob[:, u % R_PROB, 0:w],
                                              rrow[:, u:u + 1], None, ALU.mult).then_inc(s_p, 1)
                        for b, name in ((1, "b1"), (0, "b0")):
                            if b == 0 and last:
                                continue
                            half = it * 2 + 2 - b
                            k = at_step(s, 1, name)
                            if k is not None:
                                multiply(half, k, ps_o[:, 1, :])
                            k = at_step(s, LAG_LO, name)
                            if k is not None and k % 2 == 1:
                                low(b, half, k // 2)
                        c = at_step(s, 1, "wo")
                        if c is not None:
                            add_heads(it, c, ps_o[:, 1, :])
                    for c in range(2, NC4):
                        add_heads(it, c, bank(c))
                    dve.wait_ge(s_xa, it * NC4 + NC4)

                half = layer * NKV * 2
                for k in range(PARTS + 2):
                    if k < PARTS:
                        multiply(half, k, bank(k % 4))
                    if k >= 3 and k % 2 == 1:
                        low(0, half, k // 2 - 1)
                with dve.Fori(0, NKV - 1) as g:
                    group(layer * NKV + g, False)
                group(layer * NKV + NKV - 1, True)
                xf = x[:, :, :].rearrange("p t d -> p (t d)")

                rv = [0]

                def rstep(ins, alone=False):
                    rv[0] += 1
                    ins.then_inc(s_rv, 1)
                    dve.wait_ge(s_rv, layer * 14 + rv[0])
                    if alone:
                        dve.sem_inc(s_alone, 1)

                rstep(dve.tensor_scalar(xf, xf, -CLIP, CLIP, ALU.max, ALU.min))
                norm(layer * 2 + 1, False)
                logits = ps_o[:, 0, 0:NT * NE].rearrange("p (t e) -> p t e", e=NE)
                dve.wait_ge(s_rt, layer + 1)
                dve.tensor_reduce(r1[:, :], logits, AX.X, ALU.max).then_inc(s_rmax, 1)
                dve.wait_ge(s_rmax, layer + 1)
                rstep(dve.tensor_tensor(pe_[:, :, :], logits, r1[:, :].unsqueeze(2).to_broadcast([P, NT, NE]),
                                        ALU.subtract))
                dve.wait_ge(s_re, layer + 1)
                rstep(dve.tensor_reduce(r2[:, :], pe_[:, :, :], AX.X, ALU.add))
                rstep(dve.reciprocal(r2[:, :], r2[:, :]))
                rstep(dve.tensor_tensor(pr[:, :, :], pe_[:, :, :], r2[:, :].unsqueeze(2).to_broadcast([P, NT, NE]),
                                        ALU.mult), alone=True)
                for t in range(NT):
                    ins = dve.max(top[:, t, :], pr[:, t, :])
                rstep(ins, alone=True)
                for t in range(NT):
                    ins = dve.max_index(topi[:, t, :], top[:, t, :], pr[:, t, :])
                rstep(ins)
                rstep(dve.tensor_copy(topif[:, :, :], topi[:, :, :]))
                rstep(dve.tensor_tensor(r1[:, :], top[:, :, 0], top[:, :, 1], ALU.add))
                rstep(dve.reciprocal(r1[:, :], r1[:, :]))
                rstep(dve.tensor_tensor(wtop[:, :, :], top[:, :, 0:2], r1[:, :].unsqueeze(2).to_broadcast([P, NT, 2]),
                                        ALU.mult))
                iob = iota8[:, :].unsqueeze(1).to_broadcast([P, NT, NE])
                dve.tensor_tensor(comb[:, :, :], iob, topif[:, :, 0:1].to_broadcast([P, NT, NE]), ALU.is_equal)
                rstep(dve.tensor_tensor(pr[:, :, :], iob, topif[:, :, 1:2].to_broadcast([P, NT, NE]), ALU.is_equal))
                dve.tensor_tensor(comb[:, :, :], comb[:, :, :], wtop[:, :, 0:1].to_broadcast([P, NT, NE]), ALU.mult)
                rstep(dve.tensor_tensor(pr[:, :, :], pr[:, :, :], wtop[:, :, 1:2].to_broadcast([P, NT, NE]), ALU.mult))
                dve.tensor_tensor(comb[:, :, :], comb[:, :, :], pr[:, :, :], ALU.add).then_inc(s_rv, 1)
                assert rv[0] + 1 == 14
                with dve.Fori(0, NE // 2) as e2:
                    it = layer * (NE // 2) + e2
                    dve.wait_ge(s_rv, layer * 14 + 14)
                    for m in range(ITER_GU + 2):
                        if m < ITER_GU:
                            c, fh, r = m // 2, m % 2, m % 3
                            dve.wait_ge(s_sg, it * ITER_GU + m + 1)
                            if c >= 2:
                                dve.wait_ge(s_dn, it * ITER_Y + c - 1)
                            dve.tensor_tensor(a_t[:, c % 2, fh, :], sg[:, m % 2, :], bank(2 * r + 1), ALU.mult)\
                                .then_inc(s_a, 1)
                        if m % 2 == 1 and m >= 3:
                            yi = (m - 3) // 2
                            q = yi // NC4
                            dve.wait_ge(s_dn, it * ITER_Y + yi + 1)
                            if yi >= NC4:
                                dve.wait_ge(s_ya, it * ITER_Y + yi - NC4 + 1)
                            for t4 in range(4):
                                t = yi % NC4 * 4 + t4
                                ins = dve.scalar_tensor_tensor(
                                    out=x[:, t, :], in0=ps_o[:, yi % 2, t4 * P:(t4 + 1) * P],
                                    scalar=comb[:, t, bass.ds(e2 * 2 + q, 1)], in1=x[:, t, :],
                                    op0=ALU.mult, op1=ALU.add)
                            ins.then_inc(s_ya, 1)
                    dve.wait_ge(s_ya, it * ITER_Y + ITER_Y)
                dve.tensor_scalar(xf, xf, -CLIP, CLIP, ALU.max, ALU.min).then_inc(s_clip, 1)
                dve.wait_ge(s_clip, layer + 1)
            dve.wait_ge(s_x1, 1)
            step(dve.tensor_tensor(x[:, :, :], x[:, :, :], x1[:, :, :], ALU.add))
            moments(step)
            dve.wait_ge(s_pow, 2 * LAYERS + 3)
            for t in range(NT):
                ins = dve.tensor_scalar(x[:, t, :], x[:, t, :], mean_var[:, t, 0:1], rstd[:, t:t + 1],
                                        ALU.subtract, ALU.mult)
                if t % 4 == 3:
                    ins.then_inc(s_fin, 1)

        @block.tensor
        def _(pe):
            pe.wait_ge(s_in, 64)
            for b in range(BATCH):
                for j in range(4):
                    for c in range(2):
                        i = (b * 4 + j) * 2 + c
                        if i >= 8:
                            pe.wait_ge(s_pje, i - 7)
                        pe.matmul(bank(i % 8), wsm[:, j * P:(j + 1) * P],
                                  hT[:, b * SEQ + c * CW:b * SEQ + (c + 1) * CW], start=True, stop=True)\
                            .then_inc(s_pj, 1)
            pe.wait_ge(s_const, 10)
            pe.wait_ge(s_pje, 16)
            for t in range(NT):
                pe.wait_ge(s_silu, 4 * (t // TB) + 4)
                tok = slice(t * P, (t + 1) * P)
                if t >= 4:
                    pe.wait_ge(s_tre, t - 3)
                for j in range(3):
                    ins = pe.transpose(bank(t % 4)[:, j * P:(j + 1) * P], xbT[:, j, tok], ident[:, :])
                ins.then_inc(s_tr, 1)
                for j in range(2):
                    pe.matmul(bank(7)[:, t * SH:(t + 1) * SH], xbT[:, j, tok], dw[:, j, :],
                              start=(j == 0), stop=(j == 1))
                ins = pe.matmul(bank(7)[:, P + t * 8:P + (t + 1) * 8], hT[:, tok], wsm[:, 4 * P + DI:4 * P + DI + 8],
                                start=True, stop=True)
            ins.then_inc(s_dd, 1)
            pe.wait_ge(s_vs, 12)
            for d in range(2):
                pe.matmul(bank(4)[:, 0:P].rearrange("p (t h) -> p t h", h=8)[:, :, d * SH:(d + 1) * SH],
                          tri[:, d, :], a_dt[:, :, d * SH:(d + 1) * SH], start=True, stop=True)
            pe.matmul(bank(5)[:, 0:P], ones[:, :], a_dt[:, :, :].rearrange("p t h -> p (t h)"),
                      start=True, stop=True).then_inc(s_cum, 1)
            pe.wait_ge(s_tre, NT)
            pe.wait_ge(s_coef, 2)

            def products(v):
                c, b, d, t = scan_unit(v)
                rows = slice(d * SN, (d + 1) * SN)
                pe.wait_ge(s_mix, v + 1)
                if v >= 2:
                    pe.wait_ge(s_yr, v - 1)
                for h in range(SH):
                    pe.matmul(bank(4 + v % 2)[:, h * SP:(h + 1) * SP], mix[:, v % 2, h, :],
                              xb[:, t, h * SP:(h + 1) * SP], start=True, stop=True)
                if c > 0:
                    pe.wait_ge(s_yr, v - 3)
                    pe.matmul(bank(4 + v % 2)[:, DI:2 * DI], c_cols(t, d), state[rows, b, :], start=True, stop=True)
                pe.wait_ge(s_xw, v + 1)
                pe.matmul(bank(6 + v % 2)[rows, 0:DI], xb[:, t, DI + d * SN:DI + (d + 1) * SN], xw[:, v % 2, :],
                          start=True, stop=True).then_inc(s_y, 1)

            for v in range(NV + 1):
                if v < NV:
                    c, b, d, t = scan_unit(v)
                    rows = slice(d * SN, (d + 1) * SN)
                    pe.wait_ge(s_au, v + 1)
                    if v >= 2:
                        pe.wait_ge(s_mix, v - 1)
                    pe.matmul(bank(v % 2), ones[:, :], a_u[:, v % 2].rearrange("p h t -> p (h t)"),
                              start=True, stop=False)
                    pe.matmul(bank(v % 2), ident_b[:, :], mask4_b[:, d, :], start=False, stop=True)
                    pe.matmul(bank(2 + v % 2)[:, 0:P], xbT[rows, 2, t * P:(t + 1) * P], c_cols(t, d),
                              start=True, stop=True).then_inc(s_eg, 1)
                if v >= 1:
                    products(v - 1)
            pe.wait_ge(s_mix, NV)
            for i in range(NT // 2):
                if i >= 4:
                    pe.wait_ge(s_zs, i - 3)
                for k in range(2):
                    t = 2 * i + k
                    ins = pe.matmul(bank(i % 4)[:, k * DI:(k + 1) * DI], hT[:, t * P:(t + 1) * P],
                                    wsm[:, 4 * P:4 * P + DI], start=True, stop=True)
                ins.then_inc(s_z, 1)
            pe.wait_ge(s_yr, NV)
            for i in range(NT // 2):
                pe.wait_ge(s_un, 2 * i + 2)
                if i >= 2:
                    pe.wait_ge(s_une, i - 1)
                for k in range(2):
                    for j in range(2):
                        ins = pe.transpose(bank(4 + i % 2)[:, (k * 2 + j) * P:(k * 2 + j + 1) * P],
                                           y[:, 2 * i + k, j * P:(j + 1) * P], ident[:, :])
                ins.then_inc(s_unt, 1)
            pe.wait_ge(s_zs, NT // 2)
            for c in range(NC4):
                pe.wait_ge(s_une, 2 * c + 2)
                for t4 in range(4):
                    t = 4 * c + t4
                    for j in range(2):
                        ins = pe.matmul(bank(c)[:, t4 * P:(t4 + 1) * P], unT[:, j, t * P:(t + 1) * P], wout[:, j, :],
                                        start=(j == 0), stop=(j == 1))
                ins.then_inc(s_so, 1)
            pe.wait_ge(s_x, 1)

            def norm_t(n):
                for c in range(NC4):
                    pe.wait_ge(s_hn, n * NC4 + c + 1)
                    for t4 in range(4):
                        ins = pe.transpose(bank(c)[:, t4 * P:(t4 + 1) * P], hn[:, 4 * c + t4, :], ident[:, :])
                    ins.then_inc(s_nt, 1)

            with pe.Fori(0, LAYERS) as layer:
                norm_t(layer * 2)
                pe.wait_ge(s_wl, layer * 16 + 16)
                for i in range(NT // 2):
                    pe.wait_ge(s_ht, layer * 2 * NC4 + i // 2 + 1)
                    if i >= 4:
                        pe.wait_ge(s_ve, layer * (NT // 2) + i - 3)
                    for k in range(2):
                        t = 2 * i + k
                        ins = pe.matmul(bank(4 + i % 4)[:, k * 256:(k + 1) * 256], hT[:, t * P:(t + 1) * P],
                                        wlay[:, 2 + NE:WLAY], start=True, stop=True)
                    ins.then_inc(s_v, 1)

                def part(k, b, dst):
                    i = k // 2
                    c, what = i // 3, i % 3
                    col = 2 * QW if what == 0 else (what - 1) * P
                    col += k % 2 * (P if what == 0 else QW)
                    pe.matmul(dst, wqkv[:, col:col + P], hT[:, b * SEQ + c * CW:b * SEQ + (c + 1) * CW],
                              start=True, stop=True).then_inc(s_qk, 1)

                def heads_out(it, c, dst):
                    for t4 in range(4):
                        t = 4 * c + t4
                        for p in range(2):
                            ins = pe.matmul(dst[:, t4 * P:(t4 + 1) * P], o_t[:, p, t * P:(t + 1) * P],
                                            wo[:, p, :], start=(p == 0), stop=(p == 1))
                    ins.then_inc(s_ow, 1)

                def group(it, last):
                    pe.wait_ge(s_ve, layer * (NT // 2) + NT // 2)
                    pe.wait_ge(s_rc, it * 2 * PARTS + PARTS)
                    for s in range(STEPS):
                        if s < NU:
                            b, p, qt, hh = UNITS[s]
                            if s == 0 or s == NU // 2:
                                pe.wait_ge(s_lo, (it * 2 + b) * ROPES + ROPES)
                            if s >= 2:
                                pe.wait_ge(s_e, it * NU + s - 1)
                            nk = qt + 1
                            q_cols = slice(b * SEQ + qt * P, b * SEQ + (qt + 1) * P)
                            for k0 in range(0, nk, 4):
                                n = max(min(nk - k0, 4), 2) * P
                                dst = ps_s[:, s % 2, k0 * P:k0 * P + n]
                                k_cols = slice(b * SEQ + k0 * P, b * SEQ + k0 * P + n)
                                pe.matmul(dst, qs[:, 2 * p + hh, q_cols], k_hi[:, k_cols], start=True, stop=False)
                                if k0 + 4 >= nk:
                                    pe.matmul(ps_s[:, s % 2, qt * P:(qt + 1) * P], ident_b[:, :], causal_b[:, :],
                                              start=False, stop=False)
                                ins = pe.matmul(dst, qs[:, 2 * p + hh, q_cols], k_lo[:, k_cols], start=False,
                                                stop=True)
                            ins.then_inc(s_s, 1)
                        u = s - LAG_T
                        if 0 <= u < NU:
                            pe.wait_ge(s_p, it * NU + u + 1)
                            for half in range(2 if (u, 1) in CHUNK_OF else 1):
                                n = CHUNK_OF[(u, half)]
                                if n >= 2:
                                    pe.wait_ge(s_ev, it * NCH + n - 1)
                                for k in range(half * 4, min(UNITS[u][2] + 1, half * 4 + 4)):
                                    ins = pe.transpose(ps_t[:, n % 2, k % 4 * P:(k % 4 + 1) * P],
                                                       prob[:, u % R_PROB, k * P:(k + 1) * P], ident[:, :])
                                ins.then_inc(s_t, 1)
                        j2 = s - LAG_T - LAG_PV
                        if j2 >= 0 and j2 % 2 == 0 and j2 // 2 < NPAIR:
                            j = j2 // 2
                            b, p, qt, _ = UNITS[2 * j]
                            if j == 0:
                                pe.wait_ge(s_vg, it + 1)
                            pe.wait_ge(s_ev, it * NCH + CHUNK_OF.get((2 * j + 1, 1), CHUNK_OF[(2 * j + 1, 0)]) + 1)
                            if j >= 1:
                                pe.wait_ge(s_oe, it * NPAIR + j)
                            for kt in range(qt + 1):
                                for hh in range(2):
                                    ins = pe.matmul(
                                        ps_o[hh * HD:(hh + 1) * HD, 0, j % 4 * P:(j % 4 + 1) * P],
                                        v_g[:, b * TB + kt, :], prob_t[:, (2 * j + hh) % R_PT, kt, :],
                                        start=(kt == 0), stop=(kt == qt))
                            ins.then_inc(s_pv, 1)
                        kind, k = SIDE.get(s, ("", 0))
                        if kind == "b1":
                            pe.wait_ge(s_rc, (it * 2 + 1) * PARTS + k)
                            part(k, 1, ps_o[:, 1, :])
                        if kind == "wo":
                            if k == 0:
                                pe.wait_ge(s_rc, (it * 2 + 2) * PARTS)
                                pe.wait_ge(s_wo, it * 16 + 16)
                                pe.wait_ge(s_oe, it * NPAIR + NPAIR // 2)
                            else:
                                pe.wait_ge(s_xa, it * NC4 + k)
                            heads_out(it, k, ps_o[:, 1, :])
                        if kind == "b0" and not last:
                            if k == 0:
                                pe.wait_ge(s_xa, it * NC4 + 2)
                                pe.wait_ge(s_wa, it * 16 + 32)
                            else:
                                pe.wait_ge(s_rc, (it * 2 + 2) * PARTS + k)
                            part(k, 0, ps_o[:, 1, :])
                    pe.wait_ge(s_oe, it * NPAIR + NPAIR)
                    for c in range(2, NC4):
                        heads_out(it, c, bank(c))
                    pe.wait_ge(s_xa, it * NC4 + NC4)

                half = layer * NKV * 2
                pe.wait_ge(s_ht, layer * 2 * NC4 + NC4)
                pe.wait_ge(s_wa, layer * NKV * 16 + 16)
                for k in range(PARTS):
                    if k >= 4:
                        pe.wait_ge(s_rc, half * PARTS + k - 3)
                    part(k, 0, bank(k % 4))
                with pe.Fori(0, NKV - 1) as g:
                    group(layer * NKV + g, False)
                group(layer * NKV + NKV - 1, True)
                norm_t(layer * 2 + 1)
                for t in range(NT):
                    pe.wait_ge(s_ht, layer * 2 * NC4 + NC4 + t // 4 + 1)
                    ins = pe.matmul(ps_o[:, 0, t * NE:(t + 1) * NE], hT[:, t * P:(t + 1) * P], wlay[:, 2:2 + NE],
                                    start=True, stop=True)
                ins.then_inc(s_rt, 1)
                with pe.Fori(0, NE // 2) as e2:
                    it = layer * (NE // 2) + e2
                    pe.wait_ge(s_rv, layer * 14 + 2)
                    for m in range(ITER_GU + 2):
                        if m < ITER_GU:
                            q, c, fh, r = m // GU, m // 2 % NC4, m % 2, m % 3
                            if m % GU == 0:
                                pe.wait_ge(s_we[q], it * 16 + 16)
                            if m >= 3:
                                pe.wait_ge(s_a, it * ITER_GU + m - 2)
                            for k in range(2):
                                ins = pe.matmul(bank(2 * r + k), wexp[:, q, k * FF + fh * P:k * FF + (fh + 1) * P],
                                                hT[:, c * CW:(c + 1) * CW], start=True, stop=True)
                            ins.then_inc(s_gu, 1)
                        if m % 2 == 1 and m >= 3:
                            yi = (m - 3) // 2
                            q = yi // NC4
                            pe.wait_ge(s_a, it * ITER_GU + 2 * yi + 2)
                            if yi >= 2:
                                pe.wait_ge(s_ya, it * ITER_Y + yi - 1)
                            for t4 in range(4):
                                for fh in range(2):
                                    ins = pe.matmul(ps_o[:, yi % 2, t4 * P:(t4 + 1) * P],
                                                    a_t[:, yi % 2, fh, t4 * P:(t4 + 1) * P],
                                                    wexp[:, q, 2 * FF + fh * P:2 * FF + (fh + 1) * P],
                                                    start=(fh == 0), stop=(fh == 1))
                            ins.then_inc(s_dn, 1)
                    pe.wait_ge(s_ya, it * ITER_Y + ITER_Y)


def layouts(a):
    def tokens(v):
        return np.ascontiguousarray(v.reshape(NT, P, DM).transpose(1, 0, 2))

    u = a["L0_attn_u"].reshape(TOK, DM)
    w = a["L0_attn_in_proj_w"]
    z, xs = w[:DI], w[DI:2 * DI]
    bc = w[2 * DI:2 * DI + 4 * SN]
    dt = w[2 * DI + 4 * SN:]
    perm = np.concatenate([np.arange(DI), DI + np.concatenate(
        [np.arange(0, SN), np.arange(2 * SN, 3 * SN), np.arange(SN, 2 * SN), np.arange(3 * SN, 4 * SN)])])
    w_in = np.concatenate([np.concatenate([xs, bc])[perm], z, dt]).T
    cw = a["L0_attn_conv1d_w"][:, 0, :][perm].reshape(4, P, TAPS).transpose(1, 0, 2).reshape(P, -1)
    cb = a["L0_attn_conv1d_b"][perm].reshape(4, P).T
    rms = a["L0_attn_rms_w"].reshape(2, P).T

    def rows(v):
        return np.broadcast_to(v[None], (P, v.size))

    small = np.concatenate([cw, cb, rms, rows(a["L0_attn_dt_bias"]), rows(a["L0_attn_dt_bias"]),
                            rows(a["L0_attn_A_log"]), rows(a["L0_attn_A_log"]), rows(a["L0_attn_D_b"])], axis=1)
    wout = a["L0_attn_outproj_w"].T.reshape(2, P, DM).transpose(1, 0, 2).reshape(P, -1)
    dw = a["L0_attn_D_w"].T.reshape(2, P, SH).transpose(1, 0, 2).reshape(P, -1)
    scan_out = np.concatenate([wout, dw], axis=1)

    inv = (np.float32(1.0) / np.float32(THETA) ** (np.arange(0, HD, 2, dtype=np.float32) / np.float32(HD)))
    f = np.arange(SEQ, dtype=np.float32)[:, None] * inv.astype(np.float32)
    c, s = np.cos(f).T, np.sin(f).T
    rope = np.stack([np.concatenate([c, c, c, c]), np.concatenate([-s, s, -s, s])]).astype(np.float32)

    half = np.concatenate([np.arange(HD // 2, HD), np.arange(HD // 2)])
    wq = a["L0_ffn_wq"].reshape(LAYERS, DM, NKV, REP, HD)
    wk = a["L0_ffn_wk"].reshape(LAYERS, DM, NKV, 1, HD)
    attn = np.concatenate([wq, wq[..., half], wk, wk, wk[..., half], wk[..., half]], axis=3)
    attn = attn.transpose(0, 2, 1, 3, 4).reshape(LAYERS * NKV, DM, WQKV)
    w_o = a["L0_ffn_wo"].reshape(LAYERS, NKV, 2, P, DM).transpose(0, 1, 3, 2, 4).reshape(LAYERS * NKV, P, 2, DM)
    lay = np.concatenate([a["L0_ffn_ln1_w"][:, :, None], a["L0_ffn_ln2_w"][:, :, None], a["L0_ffn_wr"],
                          a["L0_ffn_wv"]], axis=2)
    wd = a["L0_ffn_wd"].reshape(LAYERS, NE, 2, P, DM).transpose(0, 1, 3, 2, 4).reshape(LAYERS, NE, P, 2 * DM)
    exp = np.concatenate([a["L0_ffn_wg"], a["L0_ffn_wu"], wd], axis=3).reshape(LAYERS * NE, P, -1)

    def ahead(v, n):
        return np.concatenate([v, v[:n]])

    return {
        "u_tok": tokens(u), "u_feat": u.T, "w_in": w_in, "conv_w": small, "w_scan_out": scan_out, "rope": rope,
        "w_attn": ahead(attn, 1), "w_o": ahead(w_o, 1), "w_layer": ahead(lay, 1), "w_expert": ahead(exp, 2),
    }


def kernel(**inputs):
    import concourse.bacc as bacc
    from concourse.bass_utils import run_bass_kernel_spmd

    arrays = {n: np.ascontiguousarray(v) for n, v in layouts({k: np.asarray(v) for k, v in inputs.items()}).items()}
    nc = bacc.Bacc("TRN2", target_bir_lowering=False, num_devices=1)
    aps = {n: nc.dram_tensor(n, v.shape, F32, kind="ExternalInput").ap() for n, v in arrays.items()}
    out = nc.dram_tensor("out", (P, NT, DM), F32, kind="ExternalOutput").ap()
    build(nc, out=out, **aps)
    r = run_bass_kernel_spmd(nc, [arrays], core_ids=[0])
    return r.results[0]["out"].transpose(1, 0, 2).reshape(BATCH, SEQ, DM)
```

```python
from contextlib import ExitStack

import numpy as np
import concourse.bass as bass
from concourse import mybir

F32 = mybir.dt.float32
F32R = mybir.dt.float32r
BF16 = mybir.dt.bfloat16
U32 = mybir.dt.uint32
ALU = mybir.AluOpType
ACT = mybir.ActivationFunctionType
AX = mybir.AxisListType

P = 128
BATCH, SEQ, DM = 2, 1024, 128
TOK = BATCH * SEQ
NT = TOK // P
TB = SEQ // P
CW = 512
NC4 = TOK // CW

SH, SP, SN = 4, 64, 64
DI = SH * SP
TAPS = 7
PAD = TAPS // 2
CONV_ORDER = [0, 3, 1, 2]
CONV_PE = [(0, 3), (1, 3), (1, 2)]
RMS_EPS = 1e-5

LAYERS, NH, NKV, HD, FF, NE = 4, 16, 4, 64, 256, 8
REP = NH // NKV
QW = REP * HD
WQKV = QW + P
WLAY = 2 + NE + NKV * HD
WEXP = 3 * FF
THETA, EPS = 10000.0, 1e-5
CLIP = 100.0

QT_ORDER = [3, 4, 2, 5, 1, 6, 0, 7]
UNITS = [(b, p, qt, hh) for b in range(BATCH) for p in range(REP // 2) for qt in QT_ORDER for hh in range(2)]
NU = len(UNITS)
NPAIR = NU // 2
CHUNKS = [(u, part) for u in range(NU) for part in range(2 if UNITS[u][2] >= 4 else 1)]
CHUNK_OF = {c: n for n, c in enumerate(CHUNKS)}
NCH = len(CHUNKS)
LAG_N, LAG_T, LAG_PV = 1, 3, 2
R_PROB, R_PT = 5, 4
ITEMS = [(c, what) for c in range(SEQ // CW) for what in (0, 1)] + [(c, 2) for c in range(SEQ // CW)]
ROPES = len(ITEMS)
FIRST = 4
ROT = HD // 2
SIDE = {s: ("b1", k) for k, s in enumerate([2, 6, 10, 14, 18, 22])}
SIDE |= {28 + 4 * k: ("b0", k) for k in range(ROPES)}
SIDE |= {42: ("wo", 0), 46: ("wo", 1), 4: ("wo", 2), 8: ("wo", 3)}
SIDE |= {52: ("tr", 0), 55: ("tr", 1)}
NORM_STEPS = {45: ("clip", 0), 48: ("clip", 1), 50: ("scale", 0), 53: ("scale", 1), 54: ("low", 0), 57: ("low", 1),
              NU + 6: ("clip", 2), NU + 10: ("clip", 3)}
SPLIT = 25
LAG_COS, LAG_HI, LAG_LO = 2, 6, 7
HEAD = 12


def chunk(u, part):
    n = CHUNK_OF.get((u % NU, part))
    return None if n is None else u // NU * NCH + n


def last_chunk(u):
    return chunk(u, 1) or chunk(u, 0)


def buffer_before(u):
    r = u % NU
    if r >= R_PROB:
        return u - R_PROB
    return u - r - 1 - (NU - 1 - r) % R_PROB if u >= NU else None


def side(s, last):
    if s < 0 or s % NU not in SIDE:
        return None
    kind, k = SIDE[s % NU]
    owner = s // NU - (kind == "wo" and k >= 2)
    if owner < 0 or last and (owner == 1 or kind == "b0") or kind == "tr" and not last:
        return None
    return kind, k, owner


def half_of(it, item):
    return (it + item[2]) * 2 + (1 if item[0] == "b1" else 2)


def side_before(s, last):
    while s > 0:
        s -= 1
        if side(s, last):
            return side(s, last)
    return None


ARENA = 20480
GU = NC4 * 2
ITER_GU, ITER_Y = 2 * GU, 2 * NC4
HEAD_M = 6
LAST_M = ITER_GU + 2
SPLIT_M = {4: 1, 12: 2}
ROUTER_M = 1
M_BANKS = [m % 3 for m in range(ITER_GU - 1)] + [1]


def split_at(m, last):
    e = SPLIT_M.get(m % ITER_GU)
    return None if e is None or last and e == 2 else m // ITER_GU * 2 + e


def item_before(m):
    n = m - 1
    while n >= 0 and M_BANKS[n % ITER_GU] != M_BANKS[m % ITER_GU]:
        n -= 1
    return n


def build(nc, u_tok, u_feat, w_in, conv_w, w_scan_out, rope, w_attn, w_o, w_layer, w_expert, out):
    with ExitStack() as ctx:
        def sb(name, shape, dt=F32):
            return ctx.enter_context(nc.sbuf_tensor(name, shape, dt))

        def sem(name):
            return ctx.enter_context(nc.semaphore(name))

        x = sb("x", [P, NT, DM])
        x1 = sb("x1", [P, NT, DM])
        hT = sb("hT", [P, TOK])
        cos_t = sb("cos_t", [P, SEQ])
        sin_t = sb("sin_t", [P, SEQ])
        q_sb = sb("q_sb", [P, 2, CW])
        wqkv = sb("wqkv", [P, WQKV])
        wqk_hi = sb("wqk_hi", [P, WQKV], F32R)
        wqk_lo = sb("wqk_lo", [P, WQKV], F32R)
        h_hi = sb("h_hi", [P, TOK], F32R)
        h_lo = sb("h_lo", [P, TOK], F32R)
        wo = sb("wo", [P, 2, DM])
        wlay = sb("wlay", [P, WLAY])
        wexp = sb("wexp", [P, 2, WEXP])
        ident = sb("ident", [P, P])
        ident_b = sb("ident_b", [P, P], BF16)
        causal_b = sb("causal_b", [P, P], BF16)
        iota8 = sb("iota8", [P, NE])
        ssq = sb("ssq", [P, NT])
        var = sb("var", [P, NT])
        rstd = sb("rstd", [P, NT])
        mean_var = sb("mean_var", [P, NT, 2])
        bn = sb("bn", [P, 2, 6])
        neg_half = sb("neg_half", [P, NT])
        negmax = sb("negmax", [P, NU])
        rowsum = sb("rowsum", [P, NU])
        rrow = sb("rrow", [P, NU])
        pr = sb("pr", [P, NT, NE])
        pe_ = sb("pe_", [P, NT, NE])
        top = sb("top", [P, NT, 8])
        topi = sb("topi", [P, NT, 8], U32)
        topif = sb("topif", [P, NT, 8])
        r1 = sb("r1", [P, NT])
        r2 = sb("r2", [P, NT])
        wtop = sb("wtop", [P, NT, 2])
        comb = sb("comb", [P, NT, NE])
        qs = sb("qs", [P, REP, TOK], F32R)
        k_hi = sb("k_hi", [P, TOK], F32R)
        k_lo = sb("k_lo", [P, TOK], F32R)
        wg_hi = qs[:, 0:2, 0:2 * FF]
        wg_lo = qs[:, 0:2, 2 * FF:4 * FF]

        arena = sb("arena", [P, ARENA])
        at = [0]

        def cut(*dims, new=False):
            if new:
                at[0] = 0
            n = int(np.prod(dims))
            v = arena[:, at[0]:at[0] + n]
            at[0] += n
            assert at[0] <= ARENA
            if len(dims) == 2:
                v = v.rearrange("p (a b) -> p a b", b=dims[1])
            if len(dims) == 3:
                v = v.rearrange("p (a b c) -> p a b c", b=dims[1], c=dims[2])
            return v

        ra = cut(2, CW, new=True)
        rb = cut(2, CW)
        v_all = cut(NT, NKV * HD)
        v_g = cut(NT, HD)
        prob = cut(R_PROB, SEQ)
        prob_t = cut(R_PT, TB, P)
        o_t = cut(2, TOK)
        hn = o_t.rearrange("p a b -> p (a b)")[:, 0:TOK].rearrange("p (t d) -> p t d", d=DM)
        sg = prob_t[:, 0]
        sg = sg.rearrange("p a b -> p (a b)").rearrange("p (a b) -> p a b", b=CW)
        a_t = prob_t[:, 1:3].rearrange("p a b c -> p (a b c)").rearrange("p (s f n) -> p s f n", s=2, f=2)

        SEQP = SEQ + 2 * PAD
        proj = cut(4, SEQP, new=True)
        xbT = cut(3, TOK)
        c_pad = cut(BATCH, SEQ + 2)
        xb = cut(NT, DI + P)
        state = cut(BATCH, DI)
        mask4 = cut(2, SH * P // 2)
        diag_b = cut(TAPS, P)
        y = xbT.rearrange("p a b -> p (a b)")[:, 0:NT * DI].rearrange("p (t d) -> p t d", d=DI)
        flat = proj.rearrange("p a b -> p (a b)")
        a_u = flat[:, 0:1024].rearrange("p (r h t) -> p r h t", r=2, h=SH)
        dec = flat[:, 1024:2048].rearrange("p (r h t) -> p r h t", r=2, h=SH)
        mix = flat[:, 2048:3072].rearrange("p (r h t) -> p r h t", r=2, h=SH)
        xw = flat[:, 3072:3584].rearrange("p (r d) -> p r d", r=2)
        tmp = flat[:, 3584:3840]
        aged = q_sb[:, :, :].rearrange("p a b -> p (a b)").rearrange("p (r d) -> p r d", r=4)
        unT = flat[:, 0:2 * TOK].rearrange("p (j t) -> p j t", j=2)
        mask4_b = mask4.bitcast(BF16)
        x1_at = [0]

        def cut_x1(*dims):
            n = int(np.prod(dims))
            v = x1[:, :, :].rearrange("p t d -> p (t d)")[:, x1_at[0]:x1_at[0] + n]
            x1_at[0] += n
            assert x1_at[0] <= NT * DM
            return v.rearrange("p (a b) -> p a b", b=dims[1]) if len(dims) == 2 else v

        wsm = cut_x1(4 * P + DI + 8)
        wout = wqkv[:, 0:2 * DM].rearrange("p (j d) -> p j d", j=2)
        dw = wqkv[:, 256:264].rearrange("p (j h) -> p j h", j=2)
        cw = wqkv[:, 264:264 + 4 * TAPS].rearrange("p (j k) -> p j k", j=4)
        cb = wqkv[:, 292:296]
        rmsw = wqkv[:, 296:298]
        hc = wqkv[:, 298:298 + 20]
        tri = cut_x1(4, P)
        ones = cut_x1(P)
        dtr = cut_x1(NT, 8)
        dt_e = cut_x1(NT, 8)
        dt_u = cut_x1(NT, 8)
        dt_l = cut_x1(NT, 8)
        dt_z = sb("dt_z", [P, NT, 8])
        dt_s = sb("dt_s", [P, NT, 8])
        a_dt = sb("a_dt", [P, NT, 8])
        ncum = sb("ncum", [P, NT, 8])
        exp_e = sb("exp_e", [P, NT, 8])
        exp_w = sb("exp_w", [P, NT, 8])
        exp_t = sb("exp_t", [P, NT, 8])
        d_t = sb("d_t", [P, NT, SH])
        exp_a = sb("exp_a", [P, 8])

        diag = {3: q_sb[:, :, :].rearrange("p a b -> p (a b)")[:, 0:TAPS * P]
                .rearrange("p (k n) -> p k n", k=TAPS), 2: diag_b}

        ps_s = ctx.enter_context(nc.psum_tensor("ps_s", [P, 2, 2 * CW], F32))
        ps_t = ctx.enter_context(nc.psum_tensor("ps_t", [P, 2, CW], F32))
        ps_o = ctx.enter_context(nc.psum_tensor("ps_o", [P, 2, CW], F32))

        def bank(i):
            if i < 4:
                return ps_s[:, i // 2, (i % 2) * CW:(i % 2 + 1) * CW]
            return (ps_t if i < 6 else ps_o)[:, i % 2, :]

        s_const = sem("s_const")
        s_cstep = sem("s_cstep")
        s_in = sem("s_in")
        s_u = sem("s_u")
        s_wa = sem("s_wa")
        s_wo = sem("s_wo")
        s_wl = sem("s_wl")
        s_we = [sem("s_we0"), sem("s_we1")]
        s_out = sem("s_out")
        s_pj = sem("s_pj")
        s_pje = sem("s_pje")
        s_diag = sem("s_diag")
        s_conv = sem("s_conv")
        s_cpe = sem("s_cpe")
        s_silu = sem("s_silu")
        s_vs = sem("s_vs")
        s_as = sem("s_as")
        s_tr = sem("s_tr")
        s_tre = sem("s_tre")
        s_dtp = sem("s_dtp")
        s_dd = sem("s_dd")
        s_cum = sem("s_cum")
        s_coef = sem("s_coef")
        s_yi = sem("s_yi")
        s_au = sem("s_au")
        s_xw = sem("s_xw")
        s_aged = sem("s_aged")
        s_eg = sem("s_eg")
        s_dec = sem("s_dec")
        s_mix = sem("s_mix")
        s_y = sem("s_y")
        s_yr = sem("s_yr")
        s_z = sem("s_z")
        s_zs = sem("s_zs")
        s_pow = sem("s_pow")
        s_var = sem("s_var")
        s_un = sem("s_un")
        s_unt = sem("s_unt")
        s_une = sem("s_une")
        s_so = sem("s_so")
        s_x = sem("s_x")
        s_x1 = sem("s_x1")
        s_qhi = sem("s_qhi")
        s_qlo = sem("s_qlo")
        s_ghi = sem("s_ghi")
        s_glo = sem("s_glo")
        s_hh = sem("s_hh")
        s_hl = sem("s_hl")
        s_hn = sem("s_hn")
        s_nt = sem("s_nt")
        s_ht = sem("s_ht")
        s_vn = sem("s_vn")
        s_v = sem("s_v")
        s_ve = sem("s_ve")
        s_vg = sem("s_vg")
        s_qk = sem("s_qk")
        s_rc = sem("s_rc")
        s_qc = sem("s_qc")
        s_rp = sem("s_rp")
        s_rs = sem("s_rs")
        s_hi = sem("s_hi")
        s_lo = sem("s_lo")
        s_s = sem("s_s")
        s_m = sem("s_m")
        s_e = sem("s_e")
        s_r = sem("s_r")
        s_p = sem("s_p")
        s_t = sem("s_t")
        s_ev = sem("s_ev")
        s_pv = sem("s_pv")
        s_oe = sem("s_oe")
        s_ow = sem("s_ow")
        s_xa = sem("s_xa")
        s_rt = sem("s_rt")
        s_rmax = sem("s_rmax")
        s_alone = sem("s_alone")
        s_clip = sem("s_clip")
        s_rv = sem("s_rv")
        s_re = sem("s_re")
        s_gu = sem("s_gu")
        s_sg = sem("s_sg")
        s_a = sem("s_a")
        s_dn = sem("s_dn")
        s_ya = sem("s_ya")
        s_fin = sem("s_fin")

        block = ctx.enter_context(nc.Block())

        def scan_unit(v):
            c, b, d = v // 4, v // 2 % 2, v % 2
            return c, b, d, b * TB + (c if d == 0 else TB - 1 - c)

        def pool_blocks(i):
            return 2 if ITEMS[i][1] else 1

        def rotated(engine, i, n, src):
            c, m = ITEMS[i][0], n ^ 1
            to, fr = slice(n * ROT, (n + 1) * ROT), slice(m * ROT, (m + 1) * ROT)
            return engine.tensor_tensor(rb[to, i % 2, :], src[fr, :], sin_t[fr, c * CW:(c + 1) * CW], ALU.mult)

        NV = 4 * TB
        N_VAR = 2
        N_RV = 13

        def c_cols(t, d):
            b, lo = t // TB, t % TB * P
            return c_pad[d * SN:(d + 1) * SN, b, lo + 2 * d:lo + 2 * d + P]

        @block.sync
        def _(sp):
            sp.dma_start(wsm[:, :], w_in).then_inc(s_in, 16)
            sp.dma_start(hT[:, :], u_feat).then_inc(s_in, 16)
            sp.dma_start(wqkv[:, 264:318], conv_w).then_inc(s_in, 16)
            sp.dma_start(wqkv[:, 0:264], w_scan_out).then_inc(s_in, 16)
            sp.dma_start(x[:, :, :], u_tok).then_inc(s_u, 16)
            sp.dma_start(cos_t[:, :], rope[0]).then_inc(s_u, 16)
            sp.dma_start(sin_t[:, :], rope[1]).then_inc(s_u, 16)
            sp.dma_start(wlay[:, :], w_layer[0]).then_inc(s_wl, 16)
            sp.dma_start(wo[:, :, :], w_o[0]).then_inc(s_wo, 16)
            for q in range(2):
                sp.dma_start(wexp[:, q, :], w_expert[q]).then_inc(s_we[q], 16)
            sp.wait_ge(s_x, 1)
            sp.dma_start(wqkv[:, :], w_attn[0]).then_inc(s_wa, 16)
            with sp.Fori(0, LAYERS) as layer:
                with sp.Fori(0, NKV) as g:
                    it = layer * NKV + g
                    sp.wait_ge(s_qlo, it + 1)
                    sp.dma_start(wqkv[:, :], w_attn[it + 1]).then_inc(s_wa, 16)
                    sp.wait_ge(s_ow, it * NC4 + NC4)
                    sp.dma_start(wo[:, :, :], w_o[it + 1]).then_inc(s_wo, 16)
                sp.wait_ge(s_rt, layer + 1)
                sp.dma_start(wlay[:, :], w_layer[layer + 1]).then_inc(s_wl, 16)
                with sp.Fori(0, NE // 2) as e2:
                    it = layer * (NE // 2) + e2
                    for q in range(2):
                        sp.wait_ge(s_dn, it * ITER_Y + (q + 1) * NC4)
                        sp.dma_start(wexp[:, q, :], w_expert[it * 2 + 2 + q]).then_inc(s_we[q], 16)
            for c in range(NC4):
                sp.wait_ge(s_fin, c + 1)
                sp.dma_start(out[:, 4 * c:4 * c + 4, :], x[:, 4 * c:4 * c + 4, :]).then_inc(s_out, 16)
            sp.wait_ge(s_out, 16 * NC4)
            sp.wait_ge(s_wa, 16 * (LAYERS * NKV + 1))
            sp.wait_ge(s_wo, 16 * (LAYERS * NKV + 1))
            sp.wait_ge(s_wl, 16 * (LAYERS + 1))
            for q in range(2):
                sp.wait_ge(s_we[q], 16 * (LAYERS * NE // 2 + 1))

        @block.gpsimd
        def _(pool):
            steps = [0]

            def fill(ap, value):
                steps[0] += 1
                pool.memset(ap, value).then_inc(s_cstep, 1)
                return steps[0]

            def keep(ap, pattern, base, ch, fill_value):
                pool.affine_select(out=ap, in_=ap, compare_op=ALU.is_ge, fill=fill_value, base=base,
                                   pattern=pattern, channel_multiplier=ch).then_inc(s_const, 1)

            fill(ident[:, :], 0.0)
            fill(ident_b[:, :], 0.0)
            fill(causal_b[:, :], 0.0)
            fill(mask4_b[:, :, :], 0.0)
            fill(tri[:, :, :], 1.0)
            fill(ones[:, :], 1.0)
            fill(neg_half[:, :], -0.5)
            fill(proj[:, :, 0:PAD], 0.0)
            fill(proj[:, :, PAD + SEQ:SEQP], 0.0)
            fill(c_pad[:, :, 0:1], 0.0)
            fill(c_pad[:, :, SEQ + 1:SEQ + 2], 0.0)
            pool.wait_ge(s_cstep, steps[0])
            for m in (ident, ident_b):
                pool.affine_select(out=m[:, :], in_=m[:, :], compare_op=ALU.not_equal, fill=1.0, base=0,
                                   pattern=[[-1, P]], channel_multiplier=1).then_inc(s_const, 1)
            pool.wait_ge(s_in, 64)
            pool.wait_ge(s_const, 2)
            for j in (3, 2):
                pool.tensor_tensor(diag[j], ident[:, :].unsqueeze(1).to_broadcast([P, TAPS, P]),
                                   cw[:, j, :].unsqueeze(2).to_broadcast([P, TAPS, P]), ALU.mult).then_inc(s_diag, 1)
            keep(causal_b[:, :], [[-1, P]], 0, 1, -1e9)
            keep(mask4_b[:, 0, :].rearrange("p (h t) -> p h t", h=SH), [[0, SH], [1, P]], -1, -1, -1e30)
            keep(mask4_b[:, 1, :].rearrange("p (h t) -> p h t", h=SH), [[0, SH], [-1, P]], -1, 1, -1e30)
            keep(tri[:, 0, :], [[1, P]], 0, -1, 0.0)
            keep(tri[:, 1, :], [[-1, P]], 0, 1, 0.0)
            keep(tri[:, 2, :], [[1, P]], -1, -1, 0.0)
            keep(tri[:, 3, :], [[-1, P]], -1, 1, 0.0)
            pool.iota(iota8[:, :], pattern=[[1, NE]], base=0, channel_multiplier=0,
                      allow_small_or_imprecise_dtypes=True).then_inc(s_const, 1)

            pool.wait_ge(s_coef, 2)
            pool.wait_ge(s_tre, NT)
            for v in range(NV):
                c, b, d, t = scan_unit(v)
                if v < NT:
                    pool.tensor_tensor(
                        y[:, t, :].rearrange("p (h e) -> p h e", h=SH),
                        xb[:, t, 0:DI].rearrange("p (h e) -> p h e", h=SH),
                        d_t[:, t, :].unsqueeze(2).to_broadcast([P, SH, SP]), ALU.mult).then_inc(s_yi, 1)
                if v >= 2:
                    pool.wait_ge(s_eg, v - 1)
                pool.tensor_tensor(
                    a_u[:, v % 2], tri[:, 2 + d, :].unsqueeze(1).to_broadcast([P, SH, P]),
                    a_dt[:, t, d * SH:(d + 1) * SH].unsqueeze(2).to_broadcast([P, SH, P]), ALU.mult)\
                    .then_inc(s_au, 1)
                if v >= 2:
                    pool.wait_ge(s_y, v - 1)
                pool.tensor_tensor(
                    xw[:, v % 2, :].rearrange("p (h e) -> p h e", h=SH),
                    xb[:, t, 0:DI].rearrange("p (h e) -> p h e", h=SH),
                    exp_w[:, t, d * SH:(d + 1) * SH].unsqueeze(2).to_broadcast([P, SH, SP]), ALU.mult)\
                    .then_inc(s_xw, 1)
                if c > 0:
                    rows, dh = slice(d * SN, (d + 1) * SN), slice(d * SH, (d + 1) * SH)
                    pool.wait_ge(s_yr, v - 3)
                    pool.wait_ge(s_xw, v + 1)
                    pool.tensor_tensor(aged[rows, v % 4, :].rearrange("p (h e) -> p h e", h=SH),
                                       state[rows, b, :].rearrange("p (h e) -> p h e", h=SH),
                                       exp_t[rows, t, dh].unsqueeze(2).to_broadcast([SN, SH, SP]), ALU.mult)\
                        .then_inc(s_aged, 1)
                    pool.wait_ge(s_aged, v - 3)

            def root(n, tiles=slice(0, NT)):
                pool.wait_ge(s_var, n)
                pool.tensor_tensor(rstd[:, tiles], var[:, tiles], neg_half[:, tiles], ALU.pow).then_inc(s_pow, 1)

            def norm_roots(n):
                for c in range(NC4):
                    root(N_VAR + n * NC4 + c + 1, slice(4 * c, 4 * c + 4))

            root(1)
            root(2)
            norm_roots(0)
            with pool.Fori(0, LAYERS) as layer:

                def item(half, i, shared=False):
                    pool.wait_ge(s_qc, half * ROPES + i + 1)
                    if i >= 1:
                        pool.wait_ge(s_rs, half * ROPES + i)
                    blocks = pool_blocks(i) if shared else 4
                    for n in range(blocks):
                        if n:
                            pool.wait_ge(s_rp, (half * ROPES + i) * 4 + n * 4 // blocks)
                        rotated(pool, i, n, q_sb[:, i % 2, :]).then_inc(s_rp, 4 // blocks)
                    pool.wait_ge(s_rp, (half * ROPES + i) * 4 + 4)
                    pool.wait_ge(s_rc, half * ROPES + i + 1)
                    pool.tensor_tensor(ra[:, i % 2, :], ra[:, i % 2, :], rb[:, i % 2, :], ALU.add)\
                        .then_inc(s_rs, 1)

                def group_v(it, g, b):
                    half = slice(b * TB, (b + 1) * TB)
                    pool.sem_inc(s_alone, 1)
                    pool.tensor_copy(v_g[:, half, :], v_all[:, half, bass.ts(g, HD)]).then_inc(s_vg, 1)
                    pool.wait_ge(s_vg, it * 2 + b + 1)
                    pool.sem_inc(s_alone, 1)

                def group(it, g, last):
                    for i in range(ROPES):
                        item(it * 2 + 1, i)
                    pool.wait_ge(s_pv, it * NPAIR + 1)
                    group_v(it, g, 1)
                    if not last:
                        for i in range(ROPES):
                            item(it * 2 + 2, i)
                            if i == 2:
                                pool.wait_ge(s_pv, it * NPAIR + NPAIR // 2)
                                group_v(it + 1, g + 1, 0)

                pool.wait_ge(s_pow, N_VAR + (layer * 2 + 1) * NC4)
                for i in range(ROPES):
                    item(layer * NKV * 2, i, shared=True)
                pool.wait_ge(s_ve, layer * (NT // 2) + NT // 2)
                group_v(layer * NKV, 0, 0)
                with pool.Fori(0, NKV - 1) as g:
                    group(layer * NKV + g, g, False)
                group(layer * NKV + NKV - 1, NKV - 1, True)
                norm_roots(layer * 2 + 1)
                norm_roots(layer * 2 + 2)
            root(N_VAR + (2 * LAYERS + 1) * NC4 + 1)

        @block.scalar
        def _(act):
            def copy_proj(b, j):
                for c in range(2):
                    i = (b * 4 + CONV_ORDER.index(j)) * 2 + c
                    act.wait_ge(s_pj, i + 1)
                    if b == 1 and c == 0:
                        act.wait_ge(*((s_cpe, 1) if j == 3 else (s_conv, j + 1)))
                    act.activation(proj[:, j, PAD + c * CW:PAD + (c + 1) * CW], bank(i % 4), ACT.Copy)\
                        .then_inc(s_pje, 1)

            def silu(b, j):
                if (b, j) in CONV_PE:
                    act.wait_ge(s_cpe, CONV_PE.index((b, j)) + 1)
                    dst = c_pad[:, b, 1:SEQ + 1] if j == 3 else xbT[:, j, b * SEQ:(b + 1) * SEQ]
                    for c in range(2):
                        ins = act.activation(dst[:, c * CW:(c + 1) * CW], bank(4 + c), ACT.Silu, bias=cb[:, j:j + 1])
                else:
                    act.wait_ge(s_conv, b * 3 + j + 1)
                    dst = xbT[:, j, b * SEQ:(b + 1) * SEQ]
                    ins = act.activation(dst, dst, ACT.Silu)
                ins.then_inc(s_silu, 1)

            def copy_xb(t):
                act.wait_ge(s_tr, t + 1)
                act.activation(xb[:, t, :], bank(t % 4)[:, 0:DI + P], ACT.Copy).then_inc(s_tre, 1)

            for j in CONV_ORDER:
                copy_proj(0, j)
            act.activation(exp_a[:, :], hc[:, 8:16], ACT.Exp).then_inc(s_as, 1)
            act.wait_ge(s_vs, 3)
            act.activation(dt_e[:, :, :], dt_u[:, :, :], ACT.Exp, scale=-1.0).then_inc(s_as, 1)
            copy_proj(1, 0)
            silu(0, 0)
            act.wait_ge(s_vs, 4)
            act.activation(dt_l[:, :, :], dt_u[:, :, :], ACT.Ln).then_inc(s_as, 1)
            copy_proj(1, 3)
            silu(0, 3)
            copy_proj(1, 1)
            silu(0, 1)
            copy_proj(1, 2)
            silu(0, 2)
            act.wait_ge(s_cum, 1)
            act.activation(exp_t[:, :, :], bank(7)[:, 2 * P:3 * P].rearrange("p (t h) -> p t h", h=8), ACT.Exp)\
                .then_inc(s_as, 1)
            act.wait_ge(s_vs, 14)
            act.activation(exp_e[:, :, :], exp_e[:, :, :], ACT.Exp).then_inc(s_as, 1)
            for t in range(TB):
                copy_xb(t)
            silu(1, 3)
            silu(1, 0)
            act.wait_ge(s_vs, 15)
            act.activation(exp_w[:, :, :], exp_w[:, :, :], ACT.Exp).then_inc(s_as, 1)
            silu(1, 1)
            silu(1, 2)
            for t in range(TB, NT):
                copy_xb(t)
            act.wait_ge(s_vs, 13)
            for v in range(NV):
                c, b, d, t = scan_unit(v)
                act.wait_ge(s_eg, v + 1)
                if v >= 2:
                    act.wait_ge(s_mix, v - 1)
                for h in range(SH):
                    ins = act.activation(dec[:, v % 2, h, :], bank(v % 2)[:, h * P:(h + 1) * P], ACT.Exp,
                                         bias=ncum[:, t, d * SH + h:d * SH + h + 1])
                ins.then_inc(s_dec, 1)
            for i in range(NT // 2):
                act.wait_ge(s_z, i + 1)
                act.activation(xb[:, 2 * i:2 * i + 2, 0:DI],
                               bank(i % 4).rearrange("p (t d) -> p t d", t=2), ACT.Silu).then_inc(s_zs, 1)
            for i in range(NT // 2):
                act.wait_ge(s_unt, i + 1)
                src = bank(4 + i % 2).rearrange("p (t j n) -> p j t n", t=2, j=2)
                for j in range(2):
                    ins = act.activation(
                        unT[:, j, i * 2 * P:(i + 1) * 2 * P].rearrange("p (t n) -> p t n", t=2),
                        src[:, j], ACT.Copy, scale=rmsw[:, j:j + 1])
                ins.then_inc(s_une, 1)

            act.wait_ge(s_x, 2)
            act.activation(x1[:, :, :], x[:, :, :], ACT.Copy).then_inc(s_x1, 1)

            def norm_scale(n, c):
                act.wait_ge(s_pow, N_VAR + n * NC4 + c + 1)
                for t in range(4 * c, 4 * c + 4):
                    ins = act.activation(hn[:, t, :], x[:, t, :], ACT.Copy, scale=rstd[:, t:t + 1])
                ins.then_inc(s_hn, 1)

            def norm_out(n, w, c, src):
                act.wait_ge(s_nt, n * NC4 + c + 1)
                for to, done in ((hT, s_ht), (h_hi, s_hh)):
                    act.activation(to[:, c * CW:(c + 1) * CW], src, ACT.Copy, scale=wlay[:, w:w + 1])\
                        .then_inc(done, 1)

            def qk_high(it):
                act.wait_ge(s_wa, it * 16 + 16)
                act.activation(wqk_hi[:, :], wqkv[:, :], ACT.Copy).then_inc(s_qhi, 1)

            def expert_high(it, e):
                act.wait_ge(s_we[e % 2], (it + e // 2 + 1) * 16)
                act.activation(wg_hi[:, e % 2, :], wexp[:, e % 2, 0:2 * FF], ACT.Copy).then_inc(s_ghi, 1)

            qk_high(0)

            with act.Fori(0, LAYERS) as layer:
                act.wait_ge(s_wl, layer * 16 + 16)

                def copy_q(half, i, src):
                    act.wait_ge(s_qk, half * ROPES + i + 1)
                    if i >= 2:
                        act.wait_ge(s_rs, half * ROPES + i - 1)
                    act.activation(q_sb[:, i % 2, :], src, ACT.Copy).then_inc(s_qc, 1)

                def high(b, half, i):
                    c, what = ITEMS[i]
                    cols = slice(b * SEQ + c * CW, b * SEQ + (c + 1) * CW)
                    act.wait_ge(s_rs, half * ROPES + i + 1)
                    if what == 0:
                        act.activation(k_hi[:, cols], ra[:, i % 2, :], ACT.Copy).then_inc(s_hi, 1)
                    else:
                        h = 2 * (what - 1)
                        act.activation(qs[0:HD, h, cols], ra[0:HD, i % 2, :], ACT.Copy, scale=HD ** -0.5)
                        act.activation(qs[HD:P, h + 1, cols], ra[HD:P, i % 2, :], ACT.Copy,
                                       scale=HD ** -0.5).then_inc(s_hi, 1)

                def steps(it, s0, s1, last=False):
                    for s in range(s0, s1):
                        j2 = s - 1 - LAG_T - LAG_PV
                        if j2 >= 0 and j2 % 2 == 0 and not (last and j2 >= NU):
                            j = j2 // 2
                            b, p, qt, _ = UNITS[j2 % NU]
                            col = (b * TB + qt) * P
                            act.wait_ge(s_pv, it * NPAIR + j + 1)
                            act.activation(o_t[:, p, col:col + P], ps_o[:, 0, j % 4 * P:(j % 4 + 1) * P],
                                           ACT.Copy).then_inc(s_oe, 1)
                        u = s - LAG_T
                        if u >= 0 and not (last and u >= NU):
                            for part in range(2 if chunk(u, 1) else 1):
                                n = chunk(u, part)
                                k0, k1 = part * 4, min(UNITS[u % NU][2] + 1, part * 4 + 4)
                                act.wait_ge(s_t, it * NCH + n + 1)
                                if u >= R_PT:
                                    act.wait_ge(s_pv, it * NPAIR + (u - R_PT) // 2 + 1)
                                act.activation(prob_t[:, u % R_PT, k0:k1, :],
                                               ps_t[:, n % 2, 0:(k1 - k0) * P].rearrange("p (k n) -> p k n", n=P),
                                               ACT.Copy).then_inc(s_ev, 1)
                        if not (last and s >= NU):
                            act.wait_ge(s_m, it * NU + s + 1)
                            if buffer_before(s) is not None:
                                act.wait_ge(s_t, it * NCH + last_chunk(buffer_before(s)) + 1)
                            u = s % NU
                            w = (UNITS[u][2] + 1) * P
                            act.activation(prob[:, u % R_PROB, 0:w], ps_s[:, s % 2, 0:w], ACT.Exp,
                                           bias=negmax[:, u:u + 1], accum_out=rowsum[:, u:u + 1])\
                                .then_inc(s_e, 1)
                        if s == SPLIT:
                            act.wait_ge(s_qk, (it * 2 + 2) * ROPES)
                            qk_high(it + 1)
                        if s0 == 0 and s in (2, 4):
                            high(0, layer * NKV * 2, FIRST + s // 2 - 1)
                        if last and s == NU + 4:
                            act.wait_ge(s_s, (layer + 1) * NKV * NU)
                            expert_high(layer * (NE // 2), 0)
                        got = side(s - 1, last)
                        if got and got[0] == "tr":
                            norm_out(layer * 2 + 1, 1, got[1], ps_o[:, 1, :])
                        if got and got[0] in ("b0", "b1"):
                            copy_q(half_of(it, got), got[1], ps_o[:, 1, :])
                        got = side(s - LAG_HI, last)
                        if got and got[0] in ("b0", "b1"):
                            high(got[0] == "b1", half_of(it, got), got[1])

                def copy_v(v):
                    act.wait_ge(s_v, layer * (NT // 2) + v + 1)
                    act.activation(v_all[:, 2 * v:2 * v + 2, :],
                                   bank(v % 4).rearrange("p (t n) -> p t n", t=2), ACT.Copy).then_inc(s_ve, 1)

                for what in "s0 s1 n0 n1 s2 c0 s3 c1 n2 h0 n3 c2 h1 v0 c3 h2 v1 v2 c4 v3 h3 v4 c5 v5 v6 v7".split():
                    i = int(what[1])
                    if what[0] == "s":
                        norm_scale(layer * 2, i)
                    if what[0] == "n":
                        norm_out(layer * 2, 0, i, bank(i))
                    if what[0] == "c":
                        copy_q(layer * NKV * 2, i, bank(4 + i % 4))
                    if what[0] == "h":
                        high(0, layer * NKV * 2, i)
                    if what[0] == "v":
                        copy_v(i)
                steps(layer * NKV, 0, HEAD)
                with act.Fori(0, NKV - 1) as g:
                    steps(layer * NKV + g, HEAD, NU + HEAD)
                steps(layer * NKV + NKV - 1, HEAD, NU + HEAD, last=True)
                def second_norm():
                    for c in range(2, NC4):
                        norm_out(layer * 2 + 1, 1, c, bank(2 + c))


                def items(it, m0, m1, last=False):
                    for m in range(m0, m1):
                        if last and m >= ITER_GU:
                            continue
                        act.wait_ge(s_gu, it * ITER_GU + m + 1)
                        if m >= 2:
                            act.wait_ge(s_a, it * ITER_GU + m - 1)
                        act.activation(sg[:, m % 2, :], bank(2 * M_BANKS[m % ITER_GU]), ACT.Silu).then_inc(s_sg, 1)
                        if m == 1:
                            second_norm()
                        e = split_at(m, last)
                        if e:
                            expert_high(it, e)

                items(layer * (NE // 2), 0, 2)
                act.wait_ge(s_rv, layer * N_RV + 1)
                act.activation(pe_[:, :, :], pe_[:, :, :], ACT.Exp).then_inc(s_re, 1)
                items(layer * (NE // 2), 2, HEAD_M)
                with act.Fori(0, NE // 2 - 1) as e2:
                    items(layer * (NE // 2) + e2, HEAD_M, HEAD_M + ITER_GU)
                items(layer * (NE // 2) + NE // 2 - 1, HEAD_M, LAST_M, last=True)

        @block.vector
        def _(dve):
            vs = [0]

            def step(ins):
                vs[0] += 1
                ins.then_inc(s_vs, 1)
                dve.wait_ge(s_vs, vs[0])

            dve.wait_ge(s_in, 64)
            dve.wait_ge(s_cstep, 11)
            cstep = [0]

            def convolve(b, j):
                dve.wait_ge(s_pje, (b * 4 + CONV_ORDER.index(j)) * 2 + 2)
                dst = xbT[:, j, b * SEQ:(b + 1) * SEQ]
                dve.tensor_scalar(dst, proj[:, j, 0:SEQ], cw[:, j, 0:1], cb[:, j:j + 1], ALU.mult, ALU.add)\
                    .then_inc(s_vn, 1)
                for k in range(1, TAPS):
                    cstep[0] += 1
                    dve.wait_ge(s_vn, cstep[0])
                    ins = dve.scalar_tensor_tensor(out=dst, in0=proj[:, j, k:k + SEQ], scalar=cw[:, j, k:k + 1],
                                                   in1=dst, op0=ALU.mult, op1=ALU.add)
                    ins.then_inc(s_vn if k < TAPS - 1 else s_conv, 1)

            convolve(0, 0)
            dve.wait_ge(s_dtp, 1)
            step(dve.tensor_tensor(dtr[:, :, :], bank(7)[:, P:2 * P].rearrange("p (t h) -> p t h", h=8),
                                   hc[:, 0:8].unsqueeze(1).to_broadcast([P, NT, 8]), ALU.add))
            step(dve.tensor_scalar(dt_s[:, :, :], dtr[:, :, :], 0.0, None, ALU.max))
            step(dve.scalar_tensor_tensor(out=dt_u[:, :, :], in0=dtr[:, :, :], scalar=-1.0, in1=dtr[:, :, :],
                                          op0=ALU.mult, op1=ALU.max))
            convolve(0, 1)
            dve.wait_ge(s_as, 2)
            step(dve.tensor_scalar(dt_u[:, :, :], dt_e[:, :, :], 1.0, None, ALU.add))
            step(dve.tensor_scalar(dt_z[:, :, :], dt_u[:, :, :], 1.0, None, ALU.is_equal))
            step(dve.scalar_tensor_tensor(out=dtr[:, :, :], in0=dt_u[:, :, :], scalar=-1.0, in1=dt_z[:, :, :],
                                          op0=ALU.add, op1=ALU.add))
            step(dve.reciprocal(dtr[:, :, :], dtr[:, :, :]))
            convolve(0, 2)
            dve.wait_ge(s_as, 3)
            step(dve.tensor_tensor(dtr[:, :, :], dtr[:, :, :], dt_l[:, :, :], ALU.mult))
            step(dve.tensor_tensor(dtr[:, :, :], dtr[:, :, :], dt_z[:, :, :], ALU.add))
            step(dve.tensor_tensor(dtr[:, :, :], dtr[:, :, :], dt_e[:, :, :], ALU.mult))
            step(dve.tensor_tensor(dt_s[:, :, :], dt_s[:, :, :], dtr[:, :, :], ALU.add))
            step(dve.scalar_tensor_tensor(out=a_dt[:, :, :], in0=dt_s[:, :, :], scalar=-1.0,
                                          in1=exp_a[:, :].unsqueeze(1).to_broadcast([P, NT, 8]),
                                          op0=ALU.mult, op1=ALU.mult))
            convolve(1, 0)
            dve.wait_ge(s_cum, 1)
            step(dve.tensor_scalar(ncum[:, :, :], bank(6)[:, 0:P].rearrange("p (t h) -> p t h", h=8),
                                   -1.0, None, ALU.mult))
            step(dve.scalar_tensor_tensor(out=exp_e[:, :, :], in0=ncum[:, :, :], scalar=-1.0, in1=a_dt[:, :, :],
                                          op0=ALU.mult, op1=ALU.subtract))
            dve.wait_ge(s_as, 4)
            step(dve.tensor_tensor(exp_w[:, :, :], bank(7)[:, 2 * P:3 * P].rearrange("p (t h) -> p t h", h=8),
                                   ncum[:, :, :], ALU.add))
            convolve(1, 1)
            N_CONV = cstep[0]
            dve.wait_ge(s_as, 6)
            dve.tensor_tensor(exp_w[:, :, :], exp_w[:, :, :], dt_s[:, :, :], ALU.mult).then_inc(s_coef, 1)
            dve.wait_ge(s_dd, 1)
            dve.tensor_tensor(d_t[:, :, :], bank(7)[:, 0:NT * SH].rearrange("p (t h) -> p t h", h=SH),
                              hc[:, 16:20].unsqueeze(1).to_broadcast([P, NT, SH]), ALU.add).then_inc(s_coef, 1)

            def combine(v):
                c, b, d, t = scan_unit(v)
                rows = slice(d * SN, (d + 1) * SN)
                dh = slice(d * SH, (d + 1) * SH)
                if v < NT:
                    dve.wait_ge(s_yi, v + 1)
                dve.wait_ge(s_y, v + 1)
                if c > 0:
                    vs[0] += 2
                    dve.tensor_tensor(tmp[:, :].rearrange("p (h e) -> p h e", h=SH),
                                      bank(4 + v % 2)[:, DI:2 * DI].rearrange("p (h e) -> p h e", h=SH),
                                      exp_e[:, t, dh].unsqueeze(2).to_broadcast([P, SH, SP]), ALU.mult)\
                        .then_inc(s_vs, 1)
                    dve.wait_ge(s_aged, v - 3)
                    dve.tensor_tensor(state[rows, b, :], aged[rows, v % 4, :], bank(6 + v % 2)[rows, 0:DI], ALU.add)\
                        .then_inc(s_vs, 1)
                    dve.wait_ge(s_vs, vs[0] - 1)
                    step(dve.tensor_tensor(tmp[:, :], tmp[:, :], bank(4 + v % 2)[:, 0:DI], ALU.add))
                    dve.tensor_tensor(y[:, t, :], y[:, t, :], tmp[:, :], ALU.add).then_inc(s_yr, 1)
                else:
                    dve.tensor_copy(state[rows, b, :], bank(6 + v % 2)[rows, 0:DI])
                    dve.tensor_tensor(y[:, t, :], y[:, t, :], bank(4 + v % 2)[:, 0:DI], ALU.add)\
                        .then_inc(s_yr, 1)
                dve.wait_ge(s_yr, v + 1)

            for v in range(NV + 1):
                if v < NV:
                    c, b, d, t = scan_unit(v)
                    dve.wait_ge(s_dec, v + 1)
                    if v >= 2:
                        dve.wait_ge(s_y, v - 1)
                    for h in range(SH):
                        ins = dve.scalar_tensor_tensor(
                            out=mix[:, v % 2, h, :], in0=dec[:, v % 2, h, :],
                            scalar=dt_s[:, t, d * SH + h:d * SH + h + 1], in1=bank(2 + v % 2)[:, 0:P],
                            op0=ALU.mult, op1=ALU.mult)
                    ins.then_inc(s_mix, 1)
                if v >= 1:
                    combine(v - 1)

            for t in range(NT):
                ins = dve.tensor_tensor_reduce(out=flat[:, t * DI:(t + 1) * DI], in0=y[:, t, :], in1=y[:, t, :],
                                               scale=1.0, scalar=0.0, op0=ALU.mult, op1=ALU.add,
                                               accum_out=ssq[:, t:t + 1])
            step(ins)
            dve.tensor_scalar(var[:, :], ssq[:, :], 1.0 / DI, RMS_EPS, ALU.mult, ALU.add).then_inc(s_var, 1)
            dve.wait_ge(s_pow, 1)
            for t in range(NT):
                dve.wait_ge(s_zs, t // 2 + 1)
                dve.scalar_tensor_tensor(out=y[:, t, :], in0=y[:, t, :], scalar=rstd[:, t:t + 1],
                                         in1=xb[:, t, 0:DI], op0=ALU.mult, op1=ALU.mult).then_inc(s_un, 1)
            for c in range(NC4):
                dve.wait_ge(s_so, c + 1)
                if c == 0:
                    dve.wait_ge(s_u, 48)
                ins = dve.tensor_tensor(x[:, 4 * c:4 * c + 4, :], bank(c).rearrange("p (t d) -> p t d", t=4),
                                        x[:, 4 * c:4 * c + 4, :], ALU.add)
            ins.then_inc(s_x, 1)
            dve.wait_ge(s_x, 1)

            def moments(chain):
                for t in range(NT):
                    chain(dve.bn_stats(bn[:, t % 2, :], x[:, t, :]))
                    ins = dve.bn_aggr(mean_var[:, t, :], bn[:, t % 2, :])
                chain(ins)
                dve.tensor_scalar(var[:, :], mean_var[:, :, 1], EPS, None, ALU.add).then_inc(s_var, 1)

            moments(step)
            dve.wait_ge(s_pow, 2)
            for t in range(NT):
                ins = dve.tensor_scalar(x[:, t, :], x[:, t, :], mean_var[:, t, 0:1], rstd[:, t:t + 1],
                                        ALU.subtract, ALU.mult)
            ins.then_inc(s_x, 1)
            dve.wait_ge(s_x, 2)

            def qk_low(it):
                dve.wait_ge(s_qhi, it + 1)
                dve.tensor_tensor(wqk_lo[:, :], wqkv[:, :], wqk_hi[:, :].bitcast(F32), ALU.subtract)\
                    .then_inc(s_qlo, 1)

            def expert_low(it, e):
                dve.wait_ge(s_ghi, it * 2 + e + 1)
                dve.tensor_tensor(wg_lo[:, e % 2, :], wexp[:, e % 2, 0:2 * FF], wg_hi[:, e % 2, :].bitcast(F32),
                                  ALU.subtract).then_inc(s_glo, 1)

            def norm_low(n, c):
                cols = slice(c * CW, (c + 1) * CW)
                dve.wait_ge(s_hh, n * NC4 + c + 1)
                dve.tensor_tensor(h_lo[:, cols], hT[:, cols], h_hi[:, cols].bitcast(F32), ALU.subtract)\
                    .then_inc(s_hl, 1)

            qk_low(0)

            def norm_squares(n, c, clip=True):
                tiles = slice(4 * c, 4 * c + 4)
                if clip:
                    dve.tensor_scalar(x[:, tiles, :], x[:, tiles, :], -CLIP, CLIP, ALU.max, ALU.min)\
                        .then_inc(s_clip, 1)
                    dve.wait_ge(s_clip, (n - 1) * NC4 + c + 1)
                for t in range(4 * c, 4 * c + 4):
                    ins = dve.tensor_tensor_reduce(out=hn[:, t, :], in0=x[:, t, :], in1=x[:, t, :], scale=1.0,
                                                   scalar=0.0, op0=ALU.mult, op1=ALU.add, accum_out=ssq[:, t:t + 1])
                ins.then_inc(s_vn, 1)
                dve.wait_ge(s_vn, N_CONV + n * NC4 + c + 1)
                dve.tensor_scalar(var[:, tiles], ssq[:, tiles], 1.0 / DM, EPS, ALU.mult, ALU.add).then_inc(s_var, 1)

            def norm_scale(n, c):
                dve.wait_ge(s_pow, N_VAR + n * NC4 + c + 1)
                for t in range(4 * c, 4 * c + 4):
                    ins = dve.tensor_scalar(hn[:, t, :], x[:, t, :], rstd[:, t:t + 1], None, ALU.mult)
                ins.then_inc(s_hn, 1)

            for c in range(NC4):
                norm_squares(0, c, clip=False)
            with dve.Fori(0, LAYERS) as layer:

                def multiply(half, i, shared=False):
                    c = ITEMS[i][0]
                    src = q_sb[:, i % 2, :]
                    dve.wait_ge(s_qc, half * ROPES + i + 1)
                    if i >= 2:
                        dve.wait_ge(s_lo, half * ROPES + i - 1)
                    ins = dve.tensor_tensor(ra[:, i % 2, :], src, cos_t[:, c * CW:(c + 1) * CW], ALU.mult)
                    if shared:
                        for n in range(pool_blocks(i), 4):
                            ins = rotated(dve, i, n, src)
                    ins.then_inc(s_rc, 1)

                def low(b, half, i):
                    c, what = ITEMS[i]
                    cols = slice(b * SEQ + c * CW, b * SEQ + (c + 1) * CW)
                    dve.wait_ge(s_hi, half * ROPES + i + 1)
                    if what == 0:
                        dve.tensor_tensor(k_lo[:, cols], ra[:, i % 2, :], k_hi[:, cols].bitcast(F32),
                                          ALU.subtract).then_inc(s_lo, 1)
                    else:
                        h = 2 * (what - 1)
                        dve.scalar_tensor_tensor(
                            out=qs[HD:P, h, cols], in0=ra[0:HD, i % 2, :], scalar=HD ** -0.5,
                            in1=qs[0:HD, h, cols].bitcast(F32), op0=ALU.mult, op1=ALU.subtract)
                        dve.scalar_tensor_tensor(
                            out=qs[0:HD, h + 1, cols], in0=ra[HD:P, i % 2, :], scalar=HD ** -0.5,
                            in1=qs[HD:P, h + 1, cols].bitcast(F32), op0=ALU.mult, op1=ALU.subtract)\
                            .then_inc(s_lo, 1)

                def add_heads(it, c, src):
                    dve.wait_ge(s_ow, it * NC4 + c + 1)
                    dve.tensor_tensor(x[:, 4 * c:4 * c + 4, :], src.rearrange("p (t d) -> p t d", t=4),
                                      x[:, 4 * c:4 * c + 4, :], ALU.add).then_inc(s_xa, 1)

                def steps(it, s0, s1, last=False):
                    for s in range(s0, s1):
                        if not (last and s >= NU):
                            u = s % NU
                            w = (UNITS[u][2] + 1) * P
                            dve.wait_ge(s_s, it * NU + s + 1)
                            dve.tensor_reduce(negmax[:, u:u + 1], ps_s[:, s % 2, 0:w], AX.X, ALU.max,
                                              negate=True).then_inc(s_m, 1)
                        u = s - LAG_N
                        if u >= 0 and not (last and u >= NU):
                            dve.wait_ge(s_e, it * NU + u + 1)
                            c = u % NU
                            dve.reciprocal(rrow[:, c:c + 1], rowsum[:, c:c + 1]).then_inc(s_r, 1)
                            dve.wait_ge(s_r, it * NU + u + 1)
                            ap = prob[:, c % R_PROB, 0:(UNITS[c][2] + 1) * P]
                            dve.tensor_scalar(ap, ap, rrow[:, c:c + 1], None, ALU.mult).then_inc(s_p, 1)
                        got = side(s - 1, last)
                        if got and got[0] == "wo":
                            add_heads(it + got[2], got[1], ps_o[:, 1, :])
                        got = side(s - LAG_COS, last)
                        if got and got[0] in ("b0", "b1"):
                            multiply(half_of(it, got), got[1])
                        got = side(s - LAG_LO, last)
                        if got and got[0] in ("b0", "b1"):
                            low(got[0] == "b1", half_of(it, got), got[1])
                        if s0 == 0:
                            for what in {0: "m4 n2", 1: "m5", 3: "l4", 4: "n3", 5: "l5"}.get(s, "").split():
                                i = int(what[1])
                                if what[0] == "m":
                                    multiply(layer * NKV * 2, i, shared=True)
                                if what[0] == "n":
                                    norm_low(layer * 2, i)
                                if what[0] == "l":
                                    low(0, layer * NKV * 2, i)
                        if last and s == NU + 5:
                            expert_low(layer * (NE // 2), 0)
                        kind, c = NORM_STEPS.get(s, (None, 0)) if last else (None, 0)
                        if kind == "clip":
                            dve.wait_ge(s_xa, it * NC4 + c + 1)
                            norm_squares(layer * 2 + 1, c)
                        if kind == "scale":
                            norm_scale(layer * 2 + 1, c)
                        if kind == "low":
                            norm_low(layer * 2 + 1, c)
                        if s == SPLIT:
                            qk_low(it + 1)

                for what in "n0 n1 m0 m1 l0 m2 l1 m3 l2 l3".split():
                    i = int(what[1])
                    if what[0] == "n":
                        norm_low(layer * 2, i)
                    if what[0] == "m":
                        multiply(layer * NKV * 2, i, shared=True)
                    if what[0] == "l":
                        low(0, layer * NKV * 2, i)
                steps(layer * NKV, 0, HEAD)
                with dve.Fori(0, NKV - 1) as g:
                    steps(layer * NKV + g, HEAD, NU + HEAD)
                steps(layer * NKV + NKV - 1, HEAD, NU + HEAD, last=True)

                def items(it, e2, m0, m1, last=False):
                    for m in range(m0, m1):
                        if not (last and m >= ITER_GU):
                            c, fh = m // 2, m % 2
                            dve.wait_ge(s_sg, it * ITER_GU + m + 1)
                            if c >= 2:
                                dve.wait_ge(s_dn, it * ITER_Y + c - 1)
                            dve.tensor_tensor(a_t[:, c % 2, fh, :], sg[:, m % 2, :],
                                              bank(2 * M_BANKS[m % ITER_GU] + 1), ALU.mult).then_inc(s_a, 1)
                            e = split_at(m, last)
                            if e:
                                expert_low(it, e)
                        if m % 2 == 1 and m >= 3:
                            yi = (m - 3) // 2
                            e = e2 * 2 + yi // NC4
                            dve.wait_ge(s_dn, it * ITER_Y + yi + 1)
                            for t4 in range(4):
                                t = yi % NC4 * 4 + t4
                                ins = dve.scalar_tensor_tensor(
                                    out=x[:, t, :], in0=ps_o[:, yi % 2, t4 * P:(t4 + 1) * P],
                                    scalar=comb[:, t, bass.ds(e, 1)], in1=x[:, t, :], op0=ALU.mult, op1=ALU.add)
                            ins.then_inc(s_ya, 1)
                            if last and yi >= NC4:
                                dve.wait_ge(s_ya, it * ITER_Y + yi + 1)
                                norm_squares(layer * 2 + 2, yi - NC4)

                for c in range(2, NC4):
                    norm_scale(layer * 2 + 1, c)
                rv = [0]

                def rstep(ins, alone=False):
                    rv[0] += 1
                    ins.then_inc(s_rv, 1)
                    dve.wait_ge(s_rv, layer * N_RV + rv[0])
                    if alone:
                        dve.sem_inc(s_alone, 1)

                logits = ps_o[:, 0, 0:NT * NE].rearrange("p (t e) -> p t e", e=NE)
                dve.wait_ge(s_rt, layer + 1)
                dve.tensor_reduce(r1[:, :], logits, AX.X, ALU.max).then_inc(s_rmax, 1)
                dve.wait_ge(s_rmax, layer + 1)
                rstep(dve.tensor_tensor(pe_[:, :, :], logits, r1[:, :].unsqueeze(2).to_broadcast([P, NT, NE]),
                                        ALU.subtract))
                for c in range(2, NC4):
                    norm_low(layer * 2 + 1, c)
                items(layer * (NE // 2), 0, 0, 2)
                dve.wait_ge(s_re, layer + 1)
                rstep(dve.tensor_reduce(r2[:, :], pe_[:, :, :], AX.X, ALU.add))
                rstep(dve.reciprocal(r2[:, :], r2[:, :]))
                rstep(dve.tensor_tensor(pr[:, :, :], pe_[:, :, :], r2[:, :].unsqueeze(2).to_broadcast([P, NT, NE]),
                                        ALU.mult), alone=True)
                for t in range(NT):
                    ins = dve.max(top[:, t, :], pr[:, t, :])
                rstep(ins, alone=True)
                items(layer * (NE // 2), 0, 2, 3)
                for t in range(NT):
                    ins = dve.max_index(topi[:, t, :], top[:, t, :], pr[:, t, :])
                rstep(ins)
                rstep(dve.tensor_copy(topif[:, :, :], topi[:, :, :]))
                rstep(dve.tensor_tensor(r1[:, :], top[:, :, 0], top[:, :, 1], ALU.add))
                rstep(dve.reciprocal(r1[:, :], r1[:, :]))
                rstep(dve.tensor_tensor(wtop[:, :, :], top[:, :, 0:2], r1[:, :].unsqueeze(2).to_broadcast([P, NT, 2]),
                                        ALU.mult))
                iob = iota8[:, :].unsqueeze(1).to_broadcast([P, NT, NE])
                dve.tensor_tensor(comb[:, :, :], iob, topif[:, :, 0:1].to_broadcast([P, NT, NE]), ALU.is_equal)
                rstep(dve.tensor_tensor(pr[:, :, :], iob, topif[:, :, 1:2].to_broadcast([P, NT, NE]), ALU.is_equal))
                dve.tensor_tensor(comb[:, :, :], comb[:, :, :], wtop[:, :, 0:1].to_broadcast([P, NT, NE]), ALU.mult)
                rstep(dve.tensor_tensor(pr[:, :, :], pr[:, :, :], wtop[:, :, 1:2].to_broadcast([P, NT, NE]), ALU.mult))
                dve.tensor_tensor(comb[:, :, :], comb[:, :, :], pr[:, :, :], ALU.add).then_inc(s_rv, 1)
                assert rv[0] + 1 == N_RV

                dve.wait_ge(s_rv, layer * N_RV + N_RV)
                items(layer * (NE // 2), 0, 3, HEAD_M)
                with dve.Fori(0, NE // 2 - 1) as e2:
                    items(layer * (NE // 2) + e2, e2, HEAD_M, HEAD_M + ITER_GU)
                items(layer * (NE // 2) + NE // 2 - 1, NE // 2 - 1, HEAD_M, LAST_M, last=True)
            dve.wait_ge(s_x1, 1)
            dve.wait_ge(s_pow, N_VAR + (2 * LAYERS + 1) * NC4)
            step(dve.tensor_tensor(x[:, :, :], x[:, :, :], x1[:, :, :], ALU.add))
            moments(step)
            dve.wait_ge(s_pow, N_VAR + (2 * LAYERS + 1) * NC4 + 1)
            for t in range(NT):
                ins = dve.tensor_scalar(x[:, t, :], x[:, t, :], mean_var[:, t, 0:1], rstd[:, t:t + 1],
                                        ALU.subtract, ALU.mult)
                if t % 4 == 3:
                    ins.then_inc(s_fin, 1)

        @block.tensor
        def _(pe):
            def project_in(b, j):
                for c in range(2):
                    i = (b * 4 + CONV_ORDER.index(j)) * 2 + c
                    if i >= 4:
                        pe.wait_ge(s_pje, i - 3)
                    pe.matmul(bank(i % 4), wsm[:, j * P:(j + 1) * P],
                              hT[:, b * SEQ + c * CW:b * SEQ + (c + 1) * CW], start=True, stop=True)\
                        .then_inc(s_pj, 1)

            def convolve_pe(b, j):
                pe.wait_ge(s_pje, (b * 4 + CONV_ORDER.index(j)) * 2 + 2)
                for c in range(2):
                    for k in range(TAPS):
                        ins = pe.matmul(bank(4 + c), diag[j][:, k, :], proj[:, j, c * CW + k:c * CW + k + CW],
                                        start=(k == 0), stop=(k == TAPS - 1))
                ins.then_inc(s_cpe, 1)

            def token_major(t):
                if t >= 4:
                    pe.wait_ge(s_tre, t - 3)
                for j in range(3):
                    ins = pe.transpose(bank(t % 4)[:, j * P:(j + 1) * P], xbT[:, j, t * P:(t + 1) * P], ident[:, :])
                ins.then_inc(s_tr, 1)

            def skips(t0, t1):
                for t in range(t0, t1):
                    for j in range(2):
                        ins = pe.matmul(bank(7)[:, t * SH:(t + 1) * SH], xbT[:, j, t * P:(t + 1) * P], dw[:, j, :],
                                        start=(j == 0), stop=(j == 1))
                return ins

            pe.wait_ge(s_in, 64)
            for j in CONV_ORDER:
                project_in(0, j)
            for t in range(NT):
                ins = pe.matmul(bank(7)[:, P + t * 8:P + (t + 1) * 8], hT[:, t * P:(t + 1) * P],
                                wsm[:, 4 * P + DI:4 * P + DI + 8], start=True, stop=True)
            ins.then_inc(s_dtp, 1)
            pe.wait_ge(s_diag, 2)
            pe.wait_ge(s_cstep, 11)
            convolve_pe(0, 3)
            for j in CONV_ORDER:
                project_in(1, j)
            pe.wait_ge(s_silu, 2)
            convolve_pe(1, 3)
            pe.wait_ge(s_const, 10)
            pe.wait_ge(s_vs, 12)
            for d in range(2):
                pe.matmul(bank(6)[:, 0:P].rearrange("p (t h) -> p t h", h=8)[:, :, d * SH:(d + 1) * SH],
                          tri[:, d, :], a_dt[:, :, d * SH:(d + 1) * SH], start=True, stop=True)
            pe.matmul(bank(7)[:, 2 * P:3 * P], ones[:, :], a_dt[:, :, :].rearrange("p t h -> p (t h)"),
                      start=True, stop=True).then_inc(s_cum, 1)
            pe.wait_ge(s_pje, 16)
            pe.wait_ge(s_silu, 4)
            for t in range(TB):
                token_major(t)
            pe.wait_ge(s_vs, 15)
            skips(0, TB)
            pe.wait_ge(s_silu, 5)
            convolve_pe(1, 2)
            pe.wait_ge(s_silu, 8)
            for t in range(TB, NT):
                token_major(t)
            skips(TB, NT).then_inc(s_dd, 1)
            pe.wait_ge(s_tre, NT)
            pe.wait_ge(s_coef, 2)

            def products(v):
                c, b, d, t = scan_unit(v)
                rows = slice(d * SN, (d + 1) * SN)
                pe.wait_ge(s_mix, v + 1)
                if v >= 2:
                    pe.wait_ge(s_yr, v - 1)
                for h in range(SH):
                    pe.matmul(bank(4 + v % 2)[:, h * SP:(h + 1) * SP], mix[:, v % 2, h, :],
                              xb[:, t, h * SP:(h + 1) * SP], start=True, stop=True)
                if c > 0:
                    pe.wait_ge(s_yr, v - 3)
                    pe.matmul(bank(4 + v % 2)[:, DI:2 * DI], c_cols(t, d), state[rows, b, :], start=True, stop=True)
                pe.wait_ge(s_xw, v + 1)
                pe.matmul(bank(6 + v % 2)[rows, 0:DI], xb[:, t, DI + d * SN:DI + (d + 1) * SN], xw[:, v % 2, :],
                          start=True, stop=True).then_inc(s_y, 1)

            for v in range(NV + 1):
                if v < NV:
                    c, b, d, t = scan_unit(v)
                    rows = slice(d * SN, (d + 1) * SN)
                    pe.wait_ge(s_au, v + 1)
                    if v >= 2:
                        pe.wait_ge(s_mix, v - 1)
                    pe.matmul(bank(v % 2), ones[:, :], a_u[:, v % 2].rearrange("p h t -> p (h t)"),
                              start=True, stop=False)
                    pe.matmul(bank(v % 2), ident_b[:, :], mask4_b[:, d, :], start=False, stop=True)
                    pe.matmul(bank(2 + v % 2)[:, 0:P], xbT[rows, 2, t * P:(t + 1) * P], c_cols(t, d),
                              start=True, stop=True).then_inc(s_eg, 1)
                if v >= 1:
                    products(v - 1)
            pe.wait_ge(s_mix, NV)
            for i in range(NT // 2):
                if i >= 4:
                    pe.wait_ge(s_zs, i - 3)
                for k in range(2):
                    t = 2 * i + k
                    ins = pe.matmul(bank(i % 4)[:, k * DI:(k + 1) * DI], hT[:, t * P:(t + 1) * P],
                                    wsm[:, 4 * P:4 * P + DI], start=True, stop=True)
                ins.then_inc(s_z, 1)
            pe.wait_ge(s_yr, NV)
            for i in range(NT // 2):
                pe.wait_ge(s_un, 2 * i + 2)
                if i >= 2:
                    pe.wait_ge(s_une, i - 1)
                for k in range(2):
                    for j in range(2):
                        ins = pe.transpose(bank(4 + i % 2)[:, (k * 2 + j) * P:(k * 2 + j + 1) * P],
                                           y[:, 2 * i + k, j * P:(j + 1) * P], ident[:, :])
                ins.then_inc(s_unt, 1)
            pe.wait_ge(s_zs, NT // 2)
            for c in range(NC4):
                pe.wait_ge(s_une, 2 * c + 2)
                for t4 in range(4):
                    t = 4 * c + t4
                    for j in range(2):
                        ins = pe.matmul(bank(c)[:, t4 * P:(t4 + 1) * P], unT[:, j, t * P:(t + 1) * P], wout[:, j, :],
                                        start=(j == 0), stop=(j == 1))
                ins.then_inc(s_so, 1)
            pe.wait_ge(s_x, 1)

            def split_product(dst, w_hi, w_lo, cols):
                pe.matmul(dst, w_hi, h_hi[:, cols], start=True, stop=False)
                pe.matmul(dst, w_hi, h_lo[:, cols], start=False, stop=False)
                return pe.matmul(dst, w_lo, h_hi[:, cols], start=False, stop=True)

            def norm_t(n, c, dst):
                pe.wait_ge(s_hn, n * NC4 + c + 1)
                for t4 in range(4):
                    ins = pe.transpose(dst[:, t4 * P:(t4 + 1) * P], hn[:, 4 * c + t4, :], ident[:, :])
                ins.then_inc(s_nt, 1)

            with pe.Fori(0, LAYERS) as layer:
                def project(i, b, dst):
                    c, what = ITEMS[i]
                    col = QW if what == 0 else (what - 1) * P
                    split_product(dst, wqk_hi[:, col:col + P], wqk_lo[:, col:col + P],
                                  slice(b * SEQ + c * CW, b * SEQ + (c + 1) * CW)).then_inc(s_qk, 1)

                def heads_out(it, c, dst):
                    for t4 in range(4):
                        t = 4 * c + t4
                        for p in range(2):
                            ins = pe.matmul(dst[:, t4 * P:(t4 + 1) * P], o_t[:, p, t * P:(t + 1) * P],
                                            wo[:, p, :], start=(p == 0), stop=(p == 1))
                    ins.then_inc(s_ow, 1)

                def steps(it, s0, s1, last=False):
                    for s in range(s0, s1):
                        if not (last and s >= NU):
                            b, p, qt, hh = UNITS[s % NU]
                            if s % (NU // 4) == 0:
                                pe.wait_ge(s_lo, (it * 2 + s // (NU // 2)) * ROPES
                                           + (ROPES if s // (NU // 4) % 2 else FIRST))
                            if s >= 2:
                                pe.wait_ge(s_e, it * NU + s - 1)
                            nk = qt + 1
                            q_cols = slice(b * SEQ + qt * P, b * SEQ + (qt + 1) * P)
                            for k0 in range(0, nk, 4):
                                n = max(min(nk - k0, 4), 2) * P
                                dst = ps_s[:, s % 2, k0 * P:k0 * P + n]
                                k_cols = slice(b * SEQ + k0 * P, b * SEQ + k0 * P + n)
                                pe.matmul(dst, qs[:, 2 * p + hh, q_cols], k_hi[:, k_cols], start=True, stop=False)
                                if k0 + 4 >= nk:
                                    pe.matmul(ps_s[:, s % 2, qt * P:(qt + 1) * P], ident_b[:, :], causal_b[:, :],
                                              start=False, stop=False)
                                ins = pe.matmul(dst, qs[:, 2 * p + hh, q_cols], k_lo[:, k_cols], start=False,
                                                stop=True)
                            ins.then_inc(s_s, 1)
                        u = s - LAG_T
                        if u >= 0 and not (last and u >= NU):
                            pe.wait_ge(s_p, it * NU + u + 1)
                            for part_ in range(2 if chunk(u, 1) else 1):
                                n = chunk(u, part_)
                                if n >= 2:
                                    pe.wait_ge(s_ev, it * NCH + n - 1)
                                for k in range(part_ * 4, min(UNITS[u % NU][2] + 1, part_ * 4 + 4)):
                                    ins = pe.transpose(ps_t[:, n % 2, k % 4 * P:(k % 4 + 1) * P],
                                                       prob[:, u % NU % R_PROB, k * P:(k + 1) * P], ident[:, :])
                                ins.then_inc(s_t, 1)
                        j2 = s - LAG_T - LAG_PV
                        if j2 >= 0 and j2 % 2 == 0 and not (last and j2 >= NU):
                            j = j2 // 2
                            b, p, qt, _ = UNITS[j2 % NU]
                            if j % (NPAIR // 2) == 0:
                                pe.wait_ge(s_vg, it * 2 + j // (NPAIR // 2) + 1)
                            pe.wait_ge(s_ev, it * NCH + last_chunk(j2 + 1) + 1)
                            if j >= 1:
                                pe.wait_ge(s_oe, it * NPAIR + j)
                            for kt in range(qt + 1):
                                for hh in range(2):
                                    ins = pe.matmul(
                                        ps_o[hh * HD:(hh + 1) * HD, 0, j % 4 * P:(j % 4 + 1) * P],
                                        v_g[:, b * TB + kt, :], prob_t[:, (j2 + hh) % R_PT, kt, :],
                                        start=(kt == 0), stop=(kt == qt))
                            ins.then_inc(s_pv, 1)
                        got = side(s, last)
                        if got:
                            kind, k, o = got
                            before = side_before(s, last)
                            if before and before[0] == "wo":
                                pe.wait_ge(s_xa, (it + before[2]) * NC4 + before[1] + 1)
                            elif before and before[0] == "tr":
                                pe.wait_ge(s_hh, (layer * 2 + 1) * NC4 + before[1] + 1)
                            elif before:
                                pe.wait_ge(s_qc, half_of(it, before) * ROPES + before[1] + 1)
                            if kind == "b1":
                                pe.wait_ge(s_hl, layer * 2 * NC4 + SEQ // CW + ITEMS[k][0] + 1)
                                project(k, 1, ps_o[:, 1, :])
                            if kind == "b0":
                                if k == 0:
                                    pe.wait_ge(s_qlo, it + o + 2)
                                project(k, 0, ps_o[:, 1, :])
                            if kind == "tr":
                                norm_t(layer * 2 + 1, k, ps_o[:, 1, :])
                            if kind == "wo":
                                if k == 0:
                                    pe.wait_ge(s_wo, (it + o) * 16 + 16)
                                if k % 2 == 0:
                                    pe.wait_ge(s_oe, (it + o) * NPAIR + (k // 2 + 1) * NPAIR // 2)
                                heads_out(it + o, k, ps_o[:, 1, :])

                for what in "n0 n1 v0 p0 p1 p2 n2 n3 p3 v1 p4 v2 p5 v3 v4 v5 v6 v7".split():
                    i = int(what[1])
                    if what[0] == "n":
                        norm_t(layer * 2, i, bank(i))
                    if what[0] == "p":
                        if i == 0:
                            pe.wait_ge(s_qlo, layer * NKV + 1)
                        pe.wait_ge(s_hl, layer * 2 * NC4 + ITEMS[i][0] + 1)
                        if i >= 4:
                            pe.wait_ge(s_qc, layer * NKV * 2 * ROPES + i - 3)
                        project(i, 0, bank(4 + i % 4))
                    if what[0] == "v":
                        if i == 0:
                            pe.wait_ge(s_wl, layer * 16 + 16)
                        pe.wait_ge(s_hh, layer * 2 * NC4 + max(i // 2, min(i, 3)) + 1)
                        if i >= 4:
                            pe.wait_ge(s_ve, layer * (NT // 2) + i - 3)
                        for k in range(2):
                            t = 2 * i + k
                            ins = pe.matmul(bank(i % 4)[:, k * 256:(k + 1) * 256], hT[:, t * P:(t + 1) * P],
                                            wlay[:, 2 + NE:WLAY], start=True, stop=True)
                        ins.then_inc(s_v, 1)
                pe.wait_ge(s_ve, layer * (NT // 2) + NT // 2)
                pe.wait_ge(s_qc, layer * NKV * 2 * ROPES + ROPES)
                steps(layer * NKV, 0, HEAD)
                with pe.Fori(0, NKV - 1) as g:
                    steps(layer * NKV + g, HEAD, NU + HEAD)
                steps(layer * NKV + NKV - 1, HEAD, NU + HEAD, last=True)
                def router():
                    for c in range(2, NC4):
                        norm_t(layer * 2 + 1, c, bank(2 + c))
                    for t in range(NT):
                        pe.wait_ge(s_hh, layer * 2 * NC4 + NC4 + t // 4 + 1)
                        ins = pe.matmul(ps_o[:, 0, t * NE:(t + 1) * NE], hT[:, t * P:(t + 1) * P],
                                        wlay[:, 2:2 + NE], start=True, stop=True)
                    ins.then_inc(s_rt, 1)

                def items(it, m0, m1, last=False):
                    for m in range(m0, m1):
                        if not (last and m >= ITER_GU):
                            e, c, fh, r = m // GU, m // 2 % NC4, m % 2, M_BANKS[m % ITER_GU]
                            if m % GU == 0:
                                pe.wait_ge(s_glo, it * 2 + e + 1)
                            if item_before(m) >= 0:
                                pe.wait_ge(s_a, it * ITER_GU + item_before(m) + 1)
                            if m < GU and m % 2 == 0:
                                pe.wait_ge(s_hl, (layer * 2 + 1) * NC4 + c + 1)
                            if m == ROUTER_M + 1:
                                pe.wait_ge(s_hh, (layer * 2 + 2) * NC4)
                            for k in range(2):
                                f = slice(k * FF + fh * P, k * FF + (fh + 1) * P)
                                ins = split_product(bank(2 * r + k), wg_hi[:, e % 2, f], wg_lo[:, e % 2, f],
                                                    slice(c * CW, (c + 1) * CW))
                            ins.then_inc(s_gu, 1)
                            if m == ROUTER_M:
                                router()
                        if m % 2 == 1 and m >= 3:
                            yi = (m - 3) // 2
                            e = yi // NC4
                            if yi == 0:
                                pe.wait_ge(s_rv, layer * N_RV + 1)
                            pe.wait_ge(s_a, it * ITER_GU + 2 * yi + 2)
                            if yi >= 2:
                                pe.wait_ge(s_ya, it * ITER_Y + yi - 1)
                            for t4 in range(4):
                                for fh in range(2):
                                    ins = pe.matmul(ps_o[:, yi % 2, t4 * P:(t4 + 1) * P],
                                                    a_t[:, yi % 2, fh, t4 * P:(t4 + 1) * P],
                                                    wexp[:, e % 2, 2 * FF + fh * P:2 * FF + (fh + 1) * P],
                                                    start=(fh == 0), stop=(fh == 1))
                            ins.then_inc(s_dn, 1)

                items(layer * (NE // 2), 0, HEAD_M)
                with pe.Fori(0, NE // 2 - 1) as e2:
                    items(layer * (NE // 2) + e2, HEAD_M, HEAD_M + ITER_GU)
                items(layer * (NE // 2) + NE // 2 - 1, HEAD_M, LAST_M, last=True)


def layouts(a):
    def tokens(v):
        return np.ascontiguousarray(v.reshape(NT, P, DM).transpose(1, 0, 2))

    u = a["L0_attn_u"].reshape(TOK, DM)
    w = a["L0_attn_in_proj_w"]
    z, xs = w[:DI], w[DI:2 * DI]
    bc = w[2 * DI:2 * DI + 4 * SN]
    dt = w[2 * DI + 4 * SN:]
    perm = np.concatenate([np.arange(DI), DI + np.concatenate(
        [np.arange(0, SN), np.arange(2 * SN, 3 * SN), np.arange(SN, 2 * SN), np.arange(3 * SN, 4 * SN)])])
    w_in = np.concatenate([np.concatenate([xs, bc])[perm], z, dt]).T
    cw = a["L0_attn_conv1d_w"][:, 0, :][perm].reshape(4, P, TAPS).transpose(1, 0, 2).reshape(P, -1)
    cb = a["L0_attn_conv1d_b"][perm].reshape(4, P).T
    rms = a["L0_attn_rms_w"].reshape(2, P).T

    def rows(v):
        return np.broadcast_to(v[None], (P, v.size))

    small = np.concatenate([cw, cb, rms, rows(a["L0_attn_dt_bias"]), rows(a["L0_attn_dt_bias"]),
                            rows(a["L0_attn_A_log"]), rows(a["L0_attn_A_log"]), rows(a["L0_attn_D_b"])], axis=1)
    wout = a["L0_attn_outproj_w"].T.reshape(2, P, DM).transpose(1, 0, 2).reshape(P, -1)
    dw = a["L0_attn_D_w"].T.reshape(2, P, SH).transpose(1, 0, 2).reshape(P, -1)
    scan_out = np.concatenate([wout, dw], axis=1)

    inv = (np.float32(1.0) / np.float32(THETA) ** (np.arange(0, HD, 2, dtype=np.float32) / np.float32(HD)))
    f = np.arange(SEQ, dtype=np.float32)[:, None] * inv.astype(np.float32)
    c, s = np.cos(f).T, np.sin(f).T
    rope = np.stack([np.concatenate([c, c, c, c]), np.concatenate([s, -s, s, -s])]).astype(np.float32)

    wq = a["L0_ffn_wq"].reshape(LAYERS, DM, NKV, REP, HD)
    wk = a["L0_ffn_wk"].reshape(LAYERS, DM, NKV, 1, HD)
    attn = np.concatenate([wq, wk, wk], axis=3)
    attn = attn.transpose(0, 2, 1, 3, 4).reshape(LAYERS * NKV, DM, WQKV)
    w_o = a["L0_ffn_wo"].reshape(LAYERS, NKV, 2, P, DM).transpose(0, 1, 3, 2, 4).reshape(LAYERS * NKV, P, 2, DM)
    lay = np.concatenate([a["L0_ffn_ln1_w"][:, :, None], a["L0_ffn_ln2_w"][:, :, None], a["L0_ffn_wr"],
                          a["L0_ffn_wv"]], axis=2)
    wd = a["L0_ffn_wd"].reshape(LAYERS, NE, 2, P, DM).transpose(0, 1, 3, 2, 4).reshape(LAYERS, NE, P, 2 * DM)
    exp = np.concatenate([a["L0_ffn_wg"], a["L0_ffn_wu"], wd], axis=3).reshape(LAYERS * NE, P, -1)

    def ahead(v, n):
        return np.concatenate([v, v[:n]])

    return {
        "u_tok": tokens(u), "u_feat": u.T, "w_in": w_in, "conv_w": small, "w_scan_out": scan_out, "rope": rope,
        "w_attn": ahead(attn, 1), "w_o": ahead(w_o, 1), "w_layer": ahead(lay, 1), "w_expert": ahead(exp, 2),
    }


def kernel(**inputs):
    import concourse.bacc as bacc
    from concourse.bass_utils import run_bass_kernel_spmd

    arrays = {n: np.ascontiguousarray(v) for n, v in layouts({k: np.asarray(v) for k, v in inputs.items()}).items()}
    nc = bacc.Bacc("TRN2", target_bir_lowering=False, num_devices=1)
    aps = {n: nc.dram_tensor(n, v.shape, F32, kind="ExternalInput").ap() for n, v in arrays.items()}
    out = nc.dram_tensor("out", (P, NT, DM), F32, kind="ExternalOutput").ap()
    build(nc, out=out, **aps)
    r = run_bass_kernel_spmd(nc, [arrays], core_ids=[0])
    return r.results[0]["out"].transpose(1, 0, 2).reshape(BATCH, SEQ, DM)
```
